# Optimizing a Trainium2 kernel written in Bass

```python
import numpy as np
import jax
import jax.numpy as jnp

def _softmax(x, axis=-1):
    return jax.nn.softmax(x, axis=axis)

def _gelu(x):
    return jax.nn.gelu(x, approximate=True)

def _silu(x):
    return jax.nn.silu(x)

def _sigmoid(x):
    return jax.nn.sigmoid(x)

def _layernorm(x, axis=-1, eps=1e-05):
    m = jnp.mean(x, axis=axis, keepdims=True)
    v = jnp.var(x, axis=axis, keepdims=True)
    return (x - m) / jnp.sqrt(v + eps)

def _scatter_add(tgt, idx, src, axis=0):
    return tgt.at[idx].add(src)

def _segment_sum(src, seg, n):
    return jax.ops.segment_sum(src, seg, n)
kernel_name = 'mk_flamingo_gated_d1_seqx_r4_3ad7b4'

def setup_inputs(seed: int=0):
    np.random.seed(seed)
    _w = jnp.asarray

    def _rec_inputs():
        import jax
        import jax.numpy as jnp
        _rk = jax.random.key(seed)
        x = -0.0002928 + 1 * jax.random.normal(jax.random.fold_in(_rk, 1), (32, 100, 256), jnp.float32)
        _lenS = 100 - jax.random.randint(jax.random.fold_in(_rk, 7), (32,), 0, max(1, 100 // 4) + 1, jnp.int32)
        _lenS2 = 361 - jax.random.randint(jax.random.fold_in(_rk, 8), (32,), 0, max(1, 361 // 4) + 1, jnp.int32)
        _ctx_1024P = jax.random.normal(jax.random.fold_in(_rk, 11), (32, 16, 256), jnp.float32)
        _ctx_1024c = jax.random.dirichlet(jax.random.fold_in(_rk, 511), 0.3 * jnp.ones((16,), jnp.float32), (32, 361))
        _ctx_1024t = jnp.einsum('bsk,bkd->bsd', _ctx_1024c, _ctx_1024P)
        _ctx_1024t = _ctx_1024t * jax.lax.rsqrt(jnp.mean(jnp.square(_ctx_1024t)) + 1e-12) * 0.953939
        ctx_1024 = -1.39393e-06 + 0.999914 * (_ctx_1024t + 0.3 * jax.random.normal(jax.random.fold_in(_rk, 611), (32, 361, 256), jnp.float32))
        _validS = jnp.arange(100)[None, :] < _lenS[:, None]
        _validS2 = jnp.arange(361)[None, :] < _lenS2[:, None]
        _causal = jnp.tril(jnp.ones((100, 100), dtype=bool))
        mask_BxSxS2_bf1 = jnp.ones((32, 100, 361), dtype=bool)
        _g = jax.random.normal(jax.random.fold_in(_rk, 9001), (2, 1), jnp.float32)
        _g = jnp.sign(_g) * jnp.maximum(jnp.abs(_g), 1.0) + (_g == 0) * 1.0
        g_xattn = _g[0]
        g_ffn = _g[1]
        return (x, ctx_1024, mask_BxSxS2_bf1, g_xattn, g_ffn)
    x, ctx_1024, mask_BxSxS2_bf1, g_xattn, g_ffn = _rec_inputs()

    def _L0_xattn_setup():
        import jax, jax.numpy as jnp
        import numpy as np
        D_MODEL = 256
        NUM_HEADS = 16
        D_H = D_MODEL // NUM_HEADS

        def _xavier(key, out_f, in_f):
            limit = np.sqrt(6.0 / (in_f + out_f))
            return jax.random.uniform(key, (out_f, in_f), jnp.float32, -limit, limit)
        key = jax.random.key(seed)
        ks = jax.random.split(key, 8)
        B, S = (2, 512)
        q = jax.random.normal(ks[0], (B, S, D_MODEL), jnp.float32)
        k = jax.random.normal(ks[1], (B, S, D_MODEL), jnp.float32)
        v = jax.random.normal(ks[2], (B, S, D_MODEL), jnp.float32)
        attn_mask = jnp.ones((B, S, S), dtype=bool)
        Wq = _xavier(ks[3], D_MODEL, D_MODEL)
        bq = jnp.zeros((D_MODEL,), jnp.float32)
        Wk = _xavier(ks[4], D_MODEL, D_MODEL)
        bk = jnp.zeros((D_MODEL,), jnp.float32)
        Wv = _xavier(ks[5], D_MODEL, D_MODEL)
        bv = jnp.zeros((D_MODEL,), jnp.float32)
        Wo = _xavier(ks[6], D_MODEL, D_MODEL)
        bo = jnp.zeros((D_MODEL,), jnp.float32)
        return {'q': q, 'k': k, 'v': v, 'attn_mask': attn_mask, 'Wq': Wq, 'bq': bq, 'Wk': Wk, 'bk': bk, 'Wv': Wv, 'bv': bv, 'Wo': Wo, 'bo': bo}
    _L0_xattn_all = _L0_xattn_setup()
    _L0_xattn_in = {k: v for k, v in _L0_xattn_all.items() if k in ('Wq', 'bq', 'Wk', 'bk', 'Wv', 'bv', 'Wo', 'bo')}
    del _L0_xattn_all

    def _L0_ffn_setup():
        import jax, jax.numpy as jnp
        import numpy as np
        B, S, D = (2, 512, 256)
        H, E, P, K = (8, 8, 128, 2)
        SCALE = 1.0 / np.sqrt(P)

        def _get_sel_gate(x, w, route_scale):
            logits = jnp.einsum('bsd,ed->bse', x, w).astype(jnp.float32)
            raw = logits.reshape(x.shape[0], x.shape[1], H, E)
            probs = jax.nn.sigmoid(raw)
            vals, idx = jax.lax.top_k(probs, K)
            vals = vals / jnp.clip(vals.sum(-1, keepdims=True), 1e-09)
            vals = vals * route_scale
            gate = (jax.nn.one_hot(idx, E, dtype=vals.dtype) * vals[..., None]).sum(-2)
            return gate
        key = jax.random.key(seed)
        ks = jax.random.split(key, 8)
        std = 1.0 / np.sqrt(D)
        return {'x': jax.random.normal(ks[0], (B, S, D), jnp.float32), 'q_w': jax.random.normal(ks[1], (H * P, D), jnp.float32) * std, 'k_w': jax.random.normal(ks[2], (H * P, D), jnp.float32) * std, 'v_w': jax.random.normal(ks[3], (H * E, D, P), jnp.float32) * std, 'o_w': jax.random.normal(ks[4], (H * E, P, D), jnp.float32) * (1.0 / np.sqrt(H * P)), 'sel_v_w': jax.random.normal(ks[5], (H * E, D), jnp.float32) * std, 'sel_o_w': jax.random.normal(ks[6], (H * E, D), jnp.float32) * std, 'route_scale': jnp.ones((1,), jnp.float32)}
    _L0_ffn_all = _L0_ffn_setup()
    _L0_ffn_in = {k: v for k, v in _L0_ffn_all.items() if k in ('q_w', 'k_w', 'v_w', 'o_w', 'sel_v_w', 'sel_o_w', 'route_scale')}
    del _L0_ffn_all
    return {'x': x, 'ctx_1024': ctx_1024, 'mask_BxSxS2_bf1': mask_BxSxS2_bf1, 'g_xattn': g_xattn, 'g_ffn': g_ffn, 'L0_xattn_Wq': _L0_xattn_in['Wq'], 'L0_xattn_bq': _L0_xattn_in['bq'], 'L0_xattn_Wk': _L0_xattn_in['Wk'], 'L0_xattn_bk': _L0_xattn_in['bk'], 'L0_xattn_Wv': _L0_xattn_in['Wv'], 'L0_xattn_bv': _L0_xattn_in['bv'], 'L0_xattn_Wo': _L0_xattn_in['Wo'], 'L0_xattn_bo': _L0_xattn_in['bo'], 'L0_ffn_q_w': _L0_ffn_in['q_w'], 'L0_ffn_k_w': _L0_ffn_in['k_w'], 'L0_ffn_v_w': _L0_ffn_in['v_w'], 'L0_ffn_o_w': _L0_ffn_in['o_w'], 'L0_ffn_sel_v_w': _L0_ffn_in['sel_v_w'], 'L0_ffn_sel_o_w': _L0_ffn_in['sel_o_w'], 'L0_ffn_route_scale': _L0_ffn_in['route_scale']}

def reference(x, ctx_1024, mask_BxSxS2_bf1, g_xattn, g_ffn, L0_xattn_Wq, L0_xattn_bq, L0_xattn_Wk, L0_xattn_bk, L0_xattn_Wv, L0_xattn_bv, L0_xattn_Wo, L0_xattn_bo, L0_ffn_q_w, L0_ffn_k_w, L0_ffn_v_w, L0_ffn_o_w, L0_ffn_sel_v_w, L0_ffn_sel_o_w, L0_ffn_route_scale):
    import jax
    import jax.numpy as jnp

    def _L0_xattn_ref(q, k, v, attn_mask, Wq, bq, Wk, bk, Wv, bv, Wo, bo):
        import jax, jax.numpy as jnp
        import numpy as np
        D_MODEL = 256
        NUM_HEADS = 16
        D_H = D_MODEL // NUM_HEADS

        def _xavier(key, out_f, in_f):
            limit = np.sqrt(6.0 / (in_f + out_f))
            return jax.random.uniform(key, (out_f, in_f), jnp.float32, -limit, limit)
        B, S, _ = q.shape
        H, Dh = (NUM_HEADS, D_H)
        Q = jnp.einsum('bsd,ed->bse', q, Wq) + bq
        K = jnp.einsum('bsd,ed->bse', k, Wk) + bk
        V = jnp.einsum('bsd,ed->bse', v, Wv) + bv
        Qm = Q.reshape(B, S, H, Dh).transpose(0, 2, 1, 3)
        Km = K.reshape(B, -1, H, Dh).transpose(0, 2, 1, 3)
        Vm = V.reshape(B, -1, H, Dh).transpose(0, 2, 1, 3)
        scores = jnp.einsum('bhqd,bhkd->bhqk', Qm, Km) / jnp.sqrt(jnp.float32(Dh))
        fill = jnp.finfo(scores.dtype).min
        scores = jnp.where(attn_mask[:, None, :, :], scores, fill)
        attn = jax.nn.softmax(scores, axis=-1)
        A = jnp.einsum('bhqk,bhkd->bhqd', attn, Vm)
        A = A.transpose(0, 2, 1, 3).reshape(B, S, H * Dh)
        O = jnp.einsum('bsd,ed->bse', A, Wo) + bo
        return O

    def _L0_ffn_ref(x, q_w, k_w, v_w, o_w, sel_v_w, sel_o_w, route_scale):
        import jax, jax.numpy as jnp
        import numpy as np
        B, S, D = (2, 512, 256)
        H, E, P, K = (8, 8, 128, 2)
        SCALE = 1.0 / np.sqrt(P)

        def _get_sel_gate(x, w, route_scale):
            logits = jnp.einsum('bsd,ed->bse', x, w).astype(jnp.float32)
            raw = logits.reshape(x.shape[0], x.shape[1], H, E)
            probs = jax.nn.sigmoid(raw)
            vals, idx = jax.lax.top_k(probs, K)
            vals = vals / jnp.clip(vals.sum(-1, keepdims=True), 1e-09)
            vals = vals * route_scale
            gate = (jax.nn.one_hot(idx, E, dtype=vals.dtype) * vals[..., None]).sum(-2)
            return gate
        rs = route_scale[0]
        gate_v = _get_sel_gate(x, sel_v_w, rs)
        gate_o = _get_sel_gate(x, sel_o_w, rs)
        q = jnp.einsum('bsd,hpd->bhsp', x, q_w.reshape(H, P, D))
        k = jnp.einsum('bsd,hpd->bhsp', x, k_w.reshape(H, P, D))
        xv = jnp.einsum('bsd,hedp->bshep', x, v_w.reshape(H, E, D, P))
        v = jnp.einsum('bshep,bshe->bhsp', xv, gate_v)
        att = jax.nn.softmax(jnp.einsum('bhqp,bhkp->bhqk', q, k) * SCALE, axis=-1)
        ctx = jnp.einsum('bhqk,bhkp->bqhp', att, v)
        weighted = ctx[:, :, :, None, :] * gate_o[..., None]
        out = jnp.einsum('bshep,hepd->bsd', weighted, o_w.reshape(H, E, P, D))
        return out
    x = x + jnp.tanh(g_xattn[0]) * _L0_xattn_ref(_layernorm(x, axis=-1), ctx_1024, ctx_1024, mask_BxSxS2_bf1, L0_xattn_Wq, L0_xattn_bq, L0_xattn_Wk, L0_xattn_bk, L0_xattn_Wv, L0_xattn_bv, L0_xattn_Wo, L0_xattn_bo)
    x = x + jnp.tanh(g_ffn[0]) * _L0_ffn_ref(_layernorm(x, axis=-1), L0_ffn_q_w, L0_ffn_k_w, L0_ffn_v_w, L0_ffn_o_w, L0_ffn_sel_v_w, L0_ffn_sel_o_w, L0_ffn_route_scale)
    return x

_drawn_inputs = setup_inputs


def setup_inputs(seed=0):
    import zlib

    import numpy as np

    out = dict(_drawn_inputs(seed))
    spreads = {'L0_xattn_bq': (0.0, 0.333),
     'L0_xattn_bk': (0.0, 0.8),
     'L0_xattn_bv': (0.0, 0.1),
     'L0_xattn_bo': (0.0, 0.1)}
    factors = {}
    for name, (base, spread) in spreads.items():
        noise = np.random.default_rng([zlib.crc32(name.encode()), seed]).standard_normal(out[name].shape)
        drawn = base * np.exp(spread * noise) if base else spread * noise
        out[name] = jnp.asarray(drawn.astype(out[name].dtype))
    for name, factor in factors.items():
        out[name] = (out[name] * factor).astype(out[name].dtype)
    return out
```

```python
from contextlib import ExitStack

import concourse.bass as bass
from concourse import mybir

F32 = mybir.dt.float32
F16 = mybir.dt.float16
U8 = mybir.dt.uint8
ALU = mybir.AluOpType
ACT = mybir.ActivationFunctionType
AX = mybir.AxisListType.X

NB, SQ, SK, D = 32, 100, 361, 256
T = NB * SQ
P = 128
NT = T // P
DC = D // P
XH, XD = 16, 16
XG = P // XD
KC = 3
KW = -(-SK // KC)
SKP = KC * KW
KL = SK - (KC - 1) * KW
H, E, PD = 8, 8, 128
HE = H * E
WS = 64.0
EPS = 1e-5
BIG = 3.4028234663852886e38
NW = 400
NC = T // NW
V_BANK = (2, 0, 1)


def at_least(eng, sem, value):
    if not isinstance(value, int) or value > 0:
        eng.wait_ge(sem, value)


def pass_wait(eng, passed):
    eng.sem_inc(passed, 1)


class Batch:

    def __init__(self, n, par, half):
        self.n, self.par, self.half = n, par, half

    def next(self):
        return Batch(self.n + 1, 1 - self.par, self.half + self.par)

    def before(self):
        return Batch(self.n - 1, 1 - self.par, self.half - (1 - self.par))


def fixed(n):
    return Batch(n, n % 2, n // 2)


def batches(eng, body):
    body(fixed(0))
    body(fixed(1))
    with eng.Fori(1, NB // 2 - 1) as i:
        body(Batch(2 * i, 0, i))
        body(Batch(2 * i + 1, 1, i))
    body(fixed(NB - 2))
    body(fixed(NB - 1))


def is_first(b):
    return isinstance(b.n, int) and b.n == 0


def is_last(b):
    return isinstance(b.n, int) and b.n == NB - 1


class Store:

    def __init__(self, nc, ctx):
        self.nc, self.ctx = nc, ctx

    def sbuf(self, name, shape, dt=F32):
        return self.ctx.enter_context(self.nc.sbuf_tensor(name, shape, dt))

    def psum(self, name, shape):
        return self.ctx.enter_context(self.nc.psum_tensor(name, shape, F32))

    def sem(self, name):
        return self.ctx.enter_context(self.nc.semaphore(name))

    def sems(self, name, n):
        return [self.sem(f"{name}_{i}") for i in range(n)]


def rstd_steps(dve, mv, std, rstd, half, s_step, s_std, base):
    var = mv[:, :, 1]
    dve.tensor_scalar(var, var, EPS, None, ALU.add).then_inc(s_step, 1)
    dve.wait_ge(s_std, 1)
    dve.reciprocal(rstd[:, :], std[:, :]).then_inc(s_step, 1)
    dve.wait_ge(s_step, base + 2)
    dve.tensor_tensor(half[:, :], rstd[:, :], rstd[:, :], ALU.mult).then_inc(s_step, 1)
    dve.wait_ge(s_step, base + 3)
    dve.tensor_tensor(half[:, :], half[:, :], var, ALU.mult).then_inc(s_step, 1)
    dve.wait_ge(s_step, base + 4)
    dve.tensor_scalar(half[:, :], half[:, :], -0.5, 1.5, ALU.mult, ALU.add).then_inc(s_step, 1)
    dve.wait_ge(s_step, base + 5)
    dve.tensor_tensor(rstd[:, :], rstd[:, :], half[:, :], ALU.mult).then_inc(s_step, 1)
    dve.wait_ge(s_step, base + 6)


def tiles(eng, body):
    for t in range(3):
        body(t, t % 2)
    with eng.Fori(0, (NT - 3) // 2) as i:
        body(2 * i + 3, 1)
        body(2 * i + 4, 0)


def stage_queries(nc, k, x, g_xattn, g_ffn, wq_t, bq, q_parts):
    with ExitStack() as ctx:
        m = Store(nc, ctx)
        xt = m.sbuf("q_x", [P, NT, D])
        xn = m.sbuf("q_xn", [P, 2, D])
        xnt = m.sbuf("q_xnt", [P, DC, T])
        wq = m.sbuf("q_wq", [P, DC, D])
        bqc = m.sbuf("q_bq", [P, DC])
        st = m.sbuf("q_st", [P, NT, 6])
        mv = m.sbuf("q_mv", [P, NT, 2])
        std, rstd, half = (m.sbuf(n, [P, NT]) for n in ("q_std", "q_rstd", "q_half"))
        qhi = m.sbuf("q_hi", [P, DC, T], F16)
        qlo = m.sbuf("q_lo", [P, DC, T], F16)
        pt = m.psum("q_pt", [P, 2, 512])
        pq = m.psum("q_pq", [P, 4, 512])
        s_x = m.sems("q_s_x", 5)
        s_w = m.sem("q_s_w")
        s_id = m.sem("q_s_id")
        s_g, s_tanh = m.sem("q_s_g"), m.sem("q_s_tanh")
        s_st, s_mv, s_step, s_std = (m.sem(f"q_s_{n}") for n in ("st", "mv", "step", "std"))
        s_xn, s_t, s_xnt, s_q, s_hi, s_lo, s_out = (
            m.sem(f"q_s_{n}") for n in ("xn", "t", "xnt", "q", "hi", "lo", "out"))
        with nc.Block() as block:

            @block.sync
            def _(sp):
                for i in range(5):
                    sp.dma_start(xt[:, 5 * i:5 * i + 5, :],
                                 x[640 * i:640 * i + 640, :].rearrange("(t p) d -> p t d", p=P)
                                 ).then_inc(s_x[i], 16)
                sp.dma_start(wq[:, :, :], wq_t.rearrange("(c p) e -> p c e", p=P)).then_inc(s_w, 16)
                sp.dma_start(bqc[:, :], bq).then_inc(s_w, 16)
                for i, g in enumerate((g_xattn, g_ffn)):
                    sp.dma_start(k.tanh_g[:, i:i + 1], g.partition_broadcast(P)).then_inc(s_g, 16)
                for g in range(2):
                    cut = slice(g * T // 2, (g + 1) * T // 2)
                    sp.wait_ge(s_hi, DC * NC // 2 * (g + 1))
                    sp.dma_start(q_parts[0, :, cut].rearrange("(c p) t -> p c t", p=P),
                                 qhi[:, :, cut]).then_inc(s_out, 16)
                    sp.wait_ge(s_lo, DC * NC // 2 * (g + 1))
                    sp.dma_start(q_parts[1, :, cut].rearrange("(c p) t -> p c t", p=P),
                                 qlo[:, :, cut]).then_inc(s_out, 16)
                sp.wait_ge(s_out, 64)

            @block.gpsimd
            def _(pool):
                pool.memset(k.ident[:, :], 0.0).then_inc(s_id, 1)
                pool.wait_ge(s_id, 1)
                pool.affine_select(out=k.ident[:, :], in_=k.ident[:, :], compare_op=ALU.not_equal,
                                   fill=1.0, base=0, pattern=[[-1, P]],
                                   channel_multiplier=1).then_inc(s_id, 1)

            @block.vector
            def _(dve):
                for t in range(NT):
                    if t % 5 == 0:
                        dve.wait_ge(s_x[t // 5], 16)
                    dve.bn_stats(st[:, t, :], xt[:, t, :]).then_inc(s_st, 1)
                dve.wait_ge(s_st, NT)
                for t in range(NT):
                    dve.bn_aggr(mv[:, t, :], st[:, t, :]).then_inc(s_mv, 1)
                dve.wait_ge(s_mv, NT)
                rstd_steps(dve, mv, std, rstd, half, s_step, s_std, 0)

                def normalize(t, par):
                    at_least(dve, s_t, t - 1)
                    dve.tensor_scalar(xn[:, par, :], xt[:, t, :], mv[:, t, 0:1], rstd[:, t:t + 1],
                                      ALU.subtract, ALU.mult).then_inc(s_xn, 1)

                for t in range(NT):
                    normalize(t, t % 2)
                dve.wait_ge(s_w, 32)
                for n in range(DC * NC):
                    c, w = n % DC, n // DC
                    dve.wait_ge(s_hi, n + 1)
                    dve.scalar_tensor_tensor(
                        out=qlo[:, c, w * NW:(w + 1) * NW], in0=pq[:, n % 4, 0:NW],
                        scalar=bqc[:, c:c + 1], in1=qhi[:, c, w * NW:(w + 1) * NW],
                        op0=ALU.add, op1=ALU.subtract).then_inc(s_lo, 1)

            @block.scalar
            def _(act):
                act.wait_ge(s_g, 32)
                act.activation(k.tanh_g[:, :], k.tanh_g[:, :], ACT.Tanh).then_inc(s_tanh, 1)
                act.wait_ge(s_step, 1)
                act.activation(std[:, :], mv[:, :, 1], ACT.Sqrt).then_inc(s_std, 1)
                for t in range(NT):
                    act.wait_ge(s_t, t + 1)
                    act.activation(xnt[:, :, t * P:(t + 1) * P],
                                   pt[:, t % 2, 0:DC * P].rearrange("p (c n) -> p c n", c=DC),
                                   ACT.Copy).then_inc(s_xnt, 1)
                act.wait_ge(s_w, 32)
                for n in range(DC * NC):
                    c, w = n % DC, n // DC
                    act.wait_ge(s_q, n + 1)
                    act.activation(qhi[:, c, w * NW:(w + 1) * NW], pq[:, n % 4, 0:NW],
                                   ACT.Identity, bias=bqc[:, c:c + 1]).then_inc(s_hi, 1)

            @block.tensor
            def _(pe):
                pe.wait_ge(s_id, 2)
                for t in range(NT):
                    pe.wait_ge(s_xn, t + 1)
                    at_least(pe, s_xnt, t - 1)
                    for c in range(DC):
                        last = pe.transpose(pt[:, t % 2, c * P:(c + 1) * P],
                                            xn[:, t % 2, c * P:(c + 1) * P], k.ident[:, :])
                    last.then_inc(s_t, 1)
                pe.wait_ge(s_w, 32)
                pe.wait_ge(s_xnt, NT)
                for n in range(DC * NC):
                    c, w = n % DC, n // DC
                    at_least(pe, s_lo, n - 3)
                    for kc in range(DC):
                        last = pe.matmul(pq[:, n % 4, 0:NW], wq[:, kc, c * P:(c + 1) * P],
                                         xnt[:, kc, w * NW:(w + 1) * NW],
                                         start=kc == 0, stop=kc == DC - 1)
                    last.then_inc(s_q, 1)


def stage_cross(nc, k, x, ctx_t, mask, wk_t, bk, wv_t, bv, wo_t, bo, q_parts, k_parts, x1):
    with ExitStack() as ctx:
        m = Store(nc, ctx)
        wk, wv, wo = (m.sbuf(f"c_{n}", [P, DC, D]) for n in ("wk", "wv", "wo"))
        bkc, bvc = m.sbuf("c_bk", [P, DC]), m.sbuf("c_bv", [P, DC])
        bor = m.sbuf("c_bo", [1, D])
        ones = m.sbuf("c_ones", [P, P])
        bvb = m.sbuf("c_bvb", [P, DC, P])
        tgbo = m.sbuf("c_tgbo", [P, D])
        ctxb = m.sbuf("c_ctx", [P, 2, DC, SK])
        khi, klo = (m.sbuf(f"c_k{n}", [P, 2, DC, SK], F16) for n in ("hi", "lo"))
        kst = m.sbuf("c_kst", [P, 2, XH // 2, SK], F16)
        qst = m.sbuf("c_qst", [P, 2, XH, SQ], F16)
        vz = m.sbuf("c_v", [KW, 2, KC, XH // 2, 3, XD])
        mraw = m.sbuf("c_mraw", [SQ, 2, SK], U8)
        mbias = m.sbuf("c_mbias", [SQ, 2, SK])
        xb = m.sbuf("c_xb", [SQ, 2, D])
        xbias = m.sbuf("c_xbias", [SQ, 2, D])
        x1b = m.sbuf("c_x1", [SQ, 2, D])
        sm = m.sbuf("c_sm", [SQ, 4, SK])
        nmax = m.sbuf("c_nmax", [SQ, 4])
        ex = m.sbuf("c_ex", [SQ, 4, SKP])
        ext = m.sbuf("c_ext", [KW, 4, KC * SQ])
        den = m.sbuf("c_den", [SQ, 2, XH])
        rden = m.sbuf("c_rden", [SQ, XH])
        rdx = m.sbuf("c_rdx", [SQ, XH, XD])
        rt = m.sbuf("c_rt", [P, DC * SQ])
        an = m.sbuf("c_an", [P, DC * SQ])
        p_s = m.psum("c_ps", [P, 2, 512])
        p_t = m.psum("c_pt", [P, 2, 512])
        p_a = m.psum("c_pa", [P, 512])
        p_p = m.psum("c_pp", [P, 3, 512])
        s_w, s_one, s_zero, s_bvb, s_bo, s_tg = (m.sem(f"c_s_{n}") for n in ("w", "one", "zero", "bvb", "bo", "tg"))
        s_ctx, s_kw, s_kst, s_qst, s_mask, s_x, s_st = (
            m.sems(f"c_s_{n}", 2) for n in ("ctx", "kw", "kst", "qst", "mask", "x", "st"))
        s_k, s_khi, s_klo, s_v, s_vz, s_mb, s_xb = (
            m.sem(f"c_s_{n}") for n in ("k", "khi", "klo", "v", "vz", "mb", "xb"))
        s_s, s_sm, s_ex, s_t, s_ext, s_pv = (m.sem(f"c_s_{n}") for n in ("s", "sm", "ex", "tr", "ext", "pv"))
        s_pass_dve, s_pass_pool, s_pass_sp = (m.sem(f"c_s_pass_{n}") for n in ("dve", "pool", "sp"))
        s_rd, s_rdx, s_r, s_rt, s_an, s_o, s_x1 = (
            m.sem(f"c_s_{n}") for n in ("rd", "rdx", "r", "rt", "an", "o", "x1"))
        with nc.Block() as block:

            @block.sync
            def _(sp):
                def load_ctx(b):
                    at_least(sp, s_v, KC * (b.n - 1))
                    sp.dma_start(ctxb[:, b.par, :, :],
                                 ctx_t[b.n, :, :].rearrange("(c p) s -> p c s", p=P)
                                 ).then_inc(s_ctx[b.par], 16)

                def load_queries(b):
                    at_least(sp, s_s, XH * (b.n - 1))
                    for ab in range(2):
                        for r in range(4):
                            row = 64 * ab + XD * r
                            src = q_parts[r // 2, :, bass.ds(b.n * SQ, SQ)].rearrange(
                                "(j a d) q -> a d j q", a=2, d=XD)
                            sp.dma_start(qst[row:row + XD, b.par, ab::2, :], src[ab]).then_inc(s_qst[b.par], 16)

                def load_rest(b):
                    at_least(sp, s_mb, b.n - 1)
                    pass_wait(sp, s_pass_sp)
                    sp.dma_start(mraw[:, b.par, :], mask[b.n, :, :]).then_inc(s_mask[b.par], 16)
                    at_least(sp, s_xb, b.n - 1)
                    sp.dma_start(xb[:, b.par, :], x[bass.ds(b.n * SQ, SQ), :]).then_inc(s_x[b.par], 16)

                def stack_keys(b):
                    for part, done, src in ((0, s_khi, khi), (1, s_klo, klo)):
                        sp.wait_ge(done, DC * (b.n + 1))
                        sp.dma_start(k_parts[b.par, part, :, :].rearrange("(c p) s -> p c s", p=P),
                                     src[:, b.par, :, :]).then_inc(s_kw[b.par], 16)
                    sp.wait_ge(s_kw[b.par], 32 * (b.half + 1))
                    at_least(sp, s_s, XH * (b.n - 1))
                    for ab in range(2):
                        for r in range(4):
                            row = 64 * ab + XD * r
                            src = k_parts[b.par, r % 2, :, :].rearrange("(j a d) s -> a d j s", a=2, d=XD)
                            sp.dma_start(kst[row:row + XD, b.par, :, :], src[ab]).then_inc(s_kst[b.par], 16)

                def store(b):
                    sp.wait_ge(s_x1, b.n + 1)
                    sp.dma_start(x1[bass.ds(b.n * SQ, SQ), :], x1b[:, b.par, :]).then_inc(s_st[b.par], 16)

                for dst, src in ((wk, wk_t), (wv, wv_t), (wo, wo_t)):
                    sp.dma_start(dst[:, :, :], src.rearrange("(c p) e -> p c e", p=P)).then_inc(s_w, 16)
                for dst, src in ((bkc, bk), (bvc, bv)):
                    sp.dma_start(dst[:, :], src).then_inc(s_w, 16)
                sp.dma_start(bor[:, :], bo.rearrange("(a n) -> a n", a=1)).then_inc(s_w, 16)
                load_ctx(fixed(0))
                load_ctx(fixed(1))
                load_rest(fixed(0))
                sp.wait_ge(s_zero, 1)
                load_queries(fixed(0))
                stack_keys(fixed(0))

                def body(b):
                    if not is_last(b):
                        n = b.next()
                        load_queries(n)
                        load_rest(n)
                        if not is_last(n):
                            load_ctx(n.next())
                        stack_keys(n)
                    if not is_first(b):
                        store(b.before())

                batches(sp, body)
                store(fixed(NB - 1))
                for par in range(2):
                    sp.wait_ge(s_st[par], 16 * NB // 2)

            @block.gpsimd
            def _(pool):
                pool.memset(qst[:, :, :, :], 0.0).then_inc(s_zero, 1)
                pool.memset(vz[:, :, :, :, :, :], 0.0).then_inc(s_zero, 1)
                pool.memset(ex[:, :, :], 0.0).then_inc(s_zero, 1)
                pool.wait_ge(s_tg, 1)

                def body(b):
                    pool.wait_ge(s_mask[b.par], 16 * (b.half + 1))
                    at_least(pool, s_sm, XH * (b.n - 1))
                    pass_wait(pool, s_pass_pool)
                    pool.tensor_scalar(mbias[:, b.par, :], mraw[:, b.par, :], BIG, -BIG,
                                       ALU.mult, ALU.add).then_inc(s_mb, 1)
                    pool.wait_ge(s_x[b.par], 16 * (b.half + 1))
                    at_least(pool, s_x1, b.n - 1)
                    pool.tensor_tensor(xbias[:, b.par, :], xb[:, b.par, :], tgbo[0:SQ, :],
                                       ALU.add).then_inc(s_xb, 1)

                batches(pool, body)

            @block.vector
            def _(dve):
                dve.memset(ones[:, :], 1.0).then_inc(s_one, 1)
                dve.wait_ge(s_w, 96)
                dve.wait_ge(s_one, 1)
                for c in range(DC):
                    dve.tensor_scalar(bvb[:, c, :], ones[:, :], bvc[:, c:c + 1], None,
                                      ALU.mult).then_inc(s_bvb, 1)
                dve.wait_ge(s_bo, 1)
                dve.tensor_scalar(tgbo[:, :], p_p[:, 2, 0:D], k.tanh_g[:, 0:1], None,
                                  ALU.mult).then_inc(s_tg, 1)

                def key_lo(b, c):
                    dve.wait_ge(s_khi, DC * b.n + c + 1)
                    at_least(dve, s_kw[b.par], 32 * b.half)
                    dve.scalar_tensor_tensor(out=klo[:, b.par, c, :], in0=p_p[:, c, 0:SK],
                                             scalar=bkc[:, c:c + 1], in1=khi[:, b.par, c, :],
                                             op0=ALU.add, op1=ALU.subtract).then_inc(s_klo, 1)

                def masked(b, h):
                    if h == 0:
                        dve.wait_ge(s_mb, b.n + 1)
                    dve.wait_ge(s_s, XH * b.n + h + 1)
                    at_least(dve, s_ex, XH * b.n + h - 3)
                    pass_wait(dve, s_pass_dve)
                    dve.tensor_tensor_reduce(
                        out=sm[:, h % 4, :], in0=p_s[0:SQ, h % 2, 0:SK], in1=mbias[:, b.par, :],
                        scale=-0.25, scalar=BIG, op0=ALU.add, op1=ALU.min,
                        accum_out=nmax[:, h % 4:h % 4 + 1]).then_inc(s_sm, 1)

                def copy_ext(b, h):
                    dve.wait_ge(s_t, XH * b.n + h + 1)
                    at_least(dve, s_pv, XH * b.n + h - 3)
                    dve.tensor_copy(ext[:, h % 4, :], p_t[0:KW, h % 2, 0:KC * SQ]).then_inc(s_ext, 1)

                def rden_spread(b):
                    dve.wait_ge(s_ex, XH * (b.n + 1))
                    dve.reciprocal(rden[:, :], den[:, b.par, :]).then_inc(s_rd, 1)
                    dve.wait_ge(s_rd, b.n + 1)
                    at_least(dve, s_r, b.n)
                    dve.tensor_copy(rdx[:, :, :], rden[:, :].unsqueeze(2).broadcast_to([SQ, XH, XD])
                                    ).then_inc(s_rdx, 1)

                def normalize(b):
                    dve.wait_ge(s_pv, XH * (b.n + 1))
                    dve.wait_ge(s_rt, b.n + 1)
                    at_least(dve, s_o, b.n)
                    dve.tensor_tensor(an[:, :], p_a[:, 0:DC * SQ], rt[:, :], ALU.mult).then_inc(s_an, 1)

                def residual(b):
                    dve.wait_ge(s_o, b.n + 1)
                    dve.wait_ge(s_xb, b.n + 1)
                    at_least(dve, s_st[b.par], 16 * b.half)
                    dve.scalar_tensor_tensor(out=x1b[:, b.par, :], in0=p_p[0:SQ, 2, 0:D],
                                             scalar=k.tanh_g[0:SQ, 0:1], in1=xbias[:, b.par, :],
                                             op0=ALU.mult, op1=ALU.add).then_inc(s_x1, 1)

                key_lo(fixed(0), 0)
                key_lo(fixed(0), 1)

                def body(b):
                    for i in range(XH + 4):
                        if i >= 4:
                            copy_ext(b, i - 4)
                        if i < XH:
                            masked(b, i)
                        if i in (1, 2) and not is_last(b):
                            key_lo(b.next(), i - 1)
                        if i == 4 and not is_first(b):
                            residual(b.before())
                        if i == XH + 1:
                            rden_spread(b)
                    normalize(b)

                batches(dve, body)
                residual(fixed(NB - 1))

            @block.scalar
            def _(act):
                def key_hi(b, c):
                    act.wait_ge(s_k, DC * b.n + c + 1)
                    at_least(act, s_kw[b.par], 32 * b.half)
                    act.activation(khi[:, b.par, c, :], p_p[:, c, 0:SK], ACT.Identity,
                                   bias=bkc[:, c:c + 1]).then_inc(s_khi, 1)

                def values(b, c):
                    if c == 0:
                        at_least(act, s_pv, XH * (b.n - 1))
                    act.wait_ge(s_v, KC * b.n + c + 1)
                    rows = KW if c < KC - 1 else KL
                    act.activation(vz[0:rows, b.par, c, :, 0:3:2, :],
                                   p_p[0:rows, V_BANK[c], 0:D].rearrange("p (j a d) -> p j a d", a=2, d=XD),
                                   ACT.Copy).then_inc(s_vz, 1)

                def exp(b, h):
                    if h == 0:
                        at_least(act, s_rd, b.n - 1)
                    act.wait_ge(s_sm, XH * b.n + h + 1)
                    at_least(act, s_t, XH * b.n + h - 3)
                    act.activation(ex[:, h % 4, 0:SK], sm[:, h % 4, :], ACT.Exp, scale=-1.0,
                                   bias=nmax[:, h % 4:h % 4 + 1],
                                   accum_out=den[:, b.par, h:h + 1]).then_inc(s_ex, 1)

                def copy_rt(b):
                    act.wait_ge(s_r, b.n + 1)
                    at_least(act, s_an, b.n)
                    act.activation(rt[:, :], p_p[:, 2, 0:DC * SQ], ACT.Copy).then_inc(s_rt, 1)

                act.wait_ge(s_zero, 3)
                key_hi(fixed(0), 0)
                key_hi(fixed(0), 1)
                for c in range(KC):
                    values(fixed(0), c)

                def body(b):
                    for i in range(XH + 3):
                        if i in (1, 2) and not is_last(b):
                            key_hi(b.next(), i - 1)
                        if i < XH:
                            exp(b, i)
                        if i == 5 and not is_last(b):
                            values(b.next(), 0)
                    if not is_last(b):
                        values(b.next(), 1)
                        values(b.next(), 2)
                    copy_rt(b)

                batches(act, body)

            @block.tensor
            def _(pe):
                def keys(b, c):
                    if c == 0:
                        pe.wait_ge(s_ctx[b.par], 16 * (b.half + 1))
                    at_least(pe, s_vz, KC * b.n - 1 + c)
                    for kc in range(DC):
                        last = pe.matmul(p_p[:, c, 0:SK], wk[:, kc, c * P:(c + 1) * P],
                                         ctxb[:, b.par, kc, :], start=kc == 0, stop=kc == DC - 1)
                    last.then_inc(s_k, 1)

                def values(b, c):
                    if c == 0:
                        at_least(pe, s_x1, b.n - 1)
                    else:
                        pe.wait_ge(s_klo, DC * b.n + c)
                    rows = KW if c < KC - 1 else KL
                    for kc in range(DC):
                        last = pe.matmul(p_p[0:rows, V_BANK[c], 0:D],
                                         ctxb[:, b.par, kc, c * KW:c * KW + rows], wv[:, kc, :],
                                         start=kc == 0, stop=kc == DC - 1)
                    last.then_inc(s_v, 1)

                def scores(b, h):
                    if h == 0:
                        pe.wait_ge(s_kst[b.par], 128 * (b.half + 1))
                        pe.wait_ge(s_qst[b.par], 128 * (b.half + 1))
                    at_least(pe, s_sm, XH * b.n + h - 1)
                    pe.matmul(p_s[0:SQ, h % 2, 0:SK], qst[:, b.par, h, :], kst[:, b.par, h // 2, :],
                              start=True, stop=True).then_inc(s_s, 1)

                def turn(b, h):
                    pe.wait_ge(s_ex, XH * b.n + h + 1)
                    at_least(pe, s_ext, XH * b.n + h - 1)
                    for c in range(KC):
                        last = pe.transpose(p_t[0:KW, h % 2, c * SQ:(c + 1) * SQ],
                                            ex[:, h % 4, c * KW:(c + 1) * KW], k.ident[0:SQ, 0:SQ])
                    last.then_inc(s_t, 1)

                def attend(b, h):
                    if h == 0:
                        pe.wait_ge(s_vz, KC * (b.n + 1))
                        at_least(pe, s_an, b.n)
                    pe.wait_ge(s_ext, XH * b.n + h + 1)
                    row, col, odd = 32 * (h % XG // 2), SQ * (h // XG), h % 2
                    for c in range(KC):
                        v = vz[:, b.par, c, h // 2, :, :].rearrange("p a d -> p (a d)")
                        last = pe.matmul(p_a[row:row + 32, col:col + SQ], v[:, XD * odd:XD * odd + 32],
                                         ext[:, h % 4, c * SQ:(c + 1) * SQ],
                                         start=odd == 0 and c == 0, stop=odd == 1 and c == KC - 1)
                    last.then_inc(s_pv, 1)

                def turn_rden(b):
                    pe.wait_ge(s_rdx, b.n + 1)
                    pe.wait_ge(s_vz, KC * b.n + KC + (0 if is_last(b) else 1))
                    at_least(pe, s_x1, b.n)
                    for c in range(DC):
                        src = rdx[:, c * XG:(c + 1) * XG, :].rearrange("p h d -> p (h d)")
                        last = pe.transpose(p_p[:, 2, c * SQ:(c + 1) * SQ], src, k.ident[0:SQ, 0:SQ])
                    last.then_inc(s_r, 1)

                def project(b):
                    pe.wait_ge(s_an, b.n + 1)
                    for c in range(DC):
                        last = pe.matmul(p_p[0:SQ, 2, 0:D], an[:, c * SQ:(c + 1) * SQ], wo[:, c, :],
                                         start=c == 0, stop=c == DC - 1)
                    last.then_inc(s_o, 1)

                pe.wait_ge(s_w, 96)
                pe.wait_ge(s_bvb, DC)
                for c in range(DC):
                    pe.matmul(p_p[:, 2, 0:D], bvb[:, c, :], wo[:, c, :], start=c == 0, stop=False)
                pe.matmul(p_p[:, 2, 0:D], ones[0:1, :], bor[:, :], start=False,
                          stop=True).then_inc(s_bo, 1)
                keys(fixed(0), 0)
                keys(fixed(0), 1)
                pe.wait_ge(s_tg, 1)
                for c in range(KC):
                    values(fixed(0), c)

                def body(b):
                    for i in range(XH + 5):
                        if i < XH:
                            scores(b, i)
                        if i in (0, 1) and not is_last(b):
                            keys(b.next(), i)
                        if i == 2 and not is_first(b):
                            project(b.before())
                        if i == 4 and not is_last(b):
                            values(b.next(), 0)
                        if 3 <= i < XH + 3:
                            turn(b, i - 3)
                        if i in (XH, XH + 1) and not is_last(b):
                            values(b.next(), i - XH + 1)
                        if i >= 5:
                            attend(b, i - 5)
                        if i == XH + 3:
                            turn_rden(b)

                batches(pe, body)
                project(fixed(NB - 1))




def stage_experts_in(nc, k, x1, sel_t, q_t, k_t, v_t, rs, qk_out, v_out):
    with ExitStack() as ctx:
        m = Store(nc, ctx)
        big = m.sbuf("e_big", [P, NT * D])
        x1t = big[:, :].rearrange("p (t d) -> p t d", d=D)
        prob = big[:, 0:T].rearrange("p (g e) -> p g e", e=E)
        pick2 = big[:, T:2 * T].rearrange("p (g e) -> p g e", e=E)
        pick1 = k.gates[:, :].rearrange("p (g e) -> p g e", e=E)
        xn = m.sbuf("e_xn", [P, 2, D])
        xhi, xlo = (m.sbuf(f"e_x{n}", [P, DC, T], F16) for n in ("hi", "lo"))
        st, mv = m.sbuf("e_st", [P, NT, 6]), m.sbuf("e_mv", [P, NT, 2])
        std, rstd, half = (m.sbuf(n, [P, NT]) for n in ("e_std", "e_rstd", "e_half"))
        wst = m.sbuf("e_wst", [P, 2, DC, H * PD])
        sst = m.sbuf("e_sst", [P, DC, P])
        shi, slo = (m.sbuf(f"e_s{n}", [P, DC, P], F16) for n in ("hi", "lo"))
        qkhi, qklo = (m.sbuf(f"e_qk{n}", [P, DC, 2 * H * PD], F16) for n in ("hi", "lo"))
        vhi, vlo = (m.sbuf(f"e_v{n}", [P, DC, HE * PD], F16) for n in ("hi", "lo"))
        out = m.sbuf("e_out", [P, 2 * T])
        qko = out[:, :].rearrange("p (u t) -> p u t", u=2)
        vout = out[:, :].rearrange("p (t a d) -> p t a d", a=2, d=PD)
        order = m.sbuf("e_order", [P, E])
        rsb = m.sbuf("e_rs", [P, 1])
        m1, m2, top, tot = (m.sbuf(f"e_{n}", [P, NT * 2 * H]) for n in ("m1", "m2", "top", "tot"))
        acc = m.sbuf("e_acc", [P, 2, 2, PD])
        dsum = m.sbuf("e_dsum", [P, 2, PD])
        tmp = m.sbuf("e_tmp", [P, 2, 4, PD])
        tsum = m.sbuf("e_tsum", [P, 2, 2, PD])
        tsum1 = m.sbuf("e_tsum1", [P, 2, PD])
        p_t = m.psum("e_pt", [P, 2, 512])
        p_v = m.psum("e_pv", [P, 2, 2, 512])
        p_q = p_v[:, :, :, :].rearrange("p a b n -> p (a b) n")
        s_x, s_vst = m.sems("e_s_x", 5), m.sems("e_s_vst", 5)
        s_sel, s_rs, s_wq, s_wk = (m.sem(f"e_s_{n}") for n in ("sel", "rs", "wq", "wk"))
        s_vw, s_qo = m.sems("e_s_vw", 2), m.sems("e_s_qo", 2)
        s_ord, s_st, s_mv, s_step, s_std = (m.sem(f"e_s_{n}") for n in ("ord", "st", "mv", "step", "std"))
        s_whi, s_wlo, s_xn, s_t, s_xhi, s_xlo, s_l, s_p, s_g = (
            m.sem(f"e_s_{n}") for n in ("whi", "wlo", "xn", "tr", "xhi", "xlo", "l", "p", "g"))
        s_qk, s_qe, s_vhi, s_vlo, s_vp = (m.sem(f"e_s_{n}") for n in ("qk", "qe", "vhi", "vlo", "vp"))
        s_pass = m.sem("e_s_pass")
        s_even, s_odd, s_dv, s_av, s_ds, s_ts, s_ts1, s_vo = (
            m.sem(f"e_s_{n}") for n in ("even", "odd", "dv", "av", "ds", "ts", "ts1", "vo"))
        NG = NT * 2 * H
        QF = 4
        with nc.Block() as block:

            @block.sync
            def _(sp):
                for u in range(2):
                    sp.sem_inc(s_qo[u], 16)
                sp.dma_start(sst[:, :, :], sel_t.rearrange("(c p) e -> p c e", p=P)).then_inc(s_sel, 16)
                sp.dma_start(rsb[:, :], rs.partition_broadcast(P)).then_inc(s_rs, 16)
                for i in range(5):
                    sp.dma_start(x1t[:, 5 * i:5 * i + 5, :],
                                 x1[640 * i:640 * i + 640, :].rearrange("(t p) d -> p t d", p=P)
                                 ).then_inc(s_x[i], 16)
                sp.dma_start(wst[:, 0, :, :], q_t.rearrange("(c p) n -> p c n", p=P)).then_inc(s_wq, 16)
                sp.dma_start(wst[:, 1, :, :], k_t.rearrange("(c p) n -> p c n", p=P)).then_inc(s_wk, 16)
                for h in range(H):
                    if h < 2:
                        sp.wait_ge(s_wlo, 2 + h)
                    else:
                        sp.wait_ge(s_vlo, h - 1)
                    sp.dma_start(wst[:, h % 2, :, :],
                                 v_t[:, h * E * PD:(h + 1) * E * PD].rearrange("(c p) n -> p c n", p=P)
                                 ).then_inc(s_vw[h % 2], 16)
                with sp.Fori(0, H) as i:
                    for u in range(2):
                        sp.wait_ge(s_qe, QF + NC * (2 * i + u + 1))
                        sp.dma_start(qk_out[2 * i + u, :, :], qko[:, u, :]).then_inc(s_qo[u], 16)
                with sp.Fori(0, H // 2) as i:
                    for g in range(5):
                        sp.wait_ge(s_vo, 50 * i + 10 * (g + 1) + 2)
                        sp.dma_start(
                            v_out[640 * g:640 * g + 640, bass.ds(i * 2 * PD, 2 * PD)].rearrange(
                                "(t p) n -> p t n", p=P),
                            vout[:, 5 * g:5 * g + 5, :, :].rearrange("p t a d -> p t (a d)")
                        ).then_inc(s_vst[g], 16)
                for g in range(5):
                    sp.wait_ge(s_vst[g], 16 * (1 + H // 2))
                for u in range(2):
                    sp.wait_ge(s_qo[u], 16 * (H + 1))

            @block.gpsimd
            def _(pool):
                for g in range(5):
                    pool.sem_inc(s_vst[g], 16)
                pool.sem_inc(s_ts, 2)
                pool.sem_inc(s_vo, 2)
                for e in range(E):
                    pool.memset(order[:, e:e + 1], float(E - e)).then_inc(s_ord, 1)
                for u in range(2):
                    pool.wait_ge(s_qo[u], 16 * (H + 1))

                def unit(i, g, t, hh):
                    n = 50 * i + 2 * t + hh
                    pool.wait_ge(s_av, 4 * n + 12)
                    pool.tensor_tensor(tsum[:, hh, :, :], tmp[:, hh, 0:2, :], tmp[:, hh, 2:4, :],
                                       ALU.add).then_inc(s_ts, 1)
                    pool.wait_ge(s_ts, n + 3)
                    pool.wait_ge(s_vo, n + 1)
                    pool.tensor_tensor(tsum1[:, hh, :], tsum[:, hh, 0, :], tsum[:, hh, 1, :],
                                       ALU.add).then_inc(s_ts1, 1)
                    pool.wait_ge(s_ts1, n + 1)
                    pool.wait_ge(s_ds, n + 3)
                    pool.tensor_tensor(vout[:, t, hh, :], tsum1[:, hh, :], dsum[:, hh, :],
                                       ALU.add).then_inc(s_vo, 1)

                with pool.Fori(0, H // 2) as i:
                    for g in range(5):
                        pool.wait_ge(s_vst[g], 16 * i + 16)
                        pass_wait(pool, s_pass)
                        with pool.Fori(5 * g, 5 * g + 5) as t:
                            unit(i, g, t, 0)
                            unit(i, g, t, 1)

            @block.vector
            def _(dve):
                dve.sem_inc(s_ds, 2)
                dve.wait_ge(s_whi, 1)
                dve.scalar_tensor_tensor(out=slo[:, :, :], in0=sst[:, :, :], scalar=WS, in1=shi[:, :, :],
                                         op0=ALU.mult, op1=ALU.subtract).then_inc(s_wlo, 1)
                for t in range(NT):
                    if t % 5 == 0:
                        dve.wait_ge(s_x[t // 5], 16)
                    dve.bn_stats(st[:, t, :], x1t[:, t, :]).then_inc(s_st, 1)
                dve.wait_ge(s_st, NT)
                for t in range(NT):
                    dve.bn_aggr(mv[:, t, :], st[:, t, :]).then_inc(s_mv, 1)
                dve.wait_ge(s_mv, NT)
                rstd_steps(dve, mv, std, rstd, half, s_step, s_std, 0)

                def x_lo(t):
                    dve.wait_ge(s_xhi, t + 1)
                    dve.tensor_tensor(xlo[:, :, t * P:(t + 1) * P],
                                      p_t[:, t % 2, 0:DC * P].rearrange("p (c n) -> p c n", c=DC),
                                      xhi[:, :, t * P:(t + 1) * P], ALU.subtract).then_inc(s_xlo, 1)

                for t in range(NT):
                    at_least(dve, s_t, t - 1)
                    dve.tensor_scalar(xn[:, t % 2, :], x1t[:, t, :], mv[:, t, 0:1], rstd[:, t:t + 1],
                                      ALU.subtract, ALU.mult).then_inc(s_xn, 1)
                    if t >= 1:
                        x_lo(t - 1)
                x_lo(NT - 1)
                for w in range(2):
                    dve.wait_ge(s_whi, 2 + w)
                    dve.scalar_tensor_tensor(
                        out=qklo[:, :, w * H * PD:(w + 1) * H * PD], in0=wst[:, w, :, :], scalar=WS,
                        in1=qkhi[:, :, w * H * PD:(w + 1) * H * PD],
                        op0=ALU.mult, op1=ALU.subtract).then_inc(s_wlo, 1)

                def spread(v):
                    return v[:, :].unsqueeze(2).broadcast_to([P, NG, E])

                steps = [0]

                def step(ins):
                    ins.then_inc(s_g, 1)
                    steps[0] += 1
                    dve.wait_ge(s_g, steps[0])

                ranks = order[:, :].unsqueeze(1).broadcast_to([P, NG, E])
                dve.wait_ge(s_p, NT)
                dve.wait_ge(s_ord, E)
                step(dve.tensor_reduce(out=m1[:, :], in_=prob, axis=AX, op=ALU.max))
                step(dve.tensor_tensor(pick1, prob, spread(m1), ALU.is_equal))
                step(dve.tensor_tensor(pick1, pick1, ranks, ALU.mult))
                step(dve.tensor_reduce(out=top[:, :], in_=pick1, axis=AX, op=ALU.max))
                step(dve.tensor_tensor(pick1, pick1, spread(top), ALU.is_equal))
                step(dve.scalar_tensor_tensor(out=pick2, in0=pick1, scalar=-3.0, in1=prob,
                                              op0=ALU.mult, op1=ALU.add))
                step(dve.tensor_reduce(out=m2[:, :], in_=pick2, axis=AX, op=ALU.max))
                step(dve.tensor_tensor(pick2, pick2, spread(m2), ALU.is_equal))
                step(dve.tensor_tensor(pick2, pick2, ranks, ALU.mult))
                step(dve.tensor_reduce(out=top[:, :], in_=pick2, axis=AX, op=ALU.max))
                step(dve.tensor_tensor(pick2, pick2, spread(top), ALU.is_equal))
                step(dve.tensor_tensor(tot[:, :], m1[:, :], m2[:, :], ALU.add))
                step(dve.tensor_scalar(tot[:, :], tot[:, :], 1e-9, None, ALU.max))
                step(dve.reciprocal(tot[:, :], tot[:, :]))
                dve.wait_ge(s_rs, 16)
                step(dve.tensor_scalar(tot[:, :], tot[:, :], rsb[:, 0:1], None, ALU.mult))
                step(dve.tensor_scalar(tot[:, :], tot[:, :], 1.0 / WS, None, ALU.mult))
                step(dve.tensor_tensor(m1[:, :], m1[:, :], tot[:, :], ALU.mult))
                step(dve.tensor_tensor(m2[:, :], m2[:, :], tot[:, :], ALU.mult))
                step(dve.tensor_tensor(pick1, pick1, spread(m1), ALU.mult))
                step(dve.tensor_tensor(pick2, pick2, spread(m2), ALU.mult))
                step(dve.tensor_tensor(pick1, pick1, pick2, ALU.add))

                for h in range(H):
                    cut = slice(h * E * PD, (h + 1) * E * PD)
                    dve.wait_ge(s_vw[h % 2], 16 * (h // 2 + 1))
                    dve.tensor_scalar(vhi[:, :, cut], wst[:, h % 2, :, :], WS, None,
                                      ALU.mult).then_inc(s_vhi, 1)
                    dve.wait_ge(s_vhi, h + 1)
                    dve.scalar_tensor_tensor(out=vlo[:, :, cut], in0=wst[:, h % 2, :, :], scalar=WS,
                                             in1=vhi[:, :, cut], op0=ALU.mult,
                                             op1=ALU.subtract).then_inc(s_vlo, 1)

                def unit(i, t, hh):
                    n = 50 * i + 2 * t + hh
                    for e in range(4):
                        gate = k.gates[:, bass.ds(t * P + 2 * E * i + E * hh + e, 1)]
                        chain = s_even if e % 2 == 0 else s_odd
                        if e < 2:
                            if e == 0:
                                dve.wait_ge(s_vp, 2 * n + 1)
                                dve.wait_ge(s_ds, n + 1)
                            dve.tensor_scalar(acc[:, hh, e, :], p_v[:, hh, 0, e * PD:(e + 1) * PD], gate,
                                              None, ALU.mult).then_inc(chain, 1)
                        else:
                            dve.wait_ge(chain, 2 * n + 1)
                            last = dve.scalar_tensor_tensor(
                                out=acc[:, hh, e % 2, :], in0=p_v[:, hh, 0, e * PD:(e + 1) * PD],
                                scalar=gate, in1=acc[:, hh, e % 2, :], op0=ALU.mult, op1=ALU.add)
                            last.then_inc(chain, 1)
                    dve.wait_ge(s_even, 2 * n + 2)
                    dve.wait_ge(s_odd, 2 * n + 2)
                    dve.wait_ge(s_vo, n + 1)
                    dve.tensor_tensor(dsum[:, hh, :], acc[:, hh, 0, :], acc[:, hh, 1, :],
                                      ALU.add).then_inc(s_ds, 1)

                with dve.Fori(0, H // 2) as i:
                    with dve.Fori(0, NT) as t:
                        unit(i, t, 0)
                        unit(i, t, 1)

            @block.scalar
            def _(act):
                act.wait_ge(s_sel, 16)
                act.activation(shi[:, :, :], sst[:, :, :], ACT.Copy, scale=WS).then_inc(s_whi, 1)
                act.wait_ge(s_step, 1)
                act.activation(std[:, :], mv[:, :, 1], ACT.Sqrt).then_inc(s_std, 1)
                for w, landed in enumerate((s_wq, s_wk)):
                    act.wait_ge(landed, 16)
                    act.activation(qkhi[:, :, w * H * PD:(w + 1) * H * PD], wst[:, w, :, :], ACT.Copy,
                                   scale=WS).then_inc(s_whi, 1)
                for t in range(NT):
                    act.wait_ge(s_t, t + 1)
                    act.activation(xhi[:, :, t * P:(t + 1) * P],
                                   p_t[:, t % 2, 0:DC * P].rearrange("p (c n) -> p c n", c=DC),
                                   ACT.Copy).then_inc(s_xhi, 1)
                for t in range(NT):
                    act.wait_ge(s_l, t + 1)
                    act.activation(big[:, t * P:(t + 1) * P], p_t[:, t % 2, 0:P], ACT.Sigmoid,
                                   scale=1.0 / WS).then_inc(s_p, 1)
                act.sem_inc(s_qe, QF)
                with act.Fori(0, H) as i:
                    for u in range(2):
                        act.wait_ge(s_qo[u], 16 * i + 16)
                        for c in range(NC):
                            act.wait_ge(s_qk, NC * (2 * i + u) + c + 1)
                            act.activation(qko[:, u, c * NW:(c + 1) * NW], p_q[:, c % QF, 0:NW],
                                           ACT.Copy).then_inc(s_qe, 1)
                act.sem_inc(s_av, 8)

                def unit(i, t, hh):
                    n = 50 * i + 2 * t + hh
                    act.wait_ge(s_vp, 2 * n + 2)
                    act.wait_ge(s_ts, n + 1)
                    for e in range(4):
                        gate = k.gates[:, bass.ds(t * P + 2 * E * i + E * hh + 4 + e, 1)]
                        act.activation(tmp[:, hh, e, :], p_v[:, hh, 1, e * PD:(e + 1) * PD], ACT.Copy,
                                       scale=gate).then_inc(s_av, 1)

                with act.Fori(0, H // 2) as i:
                    with act.Fori(0, NT) as t:
                        unit(i, t, 0)
                        unit(i, t, 1)

            @block.tensor
            def _(pe):
                for t in range(NT):
                    pe.wait_ge(s_xn, t + 1)
                    at_least(pe, s_xlo, t - 1)
                    for c in range(DC):
                        last = pe.transpose(p_t[:, t % 2, c * P:(c + 1) * P],
                                            xn[:, t % 2, c * P:(c + 1) * P], k.ident[:, :])
                    last.then_inc(s_t, 1)
                pe.wait_ge(s_wlo, 1)
                pe.wait_ge(s_xlo, NT)
                for t in range(NT):
                    at_least(pe, s_p, t - 1)
                    tok = slice(t * P, (t + 1) * P)
                    for n, (c, a, b) in enumerate((c, a, b) for c in range(DC)
                                                  for a, b in ((xhi, shi), (xhi, slo), (xlo, shi))):
                        last = pe.matmul(p_t[:, t % 2, 0:P], a[:, c, tok], b[:, c, :],
                                         start=n == 0, stop=n == 3 * DC - 1)
                    last.then_inc(s_l, 1)
                pe.wait_ge(s_wlo, 3)
                with pe.Fori(0, 2 * H) as u:
                    for w in range(NC):
                        pe.wait_ge(s_qe, NC * u + w + 1)
                        tok = slice(w * NW, (w + 1) * NW)
                        for n, (c, a, b) in enumerate((c, a, b) for c in range(DC)
                                                      for a, b in ((qkhi, xhi), (qkhi, xlo), (qklo, xhi))):
                            last = pe.matmul(p_q[:, w % QF, 0:NW], a[:, c, bass.ds(u * PD, PD)],
                                             b[:, c, tok], start=n == 0, stop=n == 3 * DC - 1)
                        last.then_inc(s_qk, 1)
                pe.wait_ge(s_qe, QF + 2 * H * NC)
                pe.wait_ge(s_vlo, H)

                def unit(i, t, hh):
                    n = 50 * i + 2 * t + hh
                    for half in range(2):
                        if half == 0:
                            pe.wait_ge(s_ds, n + 1)
                        else:
                            pe.wait_ge(s_av, 4 * n + 4)
                        col = 2 * E * PD * i + E * PD * hh + half * 512
                        for j, (c, a, b) in enumerate((c, a, b) for c in range(DC)
                                                      for a, b in ((xhi, vhi), (xhi, vlo), (xlo, vhi))):
                            last = pe.matmul(p_v[:, hh, half, :], a[:, c, bass.ds(t * P, P)],
                                             b[:, c, bass.ds(col, 512)], start=j == 0, stop=j == 3 * DC - 1)
                        last.then_inc(s_vp, 1)

                with pe.Fori(0, H // 2) as i:
                    with pe.Fori(0, NT) as t:
                        unit(i, t, 0)
                        unit(i, t, 1)



def stage_attention(nc, k, qk, v, den, chi, clo):
    SCALE = PD ** -0.5 / WS ** 2
    GH = 4
    NGR = H // GH
    with ExitStack() as ctx:
        m = Store(nc, ctx)
        qb, kb = (m.sbuf(f"a_{n}", [P, 2, H, SQ]) for n in "qk")
        vb = m.sbuf("a_v", [SQ, 2, H * PD])
        mx, mxs = m.sbuf("a_mx", [SQ, NGR, GH]), m.sbuf("a_mxs", [SQ, NGR, GH])
        ex = m.sbuf("a_ex", [SQ, NGR, GH * SQ])
        ext = m.sbuf("a_ext", [SQ, NGR, GH * SQ])
        sums = m.sbuf("a_den", [SQ, 2, H])
        p_s, p_t, p_c = (m.psum(f"a_p{n}", [P, NGR, 512]) for n in "stc")
        s_q, s_k, s_v, s_den = (m.sems(f"a_s_{n}", 2) for n in ("q", "k", "v", "den"))
        s_s, s_mx, s_mxs, s_ex, s_t, s_ext, s_c, s_hi, s_lo = (
            m.sem(f"a_s_{n}") for n in ("s", "mx", "mxs", "ex", "t", "ext", "c", "hi", "lo"))
        with nc.Block() as block:

            @block.sync
            def _(sp):
                def load(b):
                    tok = bass.ds(b.n * SQ, SQ)
                    at_least(sp, s_s, NGR * (b.n - 1))
                    for dst, units, landed in ((qb, slice(0, H), s_q), (kb, slice(H, 2 * H), s_k)):
                        sp.dma_start(dst[:, b.par, :, :], qk[units, :, tok].rearrange("h p q -> p h q")
                                     ).then_inc(landed[b.par], 16)
                    at_least(sp, s_c, NGR * (b.n - 1))
                    sp.dma_start(vb[:, b.par, :], v[tok, :]).then_inc(s_v[b.par], 16)

                def store(b):
                    sp.wait_ge(s_ex, H * (b.n + 1))
                    sp.dma_start(den[bass.ds(b.n * SQ, SQ), :], sums[:, b.par, :]).then_inc(s_den[b.par], 16)

                load(fixed(0))

                def body(b):
                    if not is_last(b):
                        load(b.next())
                    store(b)

                batches(sp, body)
                for par in range(2):
                    sp.wait_ge(s_den[par], 16 * NB // 2)

            @block.vector
            def _(dve):
                def maxima(b, g):
                    dve.wait_ge(s_s, NGR * b.n + g + 1)
                    at_least(dve, s_mxs, NGR * (b.n - 1) + g + 1)
                    dve.tensor_reduce(out=mx[:, g, :], in_=p_s[0:SQ, g, 0:GH * SQ].rearrange(
                        "p (h s) -> p h s", h=GH), axis=AX, op=ALU.max).then_inc(s_mx, 1)
                    dve.wait_ge(s_mx, NGR * b.n + g + 1)
                    at_least(dve, s_ex, H * (b.n - 1) + GH * (g + 1))
                    dve.tensor_scalar(mxs[:, g, :], mx[:, g, :], -SCALE, None, ALU.mult).then_inc(s_mxs, 1)

                def copy_ext(b, g):
                    dve.wait_ge(s_t, NGR * b.n + g + 1)
                    at_least(dve, s_c, NGR * (b.n - 1) + g + 1)
                    dve.tensor_copy(ext[:, g, :], p_t[0:SQ, g, 0:GH * SQ]).then_inc(s_ext, 1)

                def low(b, g):
                    dve.wait_ge(s_hi, NGR * b.n + g + 1)
                    heads, tok = slice(GH * g, GH * (g + 1)), bass.ds(b.n * SQ, SQ)
                    dve.tensor_tensor(clo[:, heads, tok],
                                      p_c[:, g, 0:GH * SQ].rearrange("p (h s) -> p h s", h=GH),
                                      chi[:, heads, tok], ALU.subtract).then_inc(s_lo, 1)

                def body(b):
                    maxima(b, 0)
                    if not is_first(b):
                        copy_ext(b.before(), 0)
                        copy_ext(b.before(), 1)
                    maxima(b, 1)
                    if not is_first(b):
                        low(b.before(), 0)
                        low(b.before(), 1)

                batches(dve, body)
                last = fixed(NB - 1)
                copy_ext(last, 0)
                copy_ext(last, 1)
                low(last, 0)
                low(last, 1)

            @block.scalar
            def _(act):
                def exps(b, g):
                    if g == 0:
                        at_least(act, s_den[b.par], 16 * b.half)
                    act.wait_ge(s_mxs, NGR * b.n + g + 1)
                    at_least(act, s_t, NGR * (b.n - 1) + g + 1)
                    for h in range(GH):
                        act.activation(ex[:, g, h * SQ:(h + 1) * SQ], p_s[0:SQ, g, h * SQ:(h + 1) * SQ],
                                       ACT.Exp, bias=mxs[:, g, h:h + 1], scale=SCALE,
                                       accum_out=sums[:, b.par, GH * g + h:GH * g + h + 1]
                                       ).then_inc(s_ex, 1)

                def high(b, g):
                    act.wait_ge(s_c, NGR * b.n + g + 1)
                    act.activation(chi[:, GH * g:GH * (g + 1), bass.ds(b.n * SQ, SQ)],
                                   p_c[:, g, 0:GH * SQ].rearrange("p (h s) -> p h s", h=GH),
                                   ACT.Copy).then_inc(s_hi, 1)

                def body(b):
                    exps(b, 0)
                    exps(b, 1)
                    if not is_first(b):
                        high(b.before(), 0)
                        high(b.before(), 1)

                batches(act, body)
                high(fixed(NB - 1), 0)
                high(fixed(NB - 1), 1)

            @block.tensor
            def _(pe):
                def scores(b, g):
                    if g == 0:
                        pe.wait_ge(s_q[b.par], 16 * (b.half + 1))
                        pe.wait_ge(s_k[b.par], 16 * (b.half + 1))
                    at_least(pe, s_ex, H * (b.n - 1) + GH * (g + 1))
                    for j in range(GH):
                        h = GH * g + j
                        last = pe.matmul(p_s[0:SQ, g, j * SQ:(j + 1) * SQ], qb[:, b.par, h, :],
                                         kb[:, b.par, h, :], start=True, stop=True)
                    last.then_inc(s_s, 1)

                def turn(b, g):
                    pe.wait_ge(s_ex, H * b.n + GH * (g + 1))
                    at_least(pe, s_ext, NGR * (b.n - 1) + g + 1)
                    for j in range(GH):
                        cut = slice(j * SQ, (j + 1) * SQ)
                        last = pe.transpose(p_t[0:SQ, g, cut], ex[:, g, cut], k.ident[0:SQ, 0:SQ])
                    last.then_inc(s_t, 1)

                def attend(b, g):
                    pe.wait_ge(s_v[b.par], 16 * (b.half + 1))
                    pe.wait_ge(s_ext, NGR * b.n + g + 1)
                    at_least(pe, s_lo, NGR * (b.n - 1) + g + 1)
                    for j in range(GH):
                        h, cut = GH * g + j, slice(j * SQ, (j + 1) * SQ)
                        last = pe.matmul(p_c[:, g, cut], vb[:, b.par, h * PD:(h + 1) * PD],
                                         ext[:, g, cut], start=True, stop=True)
                    last.then_inc(s_c, 1)

                def body(b):
                    scores(b, 0)
                    if not is_first(b):
                        turn(b.before(), 0)
                        turn(b.before(), 1)
                    scores(b, 1)
                    if not is_first(b):
                        attend(b.before(), 0)
                        attend(b.before(), 1)

                batches(pe, body)
                last = fixed(NB - 1)
                turn(last, 0)
                turn(last, 1)
                attend(last, 0)
                attend(last, 1)


def stage_experts_out(nc, k, x1, o_w, den, chi, clo, y):
    with ExitStack() as ctx:
        m = Store(nc, ctx)
        main = m.sbuf("o_main", [P, NT, D])
        side = m.sbuf("o_side", [P, NT, D])
        dent = m.sbuf("o_den", [P, NT, H])
        wst = m.sbuf("o_wst", [P, E * D])
        whi, wlo = (m.sbuf(f"o_w{n}", [P, 2, E * D], F16) for n in ("hi", "lo"))
        tmp = m.sbuf("o_tmp", [P, 2, D])
        p_y = m.psum("o_py", [P, 4, 2, D])
        s_x, s_y = m.sem("o_s_x"), m.sem("o_s_y")
        s_pass_pool, s_pass_pe = m.sem("o_s_pass_pool"), m.sem("o_s_pass_pe")
        s_dl, s_g, s_w, s_whi, s_wlo = (m.sem(f"o_s_{n}") for n in ("dl", "g", "w", "whi", "wlo"))
        s_p, s_av, s_main, s_side, s_pool, s_end = (
            m.sem(f"o_s_{n}") for n in ("p", "av", "main", "side", "pool", "end"))
        go = k.gates[:, :].rearrange("p (t a h e) -> p t a h e", a=2, h=H, e=E)[:, :, 1, :, :]
        MID = 12

        def heads(eng, body):
            with eng.Fori(0, H // 2 - 1) as i:
                body(2 * i, 0, True)
                body(2 * i + 1, 1, True)
            body(H - 2, 0, True)
            body(H - 1, 1, False)

        with nc.Block() as block:

            @block.sync
            def _(sp):
                sp.dma_start(dent[:, :, :], den.rearrange("(t p) h -> p t h", p=P)).then_inc(s_dl, 16)
                sp.dma_start(wst[:, :], o_w[:, 0:E * D]).then_inc(s_w, 16)
                sp.dma_start(main[:, :, :], x1.rearrange("(t p) d -> p t d", p=P)).then_inc(s_x, 16)
                with sp.Fori(1, H) as h:
                    sp.wait_ge(s_wlo, h)
                    sp.dma_start(wst[:, :], o_w[:, bass.ds(h * E * D, E * D)]).then_inc(s_w, 16)
                for g in range(5):
                    sp.wait_ge(s_end, g + 1)
                    sp.dma_start(y[640 * g:640 * g + 640, :].rearrange("(t p) d -> p t d", p=P),
                                 main[:, 5 * g:5 * g + 5, :]).then_inc(s_y, 16)
                sp.wait_ge(s_y, 80)

            @block.gpsimd
            def _(pool):
                pool.memset(side[:, :, :], 0.0).then_inc(s_pool, 2 * NT)

                def tile(h, t):
                    n = NT * h + t
                    pool.wait_ge(s_side, 3 * n + 6)
                    for j in range(2):
                        pool.wait_ge(s_av, 2 * n + j + 3)
                        pool.wait_ge(s_pool, 2 * NT + 2 * n + j)
                        pass_wait(pool, s_pass_pool)
                        pool.tensor_tensor(side[:, t, :], side[:, t, :], tmp[:, j, :],
                                           ALU.add).then_inc(s_pool, 1)

                with pool.Fori(0, H) as h:
                    with pool.Fori(0, NT) as t:
                        tile(h, t)

            @block.vector
            def _(dve):
                dve.sem_inc(s_side, 3)
                dve.wait_ge(s_dl, 16)
                dve.reciprocal(dent[:, :, :], dent[:, :, :]).then_inc(s_g, 1)
                dve.wait_ge(s_g, 1)
                dve.tensor_scalar(dent[:, :, :], dent[:, :, :], k.tanh_g[:, 1:2], None,
                                  ALU.mult).then_inc(s_g, 1)
                dve.wait_ge(s_g, 2)
                dve.tensor_tensor(go, go, dent[:, :, :].unsqueeze(3).broadcast_to([P, NT, H, E]),
                                  ALU.mult).then_inc(s_g, 1)

                def split(h, buf):
                    dve.wait_ge(s_whi, h + 1)
                    dve.scalar_tensor_tensor(out=wlo[:, buf, :], in0=wst[:, :], scalar=WS,
                                             in1=whi[:, buf, :], op0=ALU.mult,
                                             op1=ALU.subtract).then_inc(s_wlo, 1)

                split(0, 0)
                dve.wait_ge(s_x, 16)
                dve.wait_ge(s_g, 3)

                def tile(h, t):
                    n = NT * h + t
                    dve.wait_ge(s_pool, 2 * n + 2)
                    for q in range(3):
                        dve.wait_ge(s_p, 4 * n + q + 1)
                        for j, (into, chain) in enumerate(((main, s_main), (side, s_side))):
                            if q > 0:
                                dve.wait_ge(chain, 3 * n + q + 3 * j)
                            gate = k.gates[:, bass.ds(t * P + HE + h * E + 2 * q + j, 1)]
                            last = dve.scalar_tensor_tensor(
                                out=into[:, t, :], in0=p_y[:, q, j, :], scalar=gate, in1=into[:, t, :],
                                op0=ALU.mult, op1=ALU.add)
                            last.then_inc(chain, 1)

                def head(h, buf, more):
                    with dve.Fori(0, MID) as t:
                        tile(h, t)
                    if more:
                        split(h + 1, 1 - buf)
                    with dve.Fori(MID, NT) as t:
                        tile(h, t)

                heads(dve, head)
                dve.wait_ge(s_pool, 2 * NT * (H + 1))
                dve.wait_ge(s_main, 3 * NT * H)
                for g in range(5):
                    cut = slice(5 * g, 5 * g + 5)
                    dve.tensor_tensor(main[:, cut, :], main[:, cut, :], side[:, cut, :],
                                      ALU.add).then_inc(s_end, 1)

            @block.scalar
            def _(act):
                act.sem_inc(s_av, 2)

                def split(h, buf):
                    act.wait_ge(s_w, 16 * (h + 1))
                    act.activation(whi[:, buf, :], wst[:, :], ACT.Copy, scale=WS).then_inc(s_whi, 1)

                split(0, 0)
                act.wait_ge(s_g, 3)

                def tile(h, t):
                    n = NT * h + t
                    act.wait_ge(s_p, 4 * n + 4)
                    for j in range(2):
                        act.wait_ge(s_pool, 2 * NT + 2 * n - 1 + j)
                        gate = k.gates[:, bass.ds(t * P + HE + h * E + 6 + j, 1)]
                        act.activation(tmp[:, j, :], p_y[:, 3, j, :], ACT.Copy,
                                       scale=gate).then_inc(s_av, 1)

                def head(h, buf, more):
                    with act.Fori(0, MID) as t:
                        tile(h, t)
                    if more:
                        split(h + 1, 1 - buf)
                    with act.Fori(MID, NT) as t:
                        tile(h, t)

                heads(act, head)

            @block.tensor
            def _(pe):
                def tile(h, buf, t):
                    n = NT * h + t
                    for q in range(4):
                        if q < 3:
                            pe.wait_ge(s_side, 3 * n + q + 1)
                        else:
                            pe.wait_ge(s_av, 2 * n + 2)
                        cut = slice(2 * D * q, 2 * D * (q + 1))
                        for j, (a, b) in enumerate(((chi, whi), (chi, wlo), (clo, whi))):
                            last = pe.matmul(p_y[:, q, :, :].rearrange("p j d -> p (j d)"),
                                             a[:, h, bass.ds(t * P, P)], b[:, buf, cut],
                                             start=j == 0, stop=j == 2)
                        last.then_inc(s_p, 1)

                def head(h, buf, more):
                    pe.wait_ge(s_wlo, h + 1)
                    pass_wait(pe, s_pass_pe)
                    with pe.Fori(0, NT) as t:
                        tile(h, buf, t)

                heads(pe, head)


class Constants:
    pass


def constants(nc, ctx):
    k = Constants()
    m = Store(nc, ctx)
    k.ident = m.sbuf("ident", [P, P])
    k.tanh_g = m.sbuf("tanh_g", [P, 2])
    k.gates = m.sbuf("gates", [P, NT * 2 * HE])
    return k


def flamingo(nc, x, ctx_t, mask, g_xattn, g_ffn, wq, bq, wk, bk, wv, bv, wo, bo, sel, qw, kw, vw, ow, rs, y):
    def scratch(name, shape, dt=F32):
        return nc.dram_tensor(name, shape, dt, kind="Internal").ap()

    q_parts = scratch("q_parts", [2, D, T], F16)
    k_parts = scratch("k_parts", [2, 2, D, SK], F16)
    x1 = scratch("x1", [T, D])
    qk = scratch("qk", [2 * H, PD, T])
    v = scratch("v", [T, H * PD])
    den = scratch("den", [T, H])
    with ExitStack() as ctx:
        k = constants(nc, ctx)
        stage_queries(nc, k, x, g_xattn, g_ffn, wq, bq, q_parts)
        stage_cross(nc, k, x, ctx_t, mask, wk, bk, wv, bv, wo, bo, q_parts, k_parts, x1)
        stage_experts_in(nc, k, x1, sel, qw, kw, vw, rs, qk, v)
        with ExitStack() as inner:
            m = Store(nc, inner)
            chi, clo = (m.sbuf(f"c_{n}", [P, H, T], F16) for n in ("high", "low"))
            stage_attention(nc, k, qk, v, den, chi, clo)
            stage_experts_out(nc, k, x1, ow, den, chi, clo, y)


def kernel(**inputs):
    import concourse.bacc as bacc
    import numpy as np
    from concourse.bass_utils import run_bass_kernel_spmd

    def arr(name):
        return np.asarray(inputs[name])

    def turned(name):
        return np.ascontiguousarray(arr(name).T)

    def column(name):
        return np.ascontiguousarray(arr(name).reshape(DC, P).T)

    sel = np.concatenate([arr("L0_ffn_sel_v_w"), arr("L0_ffn_sel_o_w")], axis=0)
    arrays = {
        "x": np.ascontiguousarray(arr("x").reshape(T, D)),
        "ctx_t": np.ascontiguousarray(arr("ctx_1024").transpose(0, 2, 1)),
        "mask": np.ascontiguousarray(arr("mask_BxSxS2_bf1")).view(np.uint8),
        "g_xattn": arr("g_xattn"),
        "g_ffn": arr("g_ffn"),
        "wq": turned("L0_xattn_Wq"), "bq": column("L0_xattn_bq"),
        "wk": turned("L0_xattn_Wk"), "bk": column("L0_xattn_bk"),
        "wv": turned("L0_xattn_Wv"), "bv": column("L0_xattn_bv"),
        "wo": turned("L0_xattn_Wo"), "bo": arr("L0_xattn_bo"),
        "sel": np.ascontiguousarray(sel.T),
        "q_w": turned("L0_ffn_q_w"),
        "k_w": turned("L0_ffn_k_w"),
        "v_w": np.ascontiguousarray(arr("L0_ffn_v_w").transpose(1, 0, 2).reshape(D, HE * PD)),
        "o_w": np.ascontiguousarray(arr("L0_ffn_o_w").transpose(1, 0, 2).reshape(PD, HE * D)),
        "route_scale": arr("L0_ffn_route_scale"),
    }
    nc = bacc.Bacc("TRN2", target_bir_lowering=False, num_devices=1)
    ins = {f"in_{n}": a for n, a in arrays.items()}
    args = [nc.dram_tensor(n, a.shape, mybir.dt.from_np(a.dtype), kind="ExternalInput").ap()
            for n, a in ins.items()]
    y = nc.dram_tensor("y", (T, D), F32, kind="ExternalOutput").ap()
    flamingo(nc, *args, y)
    r = run_bass_kernel_spmd(nc, [ins], core_ids=[0])
    return r.results[0]["y"].reshape(NB, SQ, D)
```

```python
from contextlib import ExitStack

import concourse.bass as bass
from concourse import mybir

F32 = mybir.dt.float32
F16 = mybir.dt.float16
U8 = mybir.dt.uint8
ALU = mybir.AluOpType
ACT = mybir.ActivationFunctionType
AX = mybir.AxisListType.X

NB, SQ, SK, D = 32, 100, 361, 256
T = NB * SQ
P = 128
NT = T // P
DC = D // P
XH, XD = 16, 16
XG = P // XD
KC = 3
KW = -(-SK // KC)
SKP = KC * KW
KL = SK - (KC - 1) * KW
H, E, PD = 8, 8, 128
HE = H * E
WS = 64.0
EPS = 1e-5
BIG = 3.4028234663852886e38
NW = 400
NC = T // NW


def at_least(eng, sem, value):
    if not isinstance(value, int) or value > 0:
        eng.wait_ge(sem, value)


def pass_wait(eng, passed):
    eng.sem_inc(passed, 1)


class Batch:

    def __init__(self, n, par, half):
        self.n, self.par, self.half = n, par, half

    def next(self):
        return Batch(self.n + 1, 1 - self.par, self.half + self.par)

    def before(self):
        return Batch(self.n - 1, 1 - self.par, self.half - (1 - self.par))


def fixed(n):
    return Batch(n, n % 2, n // 2)


def batches(eng, body):
    body(fixed(0))
    body(fixed(1))
    with eng.Fori(1, NB // 2 - 1) as i:
        body(Batch(2 * i, 0, i))
        body(Batch(2 * i + 1, 1, i))
    body(fixed(NB - 2))
    body(fixed(NB - 1))


def is_first(b):
    return isinstance(b.n, int) and b.n == 0


def is_last(b):
    return isinstance(b.n, int) and b.n == NB - 1


class Store:

    def __init__(self, nc, ctx):
        self.nc, self.ctx = nc, ctx

    def sbuf(self, name, shape, dt=F32):
        return self.ctx.enter_context(self.nc.sbuf_tensor(name, shape, dt))

    def psum(self, name, shape):
        return self.ctx.enter_context(self.nc.psum_tensor(name, shape, F32))

    def sem(self, name):
        return self.ctx.enter_context(self.nc.semaphore(name))

    def sems(self, name, n):
        return [self.sem(f"{name}_{i}") for i in range(n)]


def rstd_steps(dve, mv, std, rstd, half, s_step, s_std, base):
    var = mv[:, :, 1]
    dve.tensor_scalar(var, var, EPS, None, ALU.add).then_inc(s_step, 1)
    dve.wait_ge(s_std, 1)
    dve.reciprocal(rstd[:, :], std[:, :]).then_inc(s_step, 1)
    dve.wait_ge(s_step, base + 2)
    dve.tensor_tensor(half[:, :], rstd[:, :], rstd[:, :], ALU.mult).then_inc(s_step, 1)
    dve.wait_ge(s_step, base + 3)
    dve.tensor_tensor(half[:, :], half[:, :], var, ALU.mult).then_inc(s_step, 1)
    dve.wait_ge(s_step, base + 4)
    dve.tensor_scalar(half[:, :], half[:, :], -0.5, 1.5, ALU.mult, ALU.add).then_inc(s_step, 1)
    dve.wait_ge(s_step, base + 5)
    dve.tensor_tensor(rstd[:, :], rstd[:, :], half[:, :], ALU.mult).then_inc(s_step, 1)
    dve.wait_ge(s_step, base + 6)


def tiles(eng, body):
    for t in range(3):
        body(t, t % 2)
    with eng.Fori(0, (NT - 3) // 2) as i:
        body(2 * i + 3, 1)
        body(2 * i + 4, 0)


def stage_queries(nc, k, x, g_xattn, g_ffn, wq_t, bq, q_parts):
    with ExitStack() as ctx:
        m = Store(nc, ctx)
        xt = m.sbuf("q_x", [P, NT, D])
        xn = m.sbuf("q_xn", [P, 2, D])
        xnt = m.sbuf("q_xnt", [P, DC, T])
        wq = m.sbuf("q_wq", [P, DC, D])
        bqc = m.sbuf("q_bq", [P, DC])
        st = m.sbuf("q_st", [P, NT, 6])
        mv = m.sbuf("q_mv", [P, NT, 2])
        std, rstd, half = (m.sbuf(n, [P, NT]) for n in ("q_std", "q_rstd", "q_half"))
        qhi = m.sbuf("q_hi", [P, DC, T], F16)
        qlo = m.sbuf("q_lo", [P, DC, T], F16)
        pt = m.psum("q_pt", [P, 2, 512])
        pq = m.psum("q_pq", [P, 4, 512])
        s_x = m.sems("q_s_x", 5)
        s_w = m.sem("q_s_w")
        s_id = m.sem("q_s_id")
        s_g, s_tanh = m.sem("q_s_g"), m.sem("q_s_tanh")
        s_st, s_mv, s_step, s_std = (m.sem(f"q_s_{n}") for n in ("st", "mv", "step", "std"))
        s_xn, s_t, s_xnt, s_q, s_hi, s_lo, s_out = (
            m.sem(f"q_s_{n}") for n in ("xn", "t", "xnt", "q", "hi", "lo", "out"))
        with nc.Block() as block:

            @block.sync
            def _(sp):
                for i in range(5):
                    sp.dma_start(xt[:, 5 * i:5 * i + 5, :],
                                 x[640 * i:640 * i + 640, :].rearrange("(t p) d -> p t d", p=P)
                                 ).then_inc(s_x[i], 16)
                sp.dma_start(wq[:, :, :], wq_t.rearrange("(c p) e -> p c e", p=P)).then_inc(s_w, 16)
                sp.dma_start(bqc[:, :], bq).then_inc(s_w, 16)
                for i, g in enumerate((g_xattn, g_ffn)):
                    sp.dma_start(k.tanh_g[:, i:i + 1], g.partition_broadcast(P)).then_inc(s_g, 16)
                for g in range(2):
                    cut = slice(g * T // 2, (g + 1) * T // 2)
                    sp.wait_ge(s_hi, DC * NC // 2 * (g + 1))
                    sp.dma_start(q_parts[0, :, cut].rearrange("(c p) t -> p c t", p=P),
                                 qhi[:, :, cut]).then_inc(s_out, 16)
                    sp.wait_ge(s_lo, DC * NC // 2 * (g + 1))
                    sp.dma_start(q_parts[1, :, cut].rearrange("(c p) t -> p c t", p=P),
                                 qlo[:, :, cut]).then_inc(s_out, 16)
                sp.wait_ge(s_out, 64)

            @block.gpsimd
            def _(pool):
                pool.memset(k.ident[:, :], 0.0).then_inc(s_id, 1)
                pool.wait_ge(s_id, 1)
                pool.affine_select(out=k.ident[:, :], in_=k.ident[:, :], compare_op=ALU.not_equal,
                                   fill=1.0, base=0, pattern=[[-1, P]],
                                   channel_multiplier=1).then_inc(s_id, 1)

            @block.vector
            def _(dve):
                for t in range(NT):
                    if t % 5 == 0:
                        dve.wait_ge(s_x[t // 5], 16)
                    dve.bn_stats(st[:, t, :], xt[:, t, :]).then_inc(s_st, 1)
                dve.wait_ge(s_st, NT)
                for t in range(NT):
                    dve.bn_aggr(mv[:, t, :], st[:, t, :]).then_inc(s_mv, 1)
                dve.wait_ge(s_mv, NT)
                rstd_steps(dve, mv, std, rstd, half, s_step, s_std, 0)

                def normalize(t, par):
                    at_least(dve, s_t, t - 1)
                    dve.tensor_scalar(xn[:, par, :], xt[:, t, :], mv[:, t, 0:1], rstd[:, t:t + 1],
                                      ALU.subtract, ALU.mult).then_inc(s_xn, 1)

                for t in range(NT):
                    normalize(t, t % 2)
                dve.wait_ge(s_w, 32)
                for n in range(DC * NC):
                    c, w = n % DC, n // DC
                    dve.wait_ge(s_hi, n + 1)
                    dve.scalar_tensor_tensor(
                        out=qlo[:, c, w * NW:(w + 1) * NW], in0=pq[:, n % 4, 0:NW],
                        scalar=bqc[:, c:c + 1], in1=qhi[:, c, w * NW:(w + 1) * NW],
                        op0=ALU.add, op1=ALU.subtract).then_inc(s_lo, 1)

            @block.scalar
            def _(act):
                act.wait_ge(s_g, 32)
                act.activation(k.tanh_g[:, :], k.tanh_g[:, :], ACT.Tanh).then_inc(s_tanh, 1)
                act.wait_ge(s_step, 1)
                act.activation(std[:, :], mv[:, :, 1], ACT.Sqrt).then_inc(s_std, 1)
                for t in range(NT):
                    act.wait_ge(s_t, t + 1)
                    act.activation(xnt[:, :, t * P:(t + 1) * P],
                                   pt[:, t % 2, 0:DC * P].rearrange("p (c n) -> p c n", c=DC),
                                   ACT.Copy).then_inc(s_xnt, 1)
                act.wait_ge(s_w, 32)
                for n in range(DC * NC):
                    c, w = n % DC, n // DC
                    act.wait_ge(s_q, n + 1)
                    act.activation(qhi[:, c, w * NW:(w + 1) * NW], pq[:, n % 4, 0:NW],
                                   ACT.Identity, bias=bqc[:, c:c + 1]).then_inc(s_hi, 1)

            @block.tensor
            def _(pe):
                pe.wait_ge(s_id, 2)
                for t in range(NT):
                    pe.wait_ge(s_xn, t + 1)
                    at_least(pe, s_xnt, t - 1)
                    for c in range(DC):
                        last = pe.transpose(pt[:, t % 2, c * P:(c + 1) * P],
                                            xn[:, t % 2, c * P:(c + 1) * P], k.ident[:, :])
                    last.then_inc(s_t, 1)
                pe.wait_ge(s_w, 32)
                pe.wait_ge(s_xnt, NT)
                for n in range(DC * NC):
                    c, w = n % DC, n // DC
                    at_least(pe, s_lo, n - 3)
                    for kc in range(DC):
                        last = pe.matmul(pq[:, n % 4, 0:NW], wq[:, kc, c * P:(c + 1) * P],
                                         xnt[:, kc, w * NW:(w + 1) * NW],
                                         start=kc == 0, stop=kc == DC - 1)
                    last.then_inc(s_q, 1)


def stage_cross(nc, k, x, ctx_t, mask, wk_t, bk, wv_t, bv, wo_t, bo, q_parts, k_parts, x1):
    LAG_T, LAG_C, LAG_A = 3, 4, 5
    RT = 256
    ACT_COPIES = (1, 4, 7, 10, 13, 15)

    def lagging(b, i, lag, work):
        if lag <= i < XH + lag:
            work(b, i - lag)
        elif i < lag and not is_first(b):
            work(b.before(), i - lag + XH)

    with ExitStack() as ctx:
        m = Store(nc, ctx)
        wk, wv, wo = (m.sbuf(f"c_{n}", [P, DC, D]) for n in ("wk", "wv", "wo"))
        bkc, bvc = m.sbuf("c_bk", [P, DC]), m.sbuf("c_bv", [P, DC])
        bor = m.sbuf("c_bo", [1, D])
        ones = m.sbuf("c_ones", [P, P])
        bvb = m.sbuf("c_bvb", [P, DC, P])
        tgbo = m.sbuf("c_tgbo", [P, D])
        ctxb = m.sbuf("c_ctx", [P, 2, DC, SK])
        khi, klo = (m.sbuf(f"c_k{n}", [P, 2, DC, SK], F16) for n in ("hi", "lo"))
        kst = m.sbuf("c_kst", [P, 2, XH // 2, SK], F16)
        qst = m.sbuf("c_qst", [P, 2, XH, SQ], F16)
        vz = m.sbuf("c_v", [KW, 2, KC, XH // 2, 3, XD])
        mraw = m.sbuf("c_mraw", [SQ, 2, SK], U8)
        mbias = m.sbuf("c_mbias", [SQ, 2, SK])
        xb = m.sbuf("c_xb", [SQ, 2, D])
        xbias = m.sbuf("c_xbias", [SQ, 2, D])
        x1b = m.sbuf("c_x1", [SQ, 2, D])
        sm = m.sbuf("c_sm", [SQ, 4, SK])
        nmax = m.sbuf("c_nmax", [SQ, 4])
        ex = m.sbuf("c_ex", [SQ, 4, SKP])
        ext = m.sbuf("c_ext", [KW, 4, KC * SQ])
        den = m.sbuf("c_den", [SQ, 2, XH])
        rden = m.sbuf("c_rden", [SQ, XH])
        rdx = m.sbuf("c_rdx", [SQ, XH, XD])
        rt = m.sbuf("c_rt", [P, DC * SQ])
        an = m.sbuf("c_an", [P, DC * SQ])
        p_s = m.psum("c_ps", [P, 2, 512])
        p_t = m.psum("c_pt", [P, 2, 512])
        p_a = m.psum("c_pa", [P, 2, 512])
        p_p = m.psum("c_pp", [P, 2, 512])
        s_w, s_one, s_zero, s_bvb, s_bo, s_tg = (m.sem(f"c_s_{n}") for n in ("w", "one", "zero", "bvb", "bo", "tg"))
        s_ctx, s_kw, s_kst, s_qst, s_mask, s_x, s_st = (
            m.sems(f"c_s_{n}", 2) for n in ("ctx", "kw", "kst", "qst", "mask", "x", "st"))
        s_k, s_khi, s_klo, s_v, s_vz, s_mb, s_xb = (
            m.sem(f"c_s_{n}") for n in ("k", "khi", "klo", "v", "vz", "mb", "xb"))
        s_s, s_sm, s_ex, s_t, s_extd, s_exta, s_pv = (
            m.sem(f"c_s_{n}") for n in ("s", "sm", "ex", "tr", "extd", "exta", "pv"))
        s_pass_dve, s_pass_pool, s_pass_sp = (m.sem(f"c_s_pass_{n}") for n in ("dve", "pool", "sp"))
        s_rd, s_rdx, s_r, s_rt, s_an, s_o, s_x1 = (
            m.sem(f"c_s_{n}") for n in ("rd", "rdx", "r", "rt", "an", "o", "x1"))

        def wait_copy(eng, b, h):
            if h < 0:
                if is_first(b):
                    return
                b, h = b.before(), h + XH
            by_act = sum(j in ACT_COPIES for j in range(h + 1))
            if h in ACT_COPIES:
                eng.wait_ge(s_exta, len(ACT_COPIES) * b.n + by_act)
            else:
                eng.wait_ge(s_extd, (XH - len(ACT_COPIES)) * b.n + h + 1 - by_act)

        with nc.Block() as block:

            @block.sync
            def _(sp):
                def load_ctx(b):
                    at_least(sp, s_v, KC * (b.n - 1))
                    sp.dma_start(ctxb[:, b.par, :, :],
                                 ctx_t[b.n, :, :].rearrange("(c p) s -> p c s", p=P)
                                 ).then_inc(s_ctx[b.par], 16)

                def load_queries(b):
                    at_least(sp, s_s, XH * (b.n - 1))
                    for ab in range(2):
                        for r in range(4):
                            row = 64 * ab + XD * r
                            src = q_parts[r // 2, :, bass.ds(b.n * SQ, SQ)].rearrange(
                                "(j a d) q -> a d j q", a=2, d=XD)
                            sp.dma_start(qst[row:row + XD, b.par, ab::2, :], src[ab]).then_inc(s_qst[b.par], 16)

                def load_rest(b):
                    at_least(sp, s_mb, b.n - 1)
                    pass_wait(sp, s_pass_sp)
                    sp.dma_start(mraw[:, b.par, :], mask[b.n, :, :]).then_inc(s_mask[b.par], 16)
                    at_least(sp, s_xb, b.n - 1)
                    sp.dma_start(xb[:, b.par, :], x[bass.ds(b.n * SQ, SQ), :]).then_inc(s_x[b.par], 16)

                def stack_keys(b):
                    for part, done, src in ((0, s_khi, khi), (1, s_klo, klo)):
                        sp.wait_ge(done, DC * (b.n + 1))
                        sp.dma_start(k_parts[b.par, part, :, :].rearrange("(c p) s -> p c s", p=P),
                                     src[:, b.par, :, :]).then_inc(s_kw[b.par], 16)
                    sp.wait_ge(s_kw[b.par], 32 * (b.half + 1))
                    at_least(sp, s_s, XH * (b.n - 1))
                    for ab in range(2):
                        for r in range(4):
                            row = 64 * ab + XD * r
                            src = k_parts[b.par, r % 2, :, :].rearrange("(j a d) s -> a d j s", a=2, d=XD)
                            sp.dma_start(kst[row:row + XD, b.par, :, :], src[ab]).then_inc(s_kst[b.par], 16)

                def store(b):
                    sp.wait_ge(s_x1, b.n + 1)
                    sp.dma_start(x1[bass.ds(b.n * SQ, SQ), :], x1b[:, b.par, :]).then_inc(s_st[b.par], 16)

                for dst, src in ((wk, wk_t), (wv, wv_t), (wo, wo_t)):
                    sp.dma_start(dst[:, :, :], src.rearrange("(c p) e -> p c e", p=P)).then_inc(s_w, 16)
                for dst, src in ((bkc, bk), (bvc, bv)):
                    sp.dma_start(dst[:, :], src).then_inc(s_w, 16)
                sp.dma_start(bor[:, :], bo.rearrange("(a n) -> a n", a=1)).then_inc(s_w, 16)
                load_ctx(fixed(0))
                load_ctx(fixed(1))
                load_rest(fixed(0))
                sp.wait_ge(s_zero, 1)
                load_queries(fixed(0))
                stack_keys(fixed(0))

                def body(b):
                    if not is_last(b):
                        n = b.next()
                        load_queries(n)
                        load_rest(n)
                        if not is_last(n):
                            load_ctx(n.next())
                        stack_keys(n)
                    if not is_first(b):
                        store(b.before())

                batches(sp, body)
                store(fixed(NB - 1))
                for par in range(2):
                    sp.wait_ge(s_st[par], 16 * NB // 2)

            @block.gpsimd
            def _(pool):
                pool.memset(qst[:, :, :, :], 0.0).then_inc(s_zero, 1)
                pool.memset(vz[:, :, :, :, :, :], 0.0).then_inc(s_zero, 1)
                pool.memset(ex[:, :, :], 0.0).then_inc(s_zero, 1)
                pool.wait_ge(s_tg, 1)

                def body(b):
                    pool.wait_ge(s_mask[b.par], 16 * (b.half + 1))
                    at_least(pool, s_sm, XH * (b.n - 1))
                    pass_wait(pool, s_pass_pool)
                    pool.tensor_scalar(mbias[:, b.par, :], mraw[:, b.par, :], BIG, -BIG,
                                       ALU.mult, ALU.add).then_inc(s_mb, 1)
                    pool.wait_ge(s_x[b.par], 16 * (b.half + 1))
                    at_least(pool, s_x1, b.n - 1)
                    pool.tensor_tensor(xbias[:, b.par, :], xb[:, b.par, :], tgbo[0:SQ, :],
                                       ALU.add).then_inc(s_xb, 1)

                batches(pool, body)

            @block.vector
            def _(dve):
                dve.memset(ones[:, :], 1.0).then_inc(s_one, 1)
                dve.wait_ge(s_w, 96)
                dve.wait_ge(s_one, 1)
                for c in range(DC):
                    dve.tensor_scalar(bvb[:, c, :], ones[:, :], bvc[:, c:c + 1], None,
                                      ALU.mult).then_inc(s_bvb, 1)
                dve.wait_ge(s_bo, 1)
                dve.tensor_scalar(tgbo[:, :], p_a[:, 0, 0:D], k.tanh_g[:, 0:1], None,
                                  ALU.mult).then_inc(s_tg, 1)

                def key_lo(b, c):
                    dve.wait_ge(s_khi, DC * b.n + c + 1)
                    at_least(dve, s_kw[b.par], 32 * b.half)
                    dve.scalar_tensor_tensor(out=klo[:, b.par, c, :], in0=p_p[:, c, 0:SK],
                                             scalar=bkc[:, c:c + 1], in1=khi[:, b.par, c, :],
                                             op0=ALU.add, op1=ALU.subtract).then_inc(s_klo, 1)

                def masked(b, h):
                    if h == 0:
                        dve.wait_ge(s_mb, b.n + 1)
                    dve.wait_ge(s_s, XH * b.n + h + 1)
                    at_least(dve, s_ex, XH * b.n + h - 3)
                    pass_wait(dve, s_pass_dve)
                    dve.tensor_tensor_reduce(
                        out=sm[:, h % 4, :], in0=p_s[0:SQ, h % 2, 0:SK], in1=mbias[:, b.par, :],
                        scale=-0.25, scalar=BIG, op0=ALU.add, op1=ALU.min,
                        accum_out=nmax[:, h % 4:h % 4 + 1]).then_inc(s_sm, 1)

                def copy_ext(b, h):
                    if h in ACT_COPIES:
                        return
                    dve.wait_ge(s_t, XH * b.n + h + 1)
                    at_least(dve, s_pv, XH * b.n + h - 3)
                    dve.tensor_copy(ext[:, h % 4, :], p_t[0:KW, h % 2, 0:KC * SQ]).then_inc(s_extd, 1)

                def rden_spread(b):
                    dve.wait_ge(s_ex, XH * (b.n + 1))
                    dve.reciprocal(rden[:, :], den[:, b.par, :]).then_inc(s_rd, 1)
                    dve.wait_ge(s_rd, b.n + 1)
                    at_least(dve, s_r, b.n)
                    dve.tensor_copy(rdx[:, :, :], rden[:, :].unsqueeze(2).broadcast_to([SQ, XH, XD])
                                    ).then_inc(s_rdx, 1)

                def normalize(b):
                    dve.wait_ge(s_pv, XH * (b.n + 1))
                    dve.wait_ge(s_rt, b.n + 1)
                    at_least(dve, s_o, b.n)
                    dve.tensor_tensor(an[:, :], p_a[:, b.par, 0:DC * SQ], rt[:, :], ALU.mult).then_inc(s_an, 1)

                def residual(b):
                    dve.wait_ge(s_o, b.n + 1)
                    dve.wait_ge(s_xb, b.n + 1)
                    at_least(dve, s_st[b.par], 16 * b.half)
                    dve.scalar_tensor_tensor(out=x1b[:, b.par, :], in0=p_a[0:SQ, b.par, 0:D],
                                             scalar=k.tanh_g[0:SQ, 0:1], in1=xbias[:, b.par, :],
                                             op0=ALU.mult, op1=ALU.add).then_inc(s_x1, 1)

                key_lo(fixed(0), 0)
                key_lo(fixed(0), 1)

                def body(b):
                    for i in range(XH):
                        lagging(b, i, LAG_C, copy_ext)
                        masked(b, i)
                        if i in (3, 5) and not is_last(b):
                            key_lo(b.next(), i // 2 - 1)
                        if i == 2 and not is_first(b):
                            rden_spread(b.before())
                        if i == 7 and not is_first(b):
                            normalize(b.before())
                        if i == 10 and not is_first(b):
                            residual(b.before())

                batches(dve, body)
                last = fixed(NB - 1)
                for i in range(XH, XH + LAG_C):
                    lagging(last, i, LAG_C, copy_ext)
                rden_spread(last)
                normalize(last)
                residual(last)

            @block.scalar
            def _(act):
                def key_hi(b, c):
                    act.wait_ge(s_k, DC * b.n + c + 1)
                    at_least(act, s_kw[b.par], 32 * b.half)
                    act.activation(khi[:, b.par, c, :], p_p[:, c, 0:SK], ACT.Identity,
                                   bias=bkc[:, c:c + 1]).then_inc(s_khi, 1)

                def values(b, c):
                    if c == 0:
                        at_least(act, s_pv, XH * (b.n - 1))
                    act.wait_ge(s_v, KC * b.n + c + 1)
                    rows = KW if c < KC - 1 else KL
                    act.activation(vz[0:rows, b.par, c, :, 0:3:2, :],
                                   p_p[0:rows, c % 2, 0:D].rearrange("p (j a d) -> p j a d", a=2, d=XD),
                                   ACT.Copy).then_inc(s_vz, 1)

                def exp(b, h):
                    if h == 0:
                        at_least(act, s_rd, b.n - 1)
                    act.wait_ge(s_sm, XH * b.n + h + 1)
                    at_least(act, s_t, XH * b.n + h - 3)
                    act.activation(ex[:, h % 4, 0:SK], sm[:, h % 4, :], ACT.Exp, scale=-1.0,
                                   bias=nmax[:, h % 4:h % 4 + 1],
                                   accum_out=den[:, b.par, h:h + 1]).then_inc(s_ex, 1)

                def copy_rt(b):
                    act.wait_ge(s_r, b.n + 1)
                    at_least(act, s_an, b.n)
                    act.activation(rt[:, :], p_a[:, b.par, RT:RT + DC * SQ], ACT.Copy).then_inc(s_rt, 1)

                act.wait_ge(s_zero, 3)
                key_hi(fixed(0), 0)
                key_hi(fixed(0), 1)
                for c in range(KC):
                    values(fixed(0), c)

                def copy_ext(b, h):
                    if h not in ACT_COPIES:
                        return
                    act.wait_ge(s_t, XH * b.n + h + 1)
                    at_least(act, s_pv, XH * b.n + h - 3)
                    act.activation(ext[:, h % 4, :], p_t[0:KW, h % 2, 0:KC * SQ], ACT.Copy
                                   ).then_inc(s_exta, 1)

                def body(b):
                    for i in range(XH):
                        lagging(b, i, LAG_C, copy_ext)
                        if i in (2, 4) and not is_last(b):
                            key_hi(b.next(), i // 2 - 1)
                        if i == 6 and not is_first(b):
                            copy_rt(b.before())
                        exp(b, i)
                        if i in (8, 12, 14) and not is_last(b):
                            values(b.next(), (8, 12, 14).index(i))

                batches(act, body)
                last = fixed(NB - 1)
                for i in range(XH, XH + LAG_C):
                    lagging(last, i, LAG_C, copy_ext)
                copy_rt(last)

            @block.tensor
            def _(pe):
                def keys(b, c, kc):
                    if kc == 0:
                        if c == 0:
                            pe.wait_ge(s_ctx[b.par], 16 * (b.half + 1))
                        at_least(pe, s_vz, KC * b.n - c)
                    last = pe.matmul(p_p[:, c, 0:SK], wk[:, kc, c * P:(c + 1) * P],
                                     ctxb[:, b.par, kc, :], start=kc == 0, stop=kc == DC - 1)
                    if kc == DC - 1:
                        last.then_inc(s_k, 1)

                def values(b, c, kc):
                    if kc == 0:
                        if c == KC - 1:
                            pe.wait_ge(s_vz, KC * b.n + 1)
                        else:
                            pe.wait_ge(s_klo, DC * b.n + c + 1)
                    rows = KW if c < KC - 1 else KL
                    last = pe.matmul(p_p[0:rows, c % 2, 0:D],
                                     ctxb[:, b.par, kc, c * KW:c * KW + rows], wv[:, kc, :],
                                     start=kc == 0, stop=kc == DC - 1)
                    if kc == DC - 1:
                        last.then_inc(s_v, 1)

                def scores(b, h):
                    if h == 0:
                        pe.wait_ge(s_kst[b.par], 128 * (b.half + 1))
                        pe.wait_ge(s_qst[b.par], 128 * (b.half + 1))
                    at_least(pe, s_sm, XH * b.n + h - 1)
                    pe.matmul(p_s[0:SQ, h % 2, 0:SK], qst[:, b.par, h, :], kst[:, b.par, h // 2, :],
                              start=True, stop=True).then_inc(s_s, 1)

                def turn(b, h):
                    pe.wait_ge(s_ex, XH * b.n + h + 1)
                    wait_copy(pe, b, h - 2)
                    for c in range(KC):
                        last = pe.transpose(p_t[0:KW, h % 2, c * SQ:(c + 1) * SQ],
                                            ex[:, h % 4, c * KW:(c + 1) * KW], k.ident[0:SQ, 0:SQ])
                    last.then_inc(s_t, 1)

                def attend(b, h):
                    if h == 0:
                        pe.wait_ge(s_vz, KC * (b.n + 1))
                        at_least(pe, s_x1, b.n - 1)
                    wait_copy(pe, b, h)
                    row, col, odd = 32 * (h % XG // 2), SQ * (h // XG), h % 2
                    for c in range(KC):
                        v = vz[:, b.par, c, h // 2, :, :].rearrange("p a d -> p (a d)")
                        last = pe.matmul(p_a[row:row + 32, b.par, col:col + SQ], v[:, XD * odd:XD * odd + 32],
                                         ext[:, h % 4, c * SQ:(c + 1) * SQ],
                                         start=odd == 0 and c == 0, stop=odd == 1 and c == KC - 1)
                    last.then_inc(s_pv, 1)

                def turn_rden(b):
                    pe.wait_ge(s_rdx, b.n + 1)
                    for c in range(DC):
                        src = rdx[:, c * XG:(c + 1) * XG, :].rearrange("p h d -> p (h d)")
                        last = pe.transpose(p_a[:, b.par, RT + c * SQ:RT + (c + 1) * SQ], src, k.ident[0:SQ, 0:SQ])
                    last.then_inc(s_r, 1)

                def project(b, c):
                    if c == 0:
                        pe.wait_ge(s_an, b.n + 1)
                    last = pe.matmul(p_a[0:SQ, b.par, 0:D], an[:, c * SQ:(c + 1) * SQ], wo[:, c, :],
                                     start=c == 0, stop=c == DC - 1)
                    if c == DC - 1:
                        last.then_inc(s_o, 1)

                pe.wait_ge(s_w, 96)
                pe.wait_ge(s_bvb, DC)
                for c in range(DC):
                    pe.matmul(p_a[:, 0, 0:D], bvb[:, c, :], wo[:, c, :], start=c == 0, stop=False)
                pe.matmul(p_a[:, 0, 0:D], ones[0:1, :], bor[:, :], start=False,
                          stop=True).then_inc(s_bo, 1)
                for n in range(DC * DC):
                    keys(fixed(0), n // DC, n % DC)
                pe.wait_ge(s_tg, 1)
                for n in range(KC * DC):
                    values(fixed(0), n // DC, n % DC)

                ahead = {0: (keys, 0, 0), 1: (keys, 0, 1), 2: (keys, 1, 0), 3: (keys, 1, 1),
                         6: (values, 0, 0), 7: (values, 0, 1), 10: (values, 1, 0), 11: (values, 1, 1),
                         12: (values, 2, 0), 13: (values, 2, 1)}
                behind = {5: (turn_rden,), 8: (project, 0), 9: (project, 1)}

                def body(b):
                    for i in range(XH):
                        scores(b, i)
                        if i in ahead and not is_last(b):
                            work, *args = ahead[i]
                            work(b.next(), *args)
                        if i in behind and not is_first(b):
                            work, *args = behind[i]
                            work(b.before(), *args)
                        lagging(b, i, LAG_T, turn)
                        lagging(b, i, LAG_A, attend)

                batches(pe, body)
                last = fixed(NB - 1)
                for i in range(XH, XH + LAG_A):
                    lagging(last, i, LAG_T, turn)
                    lagging(last, i, LAG_A, attend)
                turn_rden(last)
                for c in range(DC):
                    project(last, c)




def stage_experts_in(nc, k, x1, sel_t, q_t, k_t, v_t, rs, qk_out, v_out):
    with ExitStack() as ctx:
        m = Store(nc, ctx)
        big = m.sbuf("e_big", [P, NT * D])
        x1t = big[:, :].rearrange("p (t d) -> p t d", d=D)
        prob = big[:, 0:T].rearrange("p (g e) -> p g e", e=E)
        pick2 = big[:, T:2 * T].rearrange("p (g e) -> p g e", e=E)
        pick1 = k.gates[:, :].rearrange("p (g e) -> p g e", e=E)
        xn = m.sbuf("e_xn", [P, 2, D])
        xhi, xlo = (m.sbuf(f"e_x{n}", [P, DC, T], F16) for n in ("hi", "lo"))
        st, mv = m.sbuf("e_st", [P, NT, 6]), m.sbuf("e_mv", [P, NT, 2])
        std, rstd, half = (m.sbuf(n, [P, NT]) for n in ("e_std", "e_rstd", "e_half"))
        wst = m.sbuf("e_wst", [P, 2, DC, H * PD])
        sst = m.sbuf("e_sst", [P, DC, P])
        shi, slo = (m.sbuf(f"e_s{n}", [P, DC, P], F16) for n in ("hi", "lo"))
        qkhi, qklo = (m.sbuf(f"e_qk{n}", [P, DC, 2 * H * PD], F16) for n in ("hi", "lo"))
        vhi, vlo = (m.sbuf(f"e_v{n}", [P, DC, HE * PD], F16) for n in ("hi", "lo"))
        out = m.sbuf("e_out", [P, 2 * T])
        qko = out[:, :].rearrange("p (u t) -> p u t", u=2)
        vout = out[:, :].rearrange("p (t a d) -> p t a d", a=2, d=PD)
        order = m.sbuf("e_order", [P, E])
        rsb = m.sbuf("e_rs", [P, 1])
        m1, m2, top, tot = (m.sbuf(f"e_{n}", [P, NT * 2 * H]) for n in ("m1", "m2", "top", "tot"))
        acc = m.sbuf("e_acc", [P, 2, 2, PD])
        dsum = m.sbuf("e_dsum", [P, 2, PD])
        tmp = m.sbuf("e_tmp", [P, 2, 4, PD])
        tsum = m.sbuf("e_tsum", [P, 2, 2, PD])
        tsum1 = m.sbuf("e_tsum1", [P, 2, PD])
        p_t = m.psum("e_pt", [P, 2, 512])
        p_v = m.psum("e_pv", [P, 2, 2, 512])
        p_q = p_v[:, :, :, :].rearrange("p a b n -> p (a b) n")
        s_x, s_vst = m.sems("e_s_x", 5), m.sems("e_s_vst", 5)
        s_sel, s_rs, s_wq, s_wk = (m.sem(f"e_s_{n}") for n in ("sel", "rs", "wq", "wk"))
        s_vw, s_qo = m.sems("e_s_vw", 2), m.sems("e_s_qo", 2)
        s_ord, s_st, s_mv, s_step, s_std = (m.sem(f"e_s_{n}") for n in ("ord", "st", "mv", "step", "std"))
        s_whi, s_wlo, s_xn, s_t, s_xhi, s_xlo, s_l, s_p, s_g = (
            m.sem(f"e_s_{n}") for n in ("whi", "wlo", "xn", "tr", "xhi", "xlo", "l", "p", "g"))
        s_qk, s_qe, s_vhi, s_vlo, s_vp = (m.sem(f"e_s_{n}") for n in ("qk", "qe", "vhi", "vlo", "vp"))
        s_pass = m.sem("e_s_pass")
        s_even, s_odd, s_dv, s_av, s_ds, s_ts, s_ts1, s_vo = (
            m.sem(f"e_s_{n}") for n in ("even", "odd", "dv", "av", "ds", "ts", "ts1", "vo"))
        NG = NT * 2 * H
        QF = 4
        with nc.Block() as block:

            @block.sync
            def _(sp):
                for u in range(2):
                    sp.sem_inc(s_qo[u], 16)
                sp.dma_start(sst[:, :, :], sel_t.rearrange("(c p) e -> p c e", p=P)).then_inc(s_sel, 16)
                sp.dma_start(rsb[:, :], rs.partition_broadcast(P)).then_inc(s_rs, 16)
                for i in range(5):
                    sp.dma_start(x1t[:, 5 * i:5 * i + 5, :],
                                 x1[640 * i:640 * i + 640, :].rearrange("(t p) d -> p t d", p=P)
                                 ).then_inc(s_x[i], 16)
                sp.dma_start(wst[:, 0, :, :], q_t.rearrange("(c p) n -> p c n", p=P)).then_inc(s_wq, 16)
                sp.dma_start(wst[:, 1, :, :], k_t.rearrange("(c p) n -> p c n", p=P)).then_inc(s_wk, 16)
                with sp.Fori(0, H) as i:
                    for u in range(2):
                        sp.wait_ge(s_qe, QF + NC * (2 * i + u + 1))
                        sp.dma_start(qk_out[2 * i + u, :, :], qko[:, u, :]).then_inc(s_qo[u], 16)
                with sp.Fori(0, H // 2) as i:
                    for g in range(5):
                        sp.wait_ge(s_vo, 50 * i + 10 * (g + 1) + 2)
                        sp.dma_start(
                            v_out[640 * g:640 * g + 640, bass.ds(i * 2 * PD, 2 * PD)].rearrange(
                                "(t p) n -> p t n", p=P),
                            vout[:, 5 * g:5 * g + 5, :, :].rearrange("p t a d -> p t (a d)")
                        ).then_inc(s_vst[g], 16)
                for g in range(5):
                    sp.wait_ge(s_vst[g], 16 * (1 + H // 2))
                for u in range(2):
                    sp.wait_ge(s_qo[u], 16 * (H + 1))

            @block.gpsimd
            def _(pool):
                for g in range(5):
                    pool.sem_inc(s_vst[g], 16)
                pool.sem_inc(s_ts, 2)
                pool.sem_inc(s_vo, 2)
                for e in range(E):
                    pool.memset(order[:, e:e + 1], float(E - e)).then_inc(s_ord, 1)
                for h in range(H):
                    if h < 2:
                        pool.wait_ge(s_wlo, 2 + h)
                    else:
                        pool.wait_ge(s_vlo, h - 1)
                    pool.dma_start(wst[:, h % 2, :, :],
                                 v_t[:, h * E * PD:(h + 1) * E * PD].rearrange("(c p) n -> p c n", p=P)
                                 ).then_inc(s_vw[h % 2], 16)
                for u in range(2):
                    pool.wait_ge(s_qo[u], 16 * (H + 1))

                def unit(i, g, t, hh):
                    n = 50 * i + 2 * t + hh
                    pool.wait_ge(s_av, 4 * n + 12)
                    pool.tensor_tensor(tsum[:, hh, :, :], tmp[:, hh, 0:2, :], tmp[:, hh, 2:4, :],
                                       ALU.add).then_inc(s_ts, 1)
                    pool.wait_ge(s_ts, n + 3)
                    pool.wait_ge(s_vo, n + 1)
                    pool.tensor_tensor(tsum1[:, hh, :], tsum[:, hh, 0, :], tsum[:, hh, 1, :],
                                       ALU.add).then_inc(s_ts1, 1)
                    pool.wait_ge(s_ts1, n + 1)
                    pool.wait_ge(s_ds, n + 3)
                    pool.tensor_tensor(vout[:, t, hh, :], tsum1[:, hh, :], dsum[:, hh, :],
                                       ALU.add).then_inc(s_vo, 1)

                with pool.Fori(0, H // 2) as i:
                    for g in range(5):
                        pool.wait_ge(s_vst[g], 16 * i + 16)
                        pass_wait(pool, s_pass)
                        with pool.Fori(5 * g, 5 * g + 5) as t:
                            unit(i, g, t, 0)
                            unit(i, g, t, 1)

            @block.vector
            def _(dve):
                dve.sem_inc(s_ds, 2)
                dve.wait_ge(s_whi, 1)
                dve.scalar_tensor_tensor(out=slo[:, :, :], in0=sst[:, :, :], scalar=WS, in1=shi[:, :, :],
                                         op0=ALU.mult, op1=ALU.subtract).then_inc(s_wlo, 1)
                for t in range(NT):
                    if t % 5 == 0:
                        dve.wait_ge(s_x[t // 5], 16)
                    dve.bn_stats(st[:, t, :], x1t[:, t, :]).then_inc(s_st, 1)
                dve.wait_ge(s_st, NT)
                for t in range(NT):
                    dve.bn_aggr(mv[:, t, :], st[:, t, :]).then_inc(s_mv, 1)
                dve.wait_ge(s_mv, NT)
                rstd_steps(dve, mv, std, rstd, half, s_step, s_std, 0)

                def x_lo(t):
                    dve.wait_ge(s_xhi, t + 1)
                    dve.tensor_tensor(xlo[:, :, t * P:(t + 1) * P],
                                      p_t[:, t % 2, 0:DC * P].rearrange("p (c n) -> p c n", c=DC),
                                      xhi[:, :, t * P:(t + 1) * P], ALU.subtract).then_inc(s_xlo, 1)

                for t in range(NT):
                    at_least(dve, s_t, t - 1)
                    dve.tensor_scalar(xn[:, t % 2, :], x1t[:, t, :], mv[:, t, 0:1], rstd[:, t:t + 1],
                                      ALU.subtract, ALU.mult).then_inc(s_xn, 1)
                    if t >= 1:
                        x_lo(t - 1)
                x_lo(NT - 1)
                for w in range(2):
                    dve.wait_ge(s_whi, 2 + w)
                    dve.scalar_tensor_tensor(
                        out=qklo[:, :, w * H * PD:(w + 1) * H * PD], in0=wst[:, w, :, :], scalar=WS,
                        in1=qkhi[:, :, w * H * PD:(w + 1) * H * PD],
                        op0=ALU.mult, op1=ALU.subtract).then_inc(s_wlo, 1)

                def spread(v):
                    return v[:, :].unsqueeze(2).broadcast_to([P, NG, E])

                steps = [0]

                def step(ins):
                    ins.then_inc(s_g, 1)
                    steps[0] += 1
                    dve.wait_ge(s_g, steps[0])

                ranks = order[:, :].unsqueeze(1).broadcast_to([P, NG, E])
                dve.wait_ge(s_p, NT)
                dve.wait_ge(s_ord, E)
                step(dve.tensor_reduce(out=m1[:, :], in_=prob, axis=AX, op=ALU.max))
                step(dve.tensor_tensor(pick1, prob, spread(m1), ALU.is_equal))
                step(dve.tensor_tensor(pick1, pick1, ranks, ALU.mult))
                step(dve.tensor_reduce(out=top[:, :], in_=pick1, axis=AX, op=ALU.max))
                step(dve.tensor_tensor(pick1, pick1, spread(top), ALU.is_equal))
                step(dve.scalar_tensor_tensor(out=pick2, in0=pick1, scalar=-3.0, in1=prob,
                                              op0=ALU.mult, op1=ALU.add))
                step(dve.tensor_reduce(out=m2[:, :], in_=pick2, axis=AX, op=ALU.max))
                step(dve.tensor_tensor(pick2, pick2, spread(m2), ALU.is_equal))
                step(dve.tensor_tensor(pick2, pick2, ranks, ALU.mult))
                step(dve.tensor_reduce(out=top[:, :], in_=pick2, axis=AX, op=ALU.max))
                step(dve.tensor_tensor(pick2, pick2, spread(top), ALU.is_equal))
                step(dve.tensor_tensor(tot[:, :], m1[:, :], m2[:, :], ALU.add))
                step(dve.tensor_scalar(tot[:, :], tot[:, :], 1e-9, None, ALU.max))
                step(dve.reciprocal(tot[:, :], tot[:, :]))
                dve.wait_ge(s_rs, 16)
                step(dve.tensor_scalar(tot[:, :], tot[:, :], rsb[:, 0:1], None, ALU.mult))
                step(dve.tensor_scalar(tot[:, :], tot[:, :], 1.0 / WS, None, ALU.mult))
                step(dve.tensor_tensor(m1[:, :], m1[:, :], tot[:, :], ALU.mult))
                step(dve.tensor_tensor(m2[:, :], m2[:, :], tot[:, :], ALU.mult))
                step(dve.tensor_tensor(pick1, pick1, spread(m1), ALU.mult))
                step(dve.tensor_tensor(pick2, pick2, spread(m2), ALU.mult))
                step(dve.tensor_tensor(pick1, pick1, pick2, ALU.add))

                for h in range(H):
                    cut = slice(h * E * PD, (h + 1) * E * PD)
                    dve.wait_ge(s_vw[h % 2], 16 * (h // 2 + 1))
                    dve.tensor_scalar(vhi[:, :, cut], wst[:, h % 2, :, :], WS, None,
                                      ALU.mult).then_inc(s_vhi, 1)
                    dve.wait_ge(s_vhi, h + 1)
                    dve.scalar_tensor_tensor(out=vlo[:, :, cut], in0=wst[:, h % 2, :, :], scalar=WS,
                                             in1=vhi[:, :, cut], op0=ALU.mult,
                                             op1=ALU.subtract).then_inc(s_vlo, 1)

                def unit(i, t, hh):
                    n = 50 * i + 2 * t + hh
                    for e in range(4):
                        gate = k.gates[:, bass.ds(t * P + 2 * E * i + E * hh + e, 1)]
                        chain = s_even if e % 2 == 0 else s_odd
                        if e < 2:
                            if e == 0:
                                dve.wait_ge(s_vp, 2 * n + 1)
                                dve.wait_ge(s_ds, n + 1)
                            dve.tensor_scalar(acc[:, hh, e, :], p_v[:, hh, 0, e * PD:(e + 1) * PD], gate,
                                              None, ALU.mult).then_inc(chain, 1)
                        else:
                            dve.wait_ge(chain, 2 * n + 1)
                            last = dve.scalar_tensor_tensor(
                                out=acc[:, hh, e % 2, :], in0=p_v[:, hh, 0, e * PD:(e + 1) * PD],
                                scalar=gate, in1=acc[:, hh, e % 2, :], op0=ALU.mult, op1=ALU.add)
                            last.then_inc(chain, 1)
                    dve.wait_ge(s_even, 2 * n + 2)
                    dve.wait_ge(s_odd, 2 * n + 2)
                    dve.wait_ge(s_vo, n + 1)
                    dve.tensor_tensor(dsum[:, hh, :], acc[:, hh, 0, :], acc[:, hh, 1, :],
                                      ALU.add).then_inc(s_ds, 1)

                with dve.Fori(0, H // 2) as i:
                    with dve.Fori(0, NT) as t:
                        unit(i, t, 0)
                        unit(i, t, 1)

            @block.scalar
            def _(act):
                act.wait_ge(s_sel, 16)
                act.activation(shi[:, :, :], sst[:, :, :], ACT.Copy, scale=WS).then_inc(s_whi, 1)
                act.wait_ge(s_step, 1)
                act.activation(std[:, :], mv[:, :, 1], ACT.Sqrt).then_inc(s_std, 1)
                for w, landed in enumerate((s_wq, s_wk)):
                    act.wait_ge(landed, 16)
                    act.activation(qkhi[:, :, w * H * PD:(w + 1) * H * PD], wst[:, w, :, :], ACT.Copy,
                                   scale=WS).then_inc(s_whi, 1)
                for t in range(NT):
                    act.wait_ge(s_t, t + 1)
                    act.activation(xhi[:, :, t * P:(t + 1) * P],
                                   p_t[:, t % 2, 0:DC * P].rearrange("p (c n) -> p c n", c=DC),
                                   ACT.Copy).then_inc(s_xhi, 1)
                for t in range(NT):
                    act.wait_ge(s_l, t + 1)
                    act.activation(big[:, t * P:(t + 1) * P], p_t[:, t % 2, 0:P], ACT.Sigmoid,
                                   scale=1.0 / WS).then_inc(s_p, 1)
                act.sem_inc(s_qe, QF)
                with act.Fori(0, H) as i:
                    for u in range(2):
                        act.wait_ge(s_qo[u], 16 * i + 16)
                        for c in range(NC):
                            act.wait_ge(s_qk, NC * (2 * i + u) + c + 1)
                            act.activation(qko[:, u, c * NW:(c + 1) * NW], p_q[:, c % QF, 0:NW],
                                           ACT.Copy).then_inc(s_qe, 1)
                act.sem_inc(s_av, 8)

                def unit(i, t, hh):
                    n = 50 * i + 2 * t + hh
                    act.wait_ge(s_vp, 2 * n + 2)
                    act.wait_ge(s_ts, n + 1)
                    for e in range(4):
                        gate = k.gates[:, bass.ds(t * P + 2 * E * i + E * hh + 4 + e, 1)]
                        act.activation(tmp[:, hh, e, :], p_v[:, hh, 1, e * PD:(e + 1) * PD], ACT.Copy,
                                       scale=gate).then_inc(s_av, 1)

                with act.Fori(0, H // 2) as i:
                    with act.Fori(0, NT) as t:
                        unit(i, t, 0)
                        unit(i, t, 1)

            @block.tensor
            def _(pe):
                for t in range(NT):
                    pe.wait_ge(s_xn, t + 1)
                    at_least(pe, s_xlo, t - 1)
                    for c in range(DC):
                        last = pe.transpose(p_t[:, t % 2, c * P:(c + 1) * P],
                                            xn[:, t % 2, c * P:(c + 1) * P], k.ident[:, :])
                    last.then_inc(s_t, 1)
                pe.wait_ge(s_wlo, 1)
                pe.wait_ge(s_xlo, NT)
                for t in range(NT):
                    at_least(pe, s_p, t - 1)
                    tok = slice(t * P, (t + 1) * P)
                    for n, (c, a, b) in enumerate((c, a, b) for c in range(DC)
                                                  for a, b in ((xhi, shi), (xhi, slo), (xlo, shi))):
                        last = pe.matmul(p_t[:, t % 2, 0:P], a[:, c, tok], b[:, c, :],
                                         start=n == 0, stop=n == 3 * DC - 1)
                    last.then_inc(s_l, 1)
                pe.wait_ge(s_wlo, 3)
                with pe.Fori(0, 2 * H) as u:
                    for w in range(NC):
                        pe.wait_ge(s_qe, NC * u + w + 1)
                        tok = slice(w * NW, (w + 1) * NW)
                        for n, (c, a, b) in enumerate((c, a, b) for c in range(DC)
                                                      for a, b in ((qkhi, xhi), (qkhi, xlo), (qklo, xhi))):
                            last = pe.matmul(p_q[:, w % QF, 0:NW], a[:, c, bass.ds(u * PD, PD)],
                                             b[:, c, tok], start=n == 0, stop=n == 3 * DC - 1)
                        last.then_inc(s_qk, 1)
                pe.wait_ge(s_qe, QF + 2 * H * NC)
                pe.wait_ge(s_vlo, H)

                def unit(i, t, hh):
                    n = 50 * i + 2 * t + hh
                    for half in range(2):
                        if half == 0:
                            pe.wait_ge(s_ds, n + 1)
                        else:
                            pe.wait_ge(s_av, 4 * n + 4)
                        col = 2 * E * PD * i + E * PD * hh + half * 512
                        for j, (c, a, b) in enumerate((c, a, b) for c in range(DC)
                                                      for a, b in ((xhi, vhi), (xhi, vlo), (xlo, vhi))):
                            last = pe.matmul(p_v[:, hh, half, :], a[:, c, bass.ds(t * P, P)],
                                             b[:, c, bass.ds(col, 512)], start=j == 0, stop=j == 3 * DC - 1)
                        last.then_inc(s_vp, 1)

                with pe.Fori(0, H // 2) as i:
                    with pe.Fori(0, NT) as t:
                        unit(i, t, 0)
                        unit(i, t, 1)



def stage_attention_out(nc, k, x1, qk, v, o_w, y):
    SCALE = PD ** -0.5 / WS ** 2
    GB = 4
    GC = GB * SQ
    NGR = NB // GB
    TT = 3
    ACT_PAIRS = ((3,), (1, 3), (1, 3))
    DVE_PAIRS = tuple(tuple(q for q in range(4) if q not in a) for a in ACT_PAIRS)
    ACT_TURN, DVE_TURN = sum(map(len, ACT_PAIRS)), sum(map(len, DVE_PAIRS))
    ACT_HEAD = NGR * ACT_TURN + len(ACT_PAIRS[-1])
    DVE_HEAD = NGR * DVE_TURN + len(DVE_PAIRS[-1])
    PIECES = NGR // 2
    PIECE = E * D // PIECES

    class Tile:

        def __init__(self, h, j, place, last=False):
            self.t, self.last = j * TT + place, last
            self.place = TT - 1 if last else place
            self.act = h * ACT_HEAD + j * ACT_TURN + sum(map(len, ACT_PAIRS[:place]))
            self.dve = h * DVE_HEAD + j * DVE_TURN + sum(map(len, DVE_PAIRS[:place]))

    def slot(x, r):
        return sum(map(len, ACT_PAIRS[:x.place])) + r

    def place(b):
        return bass.ds(b.n % (2 * NGR) * GC, GC)

    def attention_alone(eng, group):
        group(fixed(0), ())
        group(fixed(1), ())
        with eng.Fori(1, NGR // 2) as jj:
            group(Batch(2 * jj, 0, jj), ())
            group(Batch(2 * jj + 1, 1, jj), ())

    def heads(eng, group, tile, begin, piece, rest):
        def head(h, buf, more):
            begin(h)
            if not more:
                rest()
            with eng.Fori(0, NGR // 2) as jj:
                for u in range(2):
                    tiles = [Tile(h, 2 * jj + u, p) for p in range(TT)]
                    if more:
                        group(Batch(NGR * (h + 1) + 2 * jj + u, u, NGR // 2 * (h + 1) + jj),
                              [(lambda x=x: tile(h, buf, x)) for x in tiles])
                    else:
                        for x in tiles:
                            tile(h, buf, x)
                    if more and u == 0:
                        piece(h + 1, 1 - buf, jj)
            tile(h, buf, Tile(h, NGR, 0, last=True))

        with eng.Fori(0, H // 2 - 1) as i:
            head(2 * i, 0, True)
            head(2 * i + 1, 1, True)
        head(H - 2, 0, True)
        head(H - 1, 1, False)

    with ExitStack() as ctx:
        m = Store(nc, ctx)
        qb, kb = (m.sbuf(f"a_{n}", [P, 2, GC]) for n in "qk")
        vb = m.sbuf("a_v", [SQ, 2, GB, PD])
        mx, mxs, sums, rsum = (m.sbuf(f"a_{n}", [SQ, GB]) for n in ("mx", "mxs", "sums", "rsum"))
        ex, ext = m.sbuf("a_ex", [SQ, GC]), m.sbuf("a_ext", [SQ, GC])
        chi, clo = (m.sbuf(f"a_c{n}", [P, 2 * T], F16) for n in ("hi", "lo"))
        main = m.sbuf("o_main", [P, NT, D])
        side = m.sbuf("o_side", [P, NT, D])
        wst = m.sbuf("o_wst", [P, E * D])
        whi, wlo = (m.sbuf(f"o_w{n}", [P, 2, E * D], F16) for n in ("hi", "lo"))
        tmp = m.sbuf("o_tmp", [P, ACT_TURN, 2, D])
        p_s, p_t, p_c = (m.psum(f"a_p{n}", [P, 512]) for n in "stc")
        p_y = m.psum("o_py", [P, 4, 2, D])
        s_q, s_k, s_v = (m.sems(f"a_s_{n}", 2) for n in ("q", "k", "v"))
        s_s, s_mx, s_mxs, s_ex, s_rs, s_n, s_t, s_ext, s_c, s_hi, s_lo = (
            m.sem(f"a_s_{n}") for n in ("s", "mx", "mxs", "ex", "rs", "n", "t", "ext", "c", "hi", "lo"))
        s_x, s_y, s_g, s_w, s_whi, s_wlo = (m.sem(f"o_s_{n}") for n in ("x", "y", "g", "w", "whi", "wlo"))
        s_p, s_av, s_main, s_side, s_pool, s_end = (
            m.sem(f"o_s_{n}") for n in ("p", "av", "main", "side", "pool", "end"))
        s_pass_pool, s_pass_pe, s_pass_sp = (m.sem(f"o_s_pass_{n}") for n in ("pool", "pe", "sp"))
        go = k.gates[:, :].rearrange("p (t a n) -> p t a n", a=2, n=HE)[:, :, 1, :]
        ACT_AHEAD, DVE_AHEAD = len(ACT_PAIRS[-1]), len(DVE_PAIRS[-1])
        POOL_AHEAD = 2 * ACT_HEAD
        with nc.Block() as block:

            @block.sync
            def _(sp):
                def load(b, h, j):
                    at_least(sp, s_s, b.n - 1)
                    pass_wait(sp, s_pass_sp)
                    tok = bass.ds(j * GC, GC)
                    sp.dma_start(qb[:, b.par, :], qk[h, :, tok]).then_inc(s_q[b.par], 16)
                    sp.dma_start(kb[:, b.par, :], qk[h + H, :, tok]).then_inc(s_k[b.par], 16)
                    at_least(sp, s_c, b.n - 1)
                    pass_wait(sp, s_pass_sp)
                    sp.dma_start(vb[:, b.par, :, :], v[tok, bass.ds(h * PD, PD)].rearrange(
                        "(i q) d -> q i d", i=GB)).then_inc(s_v[b.par], 16)

                sp.dma_start(wst[:, :], o_w[:, 0:E * D]).then_inc(s_w, 16)
                load(fixed(0), 0, 0)
                load(fixed(1), 0, 1)
                sp.dma_start(main[:, :, :], x1.rearrange("(t p) d -> p t d", p=P)).then_inc(s_x, 16)
                with sp.Fori(1, NGR // 2) as jj:
                    for u in range(2):
                        load(Batch(2 * jj + u, u, jj), 0, 2 * jj + u)
                with sp.Fori(1, H) as h:
                    sp.wait_ge(s_wlo, PIECES * h)
                    pass_wait(sp, s_pass_sp)
                    sp.dma_start(wst[:, :], o_w[:, bass.ds(h * E * D, E * D)]).then_inc(s_w, 16)
                    with sp.Fori(0, NGR // 2) as jj:
                        for u in range(2):
                            load(Batch(NGR * h + 2 * jj + u, u, NGR // 2 * h + jj), h, 2 * jj + u)
                for g in range(5):
                    sp.wait_ge(s_end, g + 1)
                    sp.dma_start(y[640 * g:640 * g + 640, :].rearrange("(t p) d -> p t d", p=P),
                                 main[:, 5 * g:5 * g + 5, :]).then_inc(s_y, 16)
                sp.wait_ge(s_y, 80)

            @block.gpsimd
            def _(pool):
                pool.memset(side[:, :, :], 0.0).then_inc(s_pool, POOL_AHEAD)

                def normalize(b):
                    pool.wait_ge(s_rs, b.n + 1)
                    rows = ex[:, :].rearrange("p (i s) -> p i s", i=GB)
                    pool.tensor_tensor(rows, rows, rsum[:, :].unsqueeze(2).broadcast_to([SQ, GB, SQ]),
                                       ALU.mult).then_inc(s_n, 1)

                def tile(h, buf, x):
                    pool.wait_ge(s_side, DVE_AHEAD + x.dve + len(DVE_PAIRS[x.place]))
                    for r in range(len(ACT_PAIRS[x.place])):
                        for j in range(2):
                            n = 2 * (x.act + r) + j
                            pool.wait_ge(s_av, 2 * ACT_AHEAD + n + 1)
                            pool.wait_ge(s_pool, POOL_AHEAD + n)
                            pass_wait(pool, s_pass_pool)
                            pool.tensor_tensor(side[:, x.t, :], side[:, x.t, :],
                                               tmp[:, slot(x, r), j, :], ALU.add).then_inc(s_pool, 1)

                def group(b, tiles):
                    for i, one in enumerate(tiles):
                        one()
                        if i == 0:
                            normalize(b)
                    if not tiles:
                        normalize(b)

                attention_alone(pool, group)
                heads(pool, group, tile, lambda h: None, lambda h, buf, jj: None, lambda: None)

            @block.vector
            def _(dve):
                dve.sem_inc(s_side, DVE_AHEAD)
                dve.tensor_scalar(go, go, k.tanh_g[:, 1:2], None, ALU.mult).then_inc(s_g, 1)

                def maxima(b):
                    dve.wait_ge(s_s, b.n + 1)
                    dve.tensor_reduce(out=mx[:, :], in_=p_s[0:SQ, 0:GC].rearrange(
                        "p (i s) -> p i s", i=GB), axis=AX, op=ALU.max).then_inc(s_mx, 1)
                    dve.wait_ge(s_mx, b.n + 1)
                    at_least(dve, s_ex, b.n)
                    dve.tensor_scalar(mxs[:, :], mx[:, :], -SCALE, None, ALU.mult).then_inc(s_mxs, 1)

                def invert(b):
                    dve.wait_ge(s_ex, b.n + 1)
                    at_least(dve, s_n, b.n)
                    dve.reciprocal(rsum[:, :], sums[:, :]).then_inc(s_rs, 1)

                def copy_ext(b):
                    dve.wait_ge(s_t, b.n + 1)
                    at_least(dve, s_c, b.n)
                    dve.tensor_copy(ext[:, :], p_t[0:SQ, 0:GC]).then_inc(s_ext, 1)

                def low(b, col):
                    dve.wait_ge(s_hi, b.n + 1)
                    dve.tensor_tensor(clo[:, col], p_c[:, 0:GC], chi[:, col],
                                      ALU.subtract).then_inc(s_lo, 1)

                def tile(h, buf, x):
                    dve.wait_ge(s_pool, 2 * (x.act + len(ACT_PAIRS[x.place])))
                    for r, q in enumerate(DVE_PAIRS[x.place]):
                        n = x.dve + r
                        dve.wait_ge(s_p, 4 * NT * h + 4 * x.t + q + 1)
                        for j, (into, chain, ahead) in enumerate(((main, s_main, 0), (side, s_side, DVE_AHEAD))):
                            if r > 0:
                                dve.wait_ge(chain, ahead + n)
                            gate = k.gates[:, bass.ds(x.t * P + HE + h * E + 2 * q + j, 1)]
                            dve.scalar_tensor_tensor(
                                out=into[:, x.t, :], in0=p_y[:, q, j, :], scalar=gate,
                                in1=into[:, x.t, :], op0=ALU.mult, op1=ALU.add).then_inc(chain, 1)

                def group(b, tiles):
                    if not is_first(b):
                        copy_ext(b.before())
                    maxima(b)
                    if tiles:
                        tiles[0]()
                    invert(b)
                    if not is_first(b):
                        low(b.before(), place(b.before()))
                    for one in tiles[1:]:
                        one()

                def piece(h, buf, jj):
                    dve.wait_ge(s_whi, PIECES * h + jj + 1)
                    cut = bass.ds(jj * PIECE, PIECE)
                    dve.scalar_tensor_tensor(out=wlo[:, buf, cut], in0=wst[:, cut], scalar=WS,
                                             in1=whi[:, buf, cut], op0=ALU.mult,
                                             op1=ALU.subtract).then_inc(s_wlo, 1)

                for jj in range(PIECES):
                    piece(0, 0, jj)
                attention_alone(dve, group)
                dve.wait_ge(s_x, 16)

                def rest():
                    b = fixed(NB * H // GB - 1)
                    copy_ext(b)
                    low(b, place(b))

                heads(dve, group, tile, lambda h: None, piece, rest)
                dve.wait_ge(s_pool, POOL_AHEAD + 2 * H * ACT_HEAD)
                dve.wait_ge(s_main, H * DVE_HEAD)
                for g in range(5):
                    cut = slice(5 * g, 5 * g + 5)
                    dve.tensor_tensor(main[:, cut, :], main[:, cut, :], side[:, cut, :],
                                      ALU.add).then_inc(s_end, 1)

            @block.scalar
            def _(act):
                act.sem_inc(s_av, 2 * ACT_AHEAD)

                def exps(b):
                    at_least(act, s_rs, b.n)
                    act.wait_ge(s_mxs, b.n + 1)
                    at_least(act, s_t, b.n)
                    for i in range(GB):
                        last = act.activation(ex[:, i * SQ:(i + 1) * SQ], p_s[0:SQ, i * SQ:(i + 1) * SQ],
                                              ACT.Exp, bias=mxs[:, i:i + 1], scale=SCALE,
                                              accum_out=sums[:, i:i + 1])
                    last.then_inc(s_ex, 1)

                def high(b, col):
                    act.wait_ge(s_c, b.n + 1)
                    act.activation(chi[:, col], p_c[:, 0:GC], ACT.Copy).then_inc(s_hi, 1)

                def tile(h, buf, x):
                    for r, q in enumerate(ACT_PAIRS[x.place]):
                        act.wait_ge(s_p, 4 * NT * h + 4 * x.t + q + 1)
                        if r == 0:
                            before = 0 if x.last else len(ACT_PAIRS[(x.place - 1) % TT])
                            act.wait_ge(s_pool, POOL_AHEAD + 2 * (x.act - before))
                        for j in range(2):
                            gate = k.gates[:, bass.ds(x.t * P + HE + h * E + 2 * q + j, 1)]
                            act.activation(tmp[:, slot(x, r), j, :], p_y[:, q, j, :], ACT.Copy,
                                           scale=gate).then_inc(s_av, 1)

                def group(b, tiles):
                    exps(b)
                    if tiles:
                        tiles[0]()
                    if not is_first(b):
                        high(b.before(), place(b.before()))
                    for one in tiles[1:]:
                        one()

                def piece(h, buf, jj):
                    act.wait_ge(s_w, 16 * (h + 1))
                    cut = bass.ds(jj * PIECE, PIECE)
                    act.activation(whi[:, buf, cut], wst[:, cut], ACT.Copy, scale=WS).then_inc(s_whi, 1)

                for jj in range(PIECES):
                    piece(0, 0, jj)
                attention_alone(act, group)
                act.wait_ge(s_g, 1)

                def rest():
                    b = fixed(NB * H // GB - 1)
                    high(b, place(b))

                heads(act, group, tile, lambda h: None, piece, rest)

            @block.tensor
            def _(pe):
                def scores(b):
                    pe.wait_ge(s_q[b.par], 16 * (b.half + 1))
                    pe.wait_ge(s_k[b.par], 16 * (b.half + 1))
                    at_least(pe, s_ex, b.n)
                    for i in range(GB):
                        cut = slice(i * SQ, (i + 1) * SQ)
                        last = pe.matmul(p_s[0:SQ, cut], qb[:, b.par, cut], kb[:, b.par, cut],
                                         start=True, stop=True)
                    last.then_inc(s_s, 1)

                def turn(b):
                    pe.wait_ge(s_n, b.n + 1)
                    at_least(pe, s_ext, b.n)
                    for i in range(GB):
                        cut = slice(i * SQ, (i + 1) * SQ)
                        last = pe.transpose(p_t[0:SQ, cut], ex[:, cut], k.ident[0:SQ, 0:SQ])
                    last.then_inc(s_t, 1)

                def attend(b):
                    pe.wait_ge(s_v[b.par], 16 * (b.half + 1))
                    pe.wait_ge(s_ext, b.n + 1)
                    at_least(pe, s_lo, b.n)
                    for i in range(GB):
                        cut = slice(i * SQ, (i + 1) * SQ)
                        last = pe.matmul(p_c[:, cut], vb[:, b.par, i, :], ext[:, cut], start=True, stop=True)
                    last.then_inc(s_c, 1)

                def tile(h, buf, x):
                    if not x.last and x.place == TT - 1:
                        pe.wait_ge(s_lo, NGR * h + NGR)
                    before = TT - 1 if x.place == 0 or x.last else x.place - 1
                    for q in range(4):
                        if q in ACT_PAIRS[before]:
                            left = len(ACT_PAIRS[before]) - 1 - ACT_PAIRS[before].index(q)
                            pe.wait_ge(s_av, 2 * (ACT_AHEAD + x.act - left))
                        else:
                            left = len(DVE_PAIRS[before]) - 1 - DVE_PAIRS[before].index(q)
                            pe.wait_ge(s_side, DVE_AHEAD + x.dve - left)
                        cut = slice(2 * D * q, 2 * D * (q + 1))
                        for j, (a, b) in enumerate(((chi, whi), (chi, wlo), (clo, whi))):
                            last = pe.matmul(p_y[:, q, :, :].rearrange("p j d -> p (j d)"),
                                             a[:, bass.ds(buf * T + x.t * P, P)], b[:, buf, cut],
                                             start=j == 0, stop=j == 2)
                        last.then_inc(s_p, 1)

                def group(b, tiles):
                    if not is_first(b):
                        turn(b.before())
                    scores(b)
                    if tiles:
                        tiles[0]()
                    if not is_first(b):
                        attend(b.before())
                    for one in tiles[1:]:
                        one()

                def begin(h):
                    pe.wait_ge(s_wlo, PIECES * (h + 1))
                    pe.wait_ge(s_lo, NGR * h + NGR - 1)
                    pass_wait(pe, s_pass_pe)

                def rest():
                    b = fixed(NB * H // GB - 1)
                    turn(b)
                    attend(b)

                attention_alone(pe, group)
                heads(pe, group, tile, begin, lambda h, buf, jj: None, rest)


class Constants:
    pass


def constants(nc, ctx):
    k = Constants()
    m = Store(nc, ctx)
    k.ident = m.sbuf("ident", [P, P])
    k.tanh_g = m.sbuf("tanh_g", [P, 2])
    k.gates = m.sbuf("gates", [P, NT * 2 * HE])
    return k


def flamingo(nc, x, ctx_t, mask, g_xattn, g_ffn, wq, bq, wk, bk, wv, bv, wo, bo, sel, qw, kw, vw, ow, rs, y):
    def scratch(name, shape, dt=F32):
        return nc.dram_tensor(name, shape, dt, kind="Internal").ap()

    q_parts = scratch("q_parts", [2, D, T], F16)
    k_parts = scratch("k_parts", [2, 2, D, SK], F16)
    x1 = scratch("x1", [T, D])
    qk = scratch("qk", [2 * H, PD, T])
    v = scratch("v", [T, H * PD])
    with ExitStack() as ctx:
        k = constants(nc, ctx)
        stage_queries(nc, k, x, g_xattn, g_ffn, wq, bq, q_parts)
        stage_cross(nc, k, x, ctx_t, mask, wk, bk, wv, bv, wo, bo, q_parts, k_parts, x1)
        stage_experts_in(nc, k, x1, sel, qw, kw, vw, rs, qk, v)
        stage_attention_out(nc, k, x1, qk, v, ow, y)


def kernel(**inputs):
    import concourse.bacc as bacc
    import numpy as np
    from concourse.bass_utils import run_bass_kernel_spmd

    def arr(name):
        return np.asarray(inputs[name])

    def turned(name):
        return np.ascontiguousarray(arr(name).T)

    def column(name):
        return np.ascontiguousarray(arr(name).reshape(DC, P).T)

    sel = np.concatenate([arr("L0_ffn_sel_v_w"), arr("L0_ffn_sel_o_w")], axis=0)
    arrays = {
        "x": np.ascontiguousarray(arr("x").reshape(T, D)),
        "ctx_t": np.ascontiguousarray(arr("ctx_1024").transpose(0, 2, 1)),
        "mask": np.ascontiguousarray(arr("mask_BxSxS2_bf1")).view(np.uint8),
        "g_xattn": arr("g_xattn"),
        "g_ffn": arr("g_ffn"),
        "wq": turned("L0_xattn_Wq"), "bq": column("L0_xattn_bq"),
        "wk": turned("L0_xattn_Wk"), "bk": column("L0_xattn_bk"),
        "wv": turned("L0_xattn_Wv"), "bv": column("L0_xattn_bv"),
        "wo": turned("L0_xattn_Wo"), "bo": arr("L0_xattn_bo"),
        "sel": np.ascontiguousarray(sel.T),
        "q_w": turned("L0_ffn_q_w"),
        "k_w": turned("L0_ffn_k_w"),
        "v_w": np.ascontiguousarray(arr("L0_ffn_v_w").transpose(1, 0, 2).reshape(D, HE * PD)),
        "o_w": np.ascontiguousarray(arr("L0_ffn_o_w").transpose(1, 0, 2).reshape(PD, HE * D)),
        "route_scale": arr("L0_ffn_route_scale"),
    }
    nc = bacc.Bacc("TRN2", target_bir_lowering=False, num_devices=1)
    ins = {f"in_{n}": a for n, a in arrays.items()}
    args = [nc.dram_tensor(n, a.shape, mybir.dt.from_np(a.dtype), kind="ExternalInput").ap()
            for n, a in ins.items()]
    y = nc.dram_tensor("y", (T, D), F32, kind="ExternalOutput").ap()
    flamingo(nc, *args, y)
    r = run_bass_kernel_spmd(nc, [ins], core_ids=[0])
    return r.results[0]["y"].reshape(NB, SQ, D)
```

```python
from contextlib import ExitStack

import concourse.bass as bass
from concourse import mybir

F32 = mybir.dt.float32
F16 = mybir.dt.float16
U8 = mybir.dt.uint8
ALU = mybir.AluOpType
ACT = mybir.ActivationFunctionType
AX = mybir.AxisListType.X

NB, SQ, SK, D = 32, 100, 361, 256
T = NB * SQ
P = 128
NT = T // P
DC = D // P
XH, XD = 16, 16
XG = P // XD
KC = 3
KW = -(-SK // KC)
SKP = KC * KW
KL = SK - (KC - 1) * KW
H, E, PD = 8, 8, 128
HE = H * E
WS = 64.0
EPS = 1e-5
BIG = 3.4028234663852886e38
NW = 400
NC = T // NW


def at_least(eng, sem, value):
    if not isinstance(value, int) or value > 0:
        eng.wait_ge(sem, value)


def pass_wait(eng, passed):
    eng.sem_inc(passed, 1)


class Batch:

    def __init__(self, n, par, half):
        self.n, self.par, self.half = n, par, half

    def next(self):
        return Batch(self.n + 1, 1 - self.par, self.half + self.par)

    def before(self):
        return Batch(self.n - 1, 1 - self.par, self.half - (1 - self.par))


def fixed(n):
    return Batch(n, n % 2, n // 2)


def batches(eng, body):
    body(fixed(0))
    body(fixed(1))
    with eng.Fori(1, NB // 2 - 1) as i:
        body(Batch(2 * i, 0, i))
        body(Batch(2 * i + 1, 1, i))
    body(fixed(NB - 2))
    body(fixed(NB - 1))


def is_first(b):
    return isinstance(b.n, int) and b.n == 0


def is_last(b):
    return isinstance(b.n, int) and b.n == NB - 1


class Store:

    def __init__(self, nc, ctx):
        self.nc, self.ctx = nc, ctx

    def sbuf(self, name, shape, dt=F32):
        return self.ctx.enter_context(self.nc.sbuf_tensor(name, shape, dt))

    def psum(self, name, shape):
        return self.ctx.enter_context(self.nc.psum_tensor(name, shape, F32))

    def sem(self, name):
        return self.ctx.enter_context(self.nc.semaphore(name))

    def sems(self, name, n):
        return [self.sem(f"{name}_{i}") for i in range(n)]


def rstd_steps(dve, mv, std, rstd, half, s_step, s_std, base):
    var = mv[:, :, 1]
    dve.tensor_scalar(var, var, EPS, None, ALU.add).then_inc(s_step, 1)
    dve.wait_ge(s_std, 1)
    dve.reciprocal(rstd[:, :], std[:, :]).then_inc(s_step, 1)
    dve.wait_ge(s_step, base + 2)
    dve.tensor_tensor(half[:, :], rstd[:, :], rstd[:, :], ALU.mult).then_inc(s_step, 1)
    dve.wait_ge(s_step, base + 3)
    dve.tensor_tensor(half[:, :], half[:, :], var, ALU.mult).then_inc(s_step, 1)
    dve.wait_ge(s_step, base + 4)
    dve.tensor_scalar(half[:, :], half[:, :], -0.5, 1.5, ALU.mult, ALU.add).then_inc(s_step, 1)
    dve.wait_ge(s_step, base + 5)
    dve.tensor_tensor(rstd[:, :], rstd[:, :], half[:, :], ALU.mult).then_inc(s_step, 1)
    dve.wait_ge(s_step, base + 6)


def stage_queries(nc, k, cross, x, g_xattn, g_ffn, wq_t, bq, ctx_t, weights, biases, q_parts):
    with ExitStack() as ctx:
        m = Store(nc, ctx)
        xt = m.sbuf("q_x", [P, NT, D])
        xn = m.sbuf("q_xn", [P, 2, D])
        xnt = m.sbuf("q_xnt", [P, DC, T])
        wq = m.sbuf("q_wq", [P, DC, D])
        bqc = m.sbuf("q_bq", [P, DC])
        st = m.sbuf("q_st", [P, NT, 6])
        mv = m.sbuf("q_mv", [P, NT, 2])
        std, rstd, half = (m.sbuf(n, [P, NT]) for n in ("q_std", "q_rstd", "q_half"))
        qhi = m.sbuf("q_hi", [P, DC, T], F16)
        qlo = m.sbuf("q_lo", [P, DC, T], F16)
        pt = m.psum("q_pt", [P, 2, 512])
        pq = m.psum("q_pq", [P, 4, 512])
        s_x = m.sems("q_s_x", 5)
        s_w = m.sem("q_s_w")
        s_id = m.sem("q_s_id")
        s_cw, s_cx = m.sem("q_s_cw"), m.sems("q_s_cx", 2)
        s_zero, s_chi, s_clo = (m.sem(f"q_s_{n}") for n in ("zero", "chi", "clo"))
        s_g, s_tanh = m.sem("q_s_g"), m.sem("q_s_tanh")
        s_st, s_mv, s_step, s_std = (m.sem(f"q_s_{n}") for n in ("st", "mv", "step", "std"))
        s_xn, s_t, s_xnt, s_q, s_hi, s_lo, s_out = (
            m.sem(f"q_s_{n}") for n in ("xn", "t", "xnt", "q", "hi", "lo", "out"))
        with nc.Block() as block:

            @block.sync
            def _(sp):
                for i in range(5):
                    sp.dma_start(xt[:, 5 * i:5 * i + 5, :],
                                 x[640 * i:640 * i + 640, :].rearrange("(t p) d -> p t d", p=P)
                                 ).then_inc(s_x[i], 16)
                sp.dma_start(wq[:, :, :], wq_t.rearrange("(c p) e -> p c e", p=P)).then_inc(s_w, 16)
                sp.dma_start(bqc[:, :], bq).then_inc(s_w, 16)
                for i, g in enumerate((g_xattn, g_ffn)):
                    sp.dma_start(k.tanh_g[:, i:i + 1], g.partition_broadcast(P)).then_inc(s_g, 16)
                for i, w in enumerate(weights):
                    sp.dma_start(cross.w[:, i, :, :], w.rearrange("(c p) e -> p c e", p=P)).then_inc(s_cw, 16)
                bk, bv, bo = biases
                sp.dma_start(cross.bkc[:, :], bk).then_inc(s_cw, 16)
                sp.dma_start(cross.bvc[:, :], bv).then_inc(s_cw, 16)
                sp.dma_start(cross.bor[:, :], bo.rearrange("(a n) -> a n", a=1)).then_inc(s_cw, 16)
                for b in range(2):
                    sp.dma_start(cross.ctxb[:, b, :, :], ctx_t[b, :, :].rearrange("(c p) s -> p c s", p=P)
                                 ).then_inc(s_cx[b], 16)
                for g in range(4):
                    cut = slice(g * T // 4, (g + 1) * T // 4)
                    sp.wait_ge(s_hi, DC * NC // 4 * (g + 1))
                    sp.dma_start(q_parts[0, :, cut].rearrange("(c p) t -> p c t", p=P),
                                 qhi[:, :, cut]).then_inc(s_out, 16)
                    sp.wait_ge(s_lo, DC * NC // 4 * (g + 1))
                    sp.dma_start(q_parts[1, :, cut].rearrange("(c p) t -> p c t", p=P),
                                 qlo[:, :, cut]).then_inc(s_out, 16)
                sp.wait_ge(s_out, 128)

            @block.gpsimd
            def _(pool):
                pool.memset(k.ident[:, :], 0.0).then_inc(s_id, 1)
                pool.wait_ge(s_id, 1)
                pool.affine_select(out=k.ident[:, :], in_=k.ident[:, :], compare_op=ALU.not_equal,
                                   fill=1.0, base=0, pattern=[[-1, P]],
                                   channel_multiplier=1).then_inc(s_id, 1)
                pool.memset(cross.qst[:, :, :, :], 0.0).then_inc(s_zero, 1)
                pool.memset(cross.vz[:, :, :, :, :, :], 0.0).then_inc(s_zero, 1)
                pool.memset(cross.ex[:, :, :], 0.0).then_inc(s_zero, 1)
                pool.wait_ge(s_cw, 96)
                pool.tensor_scalar(cross.bkc[:, :], cross.bkc[:, :], WS, None, ALU.mult).then_inc(s_zero, 1)
                for i in range(2):
                    pool.tensor_scalar(cross.whi[:, i, :, :], cross.w[:, i, :, :], WS, None,
                                       ALU.mult).then_inc(s_chi, 1)
                    pool.wait_ge(s_chi, 2 * i + 1)
                    pool.tensor_scalar(cross.w[:, i, :, :], cross.w[:, i, :, :], WS, None,
                                       ALU.mult).then_inc(s_chi, 1)
                    pool.wait_ge(s_chi, 2 * i + 2)
                    pool.tensor_tensor(cross.wlo[:, i, :, :], cross.w[:, i, :, :], cross.whi[:, i, :, :],
                                       ALU.subtract).then_inc(s_clo, 1)
                for b in range(2):
                    pool.wait_ge(s_cx[b], 16)
                    pool.tensor_copy(cross.ctxh[:, b, :, :], cross.ctxb[:, b, :, :]).then_inc(s_chi, 1)
                    pool.wait_ge(s_chi, 5 + b)
                    pool.tensor_tensor(cross.ctxl[:, b, :, :], cross.ctxb[:, b, :, :],
                                       cross.ctxh[:, b, :, :], ALU.subtract).then_inc(s_clo, 1)

            @block.vector
            def _(dve):
                for t in range(NT):
                    if t % 5 == 0:
                        dve.wait_ge(s_x[t // 5], 16)
                    dve.bn_stats(st[:, t, :], xt[:, t, :]).then_inc(s_st, 1)
                dve.wait_ge(s_st, NT)
                for t in range(NT):
                    dve.bn_aggr(mv[:, t, :], st[:, t, :]).then_inc(s_mv, 1)
                dve.wait_ge(s_mv, NT)
                rstd_steps(dve, mv, std, rstd, half, s_step, s_std, 0)

                def normalize(t, par):
                    at_least(dve, s_t, t - 1)
                    dve.tensor_scalar(xn[:, par, :], xt[:, t, :], mv[:, t, 0:1], rstd[:, t:t + 1],
                                      ALU.subtract, ALU.mult).then_inc(s_xn, 1)

                for t in range(NT):
                    normalize(t, t % 2)
                dve.wait_ge(s_w, 32)
                for n in range(DC * NC):
                    c, w = n % DC, n // DC
                    dve.wait_ge(s_hi, n + 1)
                    dve.scalar_tensor_tensor(
                        out=qlo[:, c, w * NW:(w + 1) * NW], in0=pq[:, n % 4, 0:NW],
                        scalar=bqc[:, c:c + 1], in1=qhi[:, c, w * NW:(w + 1) * NW],
                        op0=ALU.add, op1=ALU.subtract).then_inc(s_lo, 1)

            @block.scalar
            def _(act):
                act.wait_ge(s_g, 32)
                act.activation(k.tanh_g[:, :], k.tanh_g[:, :], ACT.Tanh).then_inc(s_tanh, 1)
                act.wait_ge(s_step, 1)
                act.activation(std[:, :], mv[:, :, 1], ACT.Sqrt).then_inc(s_std, 1)
                for t in range(NT):
                    act.wait_ge(s_t, t + 1)
                    act.activation(xnt[:, :, t * P:(t + 1) * P],
                                   pt[:, t % 2, 0:DC * P].rearrange("p (c n) -> p c n", c=DC),
                                   ACT.Copy).then_inc(s_xnt, 1)
                act.wait_ge(s_w, 32)
                for n in range(DC * NC):
                    c, w = n % DC, n // DC
                    act.wait_ge(s_q, n + 1)
                    act.activation(qhi[:, c, w * NW:(w + 1) * NW], pq[:, n % 4, 0:NW],
                                   ACT.Identity, bias=bqc[:, c:c + 1]).then_inc(s_hi, 1)

            @block.tensor
            def _(pe):
                pe.wait_ge(s_id, 2)
                for t in range(NT):
                    pe.wait_ge(s_xn, t + 1)
                    at_least(pe, s_xnt, t - 1)
                    for c in range(DC):
                        last = pe.transpose(pt[:, t % 2, c * P:(c + 1) * P],
                                            xn[:, t % 2, c * P:(c + 1) * P], k.ident[:, :])
                    last.then_inc(s_t, 1)
                pe.wait_ge(s_w, 32)
                pe.wait_ge(s_xnt, NT)
                for n in range(DC * NC):
                    c, w = n % DC, n // DC
                    at_least(pe, s_lo, n - 3)
                    for kc in range(DC):
                        last = pe.matmul(pq[:, n % 4, 0:NW], wq[:, kc, c * P:(c + 1) * P],
                                         xnt[:, kc, w * NW:(w + 1) * NW],
                                         start=kc == 0, stop=kc == DC - 1)
                    last.then_inc(s_q, 1)


def stage_cross(nc, k, cross, x, ctx_t, mask, q_parts, k_parts, big, mv, x1):
    LAG_T, LAG_C, LAG_A = 3, 4, 5
    RT = 256
    ACT_COPIES = (1, 4, 7, 10, 13, 15)

    def lagging(b, i, lag, work):
        if lag <= i < XH + lag:
            work(b, i - lag)
        elif i < lag and not is_first(b):
            work(b.before(), i - lag + XH)

    with ExitStack() as ctx:
        m = Store(nc, ctx)
        wo, bkc, bvc, bor = cross.w[:, 2, :, :], cross.bkc, cross.bvc, cross.bor
        whi, wlo, ctxb, ctxh, ctxl = cross.whi, cross.wlo, cross.ctxb, cross.ctxh, cross.ctxl
        qst, vz, ex = cross.qst, cross.vz, cross.ex
        ones = m.sbuf("c_ones", [P, P])
        bvb = m.sbuf("c_bvb", [P, DC, P])
        tgbo = m.sbuf("c_tgbo", [P, D])
        khi, klo = (m.sbuf(f"c_k{n}", [P, 2, DC, SK], F16) for n in ("hi", "lo"))
        kst = m.sbuf("c_kst", [P, 2, XH // 2, SK], F16)
        mraw = m.sbuf("c_mraw", [SQ, 2, SK], U8)
        mbias = m.sbuf("c_mbias", [SQ, 2, SK])
        xb = m.sbuf("c_xb", [SQ, 2, D])
        xbias = m.sbuf("c_xbias", [SQ, 2, D])
        x1b = big[0:SQ, :].rearrange("p (b d) -> p b d", d=D)
        st, smv = m.sbuf("c_st", [SQ, 6]), m.sbuf("c_smv", [SQ, 2])
        sm = m.sbuf("c_sm", [SQ, 4, SK])
        nmax = m.sbuf("c_nmax", [SQ, 4])
        ext = m.sbuf("c_ext", [KW, 4, KC * SQ])
        den = m.sbuf("c_den", [SQ, 2, XH])
        rden = m.sbuf("c_rden", [SQ, XH])
        rdx = m.sbuf("c_rdx", [SQ, XH, XD])
        rt = m.sbuf("c_rt", [P, DC * SQ])
        an = m.sbuf("c_an", [P, DC * SQ])
        p_s = m.psum("c_ps", [P, 2, 512])
        p_t = m.psum("c_pt", [P, 2, 512])
        p_a = m.psum("c_pa", [P, 2, 512])
        p_p = m.psum("c_pp", [P, 2, 512])
        s_one, s_bvb, s_bo, s_tg = (m.sem(f"c_s_{n}") for n in ("one", "bvb", "bo", "tg"))
        s_ctx, s_kwh, s_kwl, s_kst, s_qst, s_mask, s_x, s_st = (
            m.sems(f"c_s_{n}", 2) for n in ("ctx", "kwh", "kwl", "kst", "qst", "mask", "x", "st"))
        s_k, s_khi, s_klo, s_v, s_vz, s_mb, s_xb = (
            m.sem(f"c_s_{n}") for n in ("k", "khi", "klo", "v", "vz", "mb", "xb"))
        s_s, s_sm, s_ex, s_t, s_extd, s_exta, s_pv = (
            m.sem(f"c_s_{n}") for n in ("s", "sm", "ex", "tr", "extd", "exta", "pv"))
        s_pass_dve, s_pass_pool, s_pass_sp = (m.sem(f"c_s_pass_{n}") for n in ("dve", "pool", "sp"))
        s_bn, s_mv, s_kept = (m.sem(f"c_s_{n}") for n in ("bn", "mv", "kept"))
        s_ch, s_cl = m.sem("c_s_ch"), m.sem("c_s_cl")
        s_rd, s_rdx, s_r, s_rt, s_an, s_o, s_x1 = (
            m.sem(f"c_s_{n}") for n in ("rd", "rdx", "r", "rt", "an", "o", "x1"))

        def wait_copy(eng, b, h):
            if h < 0:
                if is_first(b):
                    return
                b, h = b.before(), h + XH
            by_act = sum(j in ACT_COPIES for j in range(h + 1))
            if h in ACT_COPIES:
                eng.wait_ge(s_exta, len(ACT_COPIES) * b.n + by_act)
            else:
                eng.wait_ge(s_extd, (XH - len(ACT_COPIES)) * b.n + h + 1 - by_act)

        with nc.Block() as block:

            @block.sync
            def _(sp):
                def load_ctx(b):
                    at_least(sp, s_cl, b.n - 1)
                    sp.dma_start(ctxb[:, b.par, :, :],
                                 ctx_t[b.n, :, :].rearrange("(c p) s -> p c s", p=P)
                                 ).then_inc(s_ctx[b.par], 16)

                def load_queries(b):
                    at_least(sp, s_s, XH * (b.n - 1))
                    for ab in range(2):
                        for r in range(4):
                            row = 64 * ab + XD * r
                            src = q_parts[r // 2, :, bass.ds(b.n * SQ, SQ)].rearrange(
                                "(j a d) q -> a d j q", a=2, d=XD)
                            sp.dma_start(qst[row:row + XD, b.par, ab::2, :], src[ab]).then_inc(s_qst[b.par], 16)

                def load_rest(b):
                    at_least(sp, s_mb, b.n - 1)
                    pass_wait(sp, s_pass_sp)
                    sp.dma_start(mraw[:, b.par, :], mask[b.n, :, :]).then_inc(s_mask[b.par], 16)
                    at_least(sp, s_xb, b.n - 1)
                    sp.dma_start(xb[:, b.par, :], x[bass.ds(b.n * SQ, SQ), :]).then_inc(s_x[b.par], 16)

                def stack_keys(b):
                    for part, done, src, landed in ((0, s_khi, khi, s_kwh), (1, s_klo, klo, s_kwl)):
                        sp.wait_ge(done, DC * (b.n + 1))
                        sp.dma_start(k_parts[b.par, part, :, :].rearrange("(c p) s -> p c s", p=P),
                                     src[:, b.par, :, :]).then_inc(landed[b.par], 16)
                    at_least(sp, s_s, XH * (b.n - 1))
                    for part, landed in enumerate((s_kwh, s_kwl)):
                        sp.wait_ge(landed[b.par], 16 * (b.half + 1))
                        src = k_parts[b.par, part, :, :].rearrange("(j a d) s -> a d j s", a=2, d=XD)
                        for ab in range(2):
                            for r in (part, part + 2):
                                row = 64 * ab + XD * r
                                sp.dma_start(kst[row:row + XD, b.par, :, :], src[ab]
                                             ).then_inc(s_kst[b.par], 16)

                def store(b):
                    sp.wait_ge(s_x1, b.n + 1)
                    sp.dma_start(x1[bass.ds(b.n * SQ, SQ), :], x1b[:, b.n, :]).then_inc(s_st[b.par], 16)

                for par in range(2):
                    sp.sem_inc(s_ctx[par], 16)
                load_rest(fixed(0))
                load_queries(fixed(0))
                stack_keys(fixed(0))

                def body(b):
                    if not is_last(b):
                        n = b.next()
                        load_queries(n)
                        load_rest(n)
                        if not is_last(n):
                            load_ctx(n.next())
                        stack_keys(n)
                    if not is_first(b):
                        store(b.before())

                batches(sp, body)
                store(fixed(NB - 1))
                for par in range(2):
                    sp.wait_ge(s_st[par], 16 * NB // 2)

            @block.gpsimd
            def _(pool):
                def split(b):
                    pool.wait_ge(s_ctx[b.par], 16 * (b.half + 1))
                    at_least(pool, s_v, KC * (b.n - 1))
                    pass_wait(pool, s_pass_pool)
                    pool.tensor_copy(ctxh[:, b.par, :, :], ctxb[:, b.par, :, :]).then_inc(s_ch, 1)
                    pool.wait_ge(s_ch, b.n + 1)
                    pool.tensor_tensor(ctxl[:, b.par, :, :], ctxb[:, b.par, :, :], ctxh[:, b.par, :, :],
                                       ALU.subtract).then_inc(s_cl, 1)

                pool.sem_inc(s_ch, 2)
                pool.sem_inc(s_cl, 2)
                pool.wait_ge(s_tg, 1)

                def body(b):
                    pool.wait_ge(s_mask[b.par], 16 * (b.half + 1))
                    at_least(pool, s_sm, XH * (b.n - 1))
                    pass_wait(pool, s_pass_pool)
                    pool.tensor_scalar(mbias[:, b.par, :], mraw[:, b.par, :], BIG, -BIG,
                                       ALU.mult, ALU.add).then_inc(s_mb, 1)
                    pool.wait_ge(s_x[b.par], 16 * (b.half + 1))
                    at_least(pool, s_x1, b.n - 1)
                    pool.tensor_tensor(xbias[:, b.par, :], xb[:, b.par, :], tgbo[0:SQ, :],
                                       ALU.add).then_inc(s_xb, 1)
                    if not is_last(b) and not is_last(b.next()):
                        split(b.next().next())

                batches(pool, body)

            @block.vector
            def _(dve):
                dve.memset(ones[:, :], 1.0).then_inc(s_one, 1)
                dve.wait_ge(s_one, 1)
                for c in range(DC):
                    dve.tensor_scalar(bvb[:, c, :], ones[:, :], bvc[:, c:c + 1], None,
                                      ALU.mult).then_inc(s_bvb, 1)

                def key_lo(b, c):
                    dve.wait_ge(s_khi, DC * b.n + c + 1)
                    at_least(dve, s_kwl[b.par], 16 * b.half)
                    dve.scalar_tensor_tensor(out=klo[:, b.par, c, :], in0=p_p[:, c, 0:SK],
                                             scalar=bkc[:, c:c + 1], in1=khi[:, b.par, c, :],
                                             op0=ALU.add, op1=ALU.subtract).then_inc(s_klo, 1)

                def masked(b, h):
                    if h == 0:
                        dve.wait_ge(s_mb, b.n + 1)
                    dve.wait_ge(s_s, XH * b.n + h + 1)
                    at_least(dve, s_ex, XH * b.n + h - 3)
                    pass_wait(dve, s_pass_dve)
                    dve.tensor_tensor_reduce(
                        out=sm[:, h % 4, :], in0=p_s[0:SQ, h % 2, 0:SK], in1=mbias[:, b.par, :],
                        scale=-0.25 / WS, scalar=BIG, op0=ALU.add, op1=ALU.min,
                        accum_out=nmax[:, h % 4:h % 4 + 1]).then_inc(s_sm, 1)

                def copy_ext(b, h):
                    if h in ACT_COPIES:
                        return
                    dve.wait_ge(s_t, XH * b.n + h + 1)
                    at_least(dve, s_pv, XH * b.n + h - 3)
                    dve.tensor_copy(ext[:, h % 4, :], p_t[0:KW, h % 2, 0:KC * SQ]).then_inc(s_extd, 1)

                def rden_spread(b):
                    dve.wait_ge(s_ex, XH * (b.n + 1))
                    dve.reciprocal(rden[:, :], den[:, b.par, :]).then_inc(s_rd, 1)
                    dve.wait_ge(s_rd, b.n + 1)
                    at_least(dve, s_r, b.n)
                    dve.tensor_copy(rdx[:, :, :], rden[:, :].unsqueeze(2).broadcast_to([SQ, XH, XD])
                                    ).then_inc(s_rdx, 1)

                def normalize(b):
                    dve.wait_ge(s_pv, XH * (b.n + 1))
                    dve.wait_ge(s_rt, b.n + 1)
                    at_least(dve, s_o, b.n)
                    dve.tensor_tensor(an[:, :], p_a[:, b.par, 0:DC * SQ], rt[:, :], ALU.mult).then_inc(s_an, 1)

                def residual(b):
                    dve.wait_ge(s_o, b.n + 1)
                    dve.wait_ge(s_xb, b.n + 1)
                    dve.scalar_tensor_tensor(out=x1b[:, b.n, :], in0=p_a[0:SQ, b.par, 0:D],
                                             scalar=k.tanh_g[0:SQ, 0:1], in1=xbias[:, b.par, :],
                                             op0=ALU.mult, op1=ALU.add).then_inc(s_x1, 1)

                def moments(b):
                    dve.wait_ge(s_x1, b.n + 1)
                    at_least(dve, s_mv, b.n)
                    pass_wait(dve, s_pass_dve)
                    dve.bn_stats(st[:, :], x1b[:, b.n, :]).then_inc(s_bn, 1)

                def mean_var(b):
                    dve.wait_ge(s_bn, b.n + 1)
                    at_least(dve, s_kept, b.n)
                    pass_wait(dve, s_pass_dve)
                    dve.bn_aggr(smv[:, :], st[:, :]).then_inc(s_mv, 1)

                def keep(b):
                    dve.wait_ge(s_mv, b.n + 1)
                    dve.tensor_copy(mv[0:SQ, b.n, :], smv[:, :]).then_inc(s_kept, 1)

                key_lo(fixed(0), 0)
                key_lo(fixed(0), 1)
                dve.wait_ge(s_bo, 1)
                dve.tensor_scalar(tgbo[:, :], p_a[:, 0, 0:D], k.tanh_g[:, 0:1], None,
                                  ALU.mult).then_inc(s_tg, 1)

                def body(b):
                    for i in range(XH):
                        lagging(b, i, LAG_C, copy_ext)
                        masked(b, i)
                        if i in (3, 5) and not is_last(b):
                            key_lo(b.next(), i // 2 - 1)
                        if i == 2 and not is_first(b):
                            rden_spread(b.before())
                        if i == 7 and not is_first(b):
                            normalize(b.before())
                        if i == 12 and not is_first(b):
                            residual(b.before())
                        if i == 13 and not is_first(b):
                            moments(b.before())
                        if i == 14 and not is_first(b):
                            mean_var(b.before())
                        if i == 15 and not is_first(b):
                            keep(b.before())

                batches(dve, body)
                last = fixed(NB - 1)
                for i in range(XH, XH + LAG_C):
                    lagging(last, i, LAG_C, copy_ext)
                rden_spread(last)
                normalize(last)
                residual(last)
                moments(last)
                mean_var(last)
                keep(last)

            @block.scalar
            def _(act):
                def key_hi(b, c):
                    act.wait_ge(s_k, DC * b.n + c + 1)
                    at_least(act, s_kwh[b.par], 16 * b.half)
                    act.activation(khi[:, b.par, c, :], p_p[:, c, 0:SK], ACT.Identity,
                                   bias=bkc[:, c:c + 1]).then_inc(s_khi, 1)

                def values(b, c):
                    if c == 0:
                        at_least(act, s_pv, XH * (b.n - 1))
                    act.wait_ge(s_v, KC * b.n + c + 1)
                    rows = KW if c < KC - 1 else KL
                    act.activation(vz[0:rows, b.par, c, :, 0:3:2, :],
                                   p_p[0:rows, c % 2, 0:D].rearrange("p (j a d) -> p j a d", a=2, d=XD),
                                   ACT.Copy, scale=1.0 / WS).then_inc(s_vz, 1)

                def exp(b, h):
                    if h == 0:
                        at_least(act, s_rd, b.n - 1)
                    act.wait_ge(s_sm, XH * b.n + h + 1)
                    at_least(act, s_t, XH * b.n + h - 3)
                    act.activation(ex[:, h % 4, 0:SK], sm[:, h % 4, :], ACT.Exp, scale=-1.0,
                                   bias=nmax[:, h % 4:h % 4 + 1],
                                   accum_out=den[:, b.par, h:h + 1]).then_inc(s_ex, 1)

                def copy_rt(b):
                    act.wait_ge(s_r, b.n + 1)
                    at_least(act, s_an, b.n)
                    act.activation(rt[:, :], p_a[:, b.par, RT:RT + DC * SQ], ACT.Copy).then_inc(s_rt, 1)

                key_hi(fixed(0), 0)
                key_hi(fixed(0), 1)
                for c in range(KC):
                    values(fixed(0), c)

                def copy_ext(b, h):
                    if h not in ACT_COPIES:
                        return
                    act.wait_ge(s_t, XH * b.n + h + 1)
                    at_least(act, s_pv, XH * b.n + h - 3)
                    act.activation(ext[:, h % 4, :], p_t[0:KW, h % 2, 0:KC * SQ], ACT.Copy
                                   ).then_inc(s_exta, 1)

                def body(b):
                    for i in range(XH):
                        lagging(b, i, LAG_C, copy_ext)
                        if i in (2, 4) and not is_last(b):
                            key_hi(b.next(), i // 2 - 1)
                        if i == 6 and not is_first(b):
                            copy_rt(b.before())
                        exp(b, i)
                        if i in (8, 10, 14) and not is_last(b):
                            values(b.next(), (8, 10, 14).index(i))

                batches(act, body)
                last = fixed(NB - 1)
                for i in range(XH, XH + LAG_C):
                    lagging(last, i, LAG_C, copy_ext)
                copy_rt(last)

            @block.tensor
            def _(pe):
                def keys(b, c, kc):
                    if kc == 0:
                        if c == 0:
                            pe.wait_ge(s_cl, b.n + 1)
                        at_least(pe, s_vz, KC * b.n - c)
                    for i, (w, x) in enumerate(((whi, ctxh), (whi, ctxl), (wlo, ctxh))):
                        last = pe.matmul(p_p[:, c, 0:SK], w[:, 0, kc, c * P:(c + 1) * P],
                                         x[:, b.par, kc, :], start=kc == 0 and i == 0,
                                         stop=kc == DC - 1 and i == 2)
                    if kc == DC - 1:
                        last.then_inc(s_k, 1)

                def values(b, c, kc):
                    if kc == 0:
                        if c == KC - 1:
                            pe.wait_ge(s_vz, KC * b.n + 1)
                        else:
                            pe.wait_ge(s_klo, DC * b.n + c + 1)
                    rows = KW if c < KC - 1 else KL
                    for i, (x, w) in enumerate(((ctxh, whi), (ctxh, wlo), (ctxl, whi))):
                        last = pe.matmul(p_p[0:rows, c % 2, 0:D], x[:, b.par, kc, c * KW:c * KW + rows],
                                         w[:, 1, kc, :], start=kc == 0 and i == 0,
                                         stop=kc == DC - 1 and i == 2)
                    if kc == DC - 1:
                        last.then_inc(s_v, 1)

                def scores(b, h):
                    if h == 0:
                        pe.wait_ge(s_kst[b.par], 128 * (b.half + 1))
                        pe.wait_ge(s_qst[b.par], 128 * (b.half + 1))
                    at_least(pe, s_sm, XH * b.n + h - 1)
                    pe.matmul(p_s[0:SQ, h % 2, 0:SK], qst[:, b.par, h, :], kst[:, b.par, h // 2, :],
                              start=True, stop=True).then_inc(s_s, 1)

                def turn(b, h):
                    pe.wait_ge(s_ex, XH * b.n + h + 1)
                    wait_copy(pe, b, h - 2)
                    for c in range(KC):
                        last = pe.transpose(p_t[0:KW, h % 2, c * SQ:(c + 1) * SQ],
                                            ex[:, h % 4, c * KW:(c + 1) * KW], k.ident[0:SQ, 0:SQ])
                    last.then_inc(s_t, 1)

                def attend(b, h):
                    if h == 0:
                        pe.wait_ge(s_vz, KC * (b.n + 1))
                        at_least(pe, s_x1, b.n - 1)
                    wait_copy(pe, b, h)
                    row, col, odd = 32 * (h % XG // 2), SQ * (h // XG), h % 2
                    for c in range(KC):
                        v = vz[:, b.par, c, h // 2, :, :].rearrange("p a d -> p (a d)")
                        last = pe.matmul(p_a[row:row + 32, b.par, col:col + SQ], v[:, XD * odd:XD * odd + 32],
                                         ext[:, h % 4, c * SQ:(c + 1) * SQ],
                                         start=odd == 0 and c == 0, stop=odd == 1 and c == KC - 1)
                    last.then_inc(s_pv, 1)

                def turn_rden(b):
                    pe.wait_ge(s_rdx, b.n + 1)
                    for c in range(DC):
                        src = rdx[:, c * XG:(c + 1) * XG, :].rearrange("p h d -> p (h d)")
                        last = pe.transpose(p_a[:, b.par, RT + c * SQ:RT + (c + 1) * SQ], src,
                                            k.ident[0:SQ, 0:SQ])
                    last.then_inc(s_r, 1)

                def project(b, c):
                    if c == 0:
                        pe.wait_ge(s_an, b.n + 1)
                    last = pe.matmul(p_a[0:SQ, b.par, 0:D], an[:, c * SQ:(c + 1) * SQ], wo[:, c, :],
                                     start=c == 0, stop=c == DC - 1)
                    if c == DC - 1:
                        last.then_inc(s_o, 1)

                for n in range(DC * DC):
                    keys(fixed(0), n // DC, n % DC)
                for n in range(KC * DC):
                    values(fixed(0), n // DC, n % DC)
                pe.wait_ge(s_bvb, DC)
                for c in range(DC):
                    pe.matmul(p_a[:, 0, 0:D], bvb[:, c, :], wo[:, c, :], start=c == 0, stop=False)
                pe.matmul(p_a[:, 0, 0:D], ones[0:1, :], bor[:, :], start=False,
                          stop=True).then_inc(s_bo, 1)
                pe.wait_ge(s_tg, 1)

                ahead = {0: (keys, 0, 0), 1: (keys, 0, 1), 2: (keys, 1, 0), 3: (keys, 1, 1),
                         6: (values, 0, 0), 7: (values, 0, 1), 8: (values, 1, 0), 9: (values, 1, 1),
                         12: (values, 2, 0), 13: (values, 2, 1)}
                behind = {5: (turn_rden,), 10: (project, 0), 11: (project, 1)}

                def body(b):
                    for i in range(XH):
                        scores(b, i)
                        if i in ahead and not is_last(b):
                            work, *args = ahead[i]
                            work(b.next(), *args)
                        if i in behind and not is_first(b):
                            work, *args = behind[i]
                            work(b.before(), *args)
                        lagging(b, i, LAG_T, turn)
                        lagging(b, i, LAG_A, attend)

                batches(pe, body)
                last = fixed(NB - 1)
                for i in range(XH, XH + LAG_A):
                    lagging(last, i, LAG_T, turn)
                    lagging(last, i, LAG_A, attend)
                turn_rden(last)
                for c in range(DC):
                    project(last, c)




def stage_experts_in(nc, k, big, mv, sel_t, q_t, k_t, v_t, rs, qk_out, v_out):
    with ExitStack() as ctx:
        m = Store(nc, ctx)
        x1t = big[0:SQ, :].rearrange("p (b d) -> p b d", d=D)
        prob = big[:, 0:T].rearrange("p (g e) -> p g e", e=E)
        pick2 = big[:, T:2 * T].rearrange("p (g e) -> p g e", e=E)
        pick1 = k.gates[:, :].rearrange("p (g e) -> p g e", e=E)
        xhi, xlo = (m.sbuf(f"e_x{n}", [P, DC, T], F16) for n in ("hi", "lo"))
        std, rstd, half = (m.sbuf(n, [SQ, NB]) for n in ("e_std", "e_rstd", "e_half"))
        wst = m.sbuf("e_wst", [P, 2, DC, H * PD])
        sst = m.sbuf("e_sst", [P, DC, P])
        shi, slo = (m.sbuf(f"e_s{n}", [P, DC, P], F16) for n in ("hi", "lo"))
        qkhi, qklo = (m.sbuf(f"e_qk{n}", [P, DC, 2 * H * PD], F16) for n in ("hi", "lo"))
        vhi, vlo = (m.sbuf(f"e_v{n}", [P, DC, HE * PD], F16) for n in ("hi", "lo"))
        out = m.sbuf("e_out", [P, 2 * T])
        qko = out[:, :].rearrange("p (u t) -> p u t", u=2)
        vout = out[:, :].rearrange("p (t a d) -> p t a d", a=2, d=PD)
        xn = out[0:SQ, 0:4 * D].rearrange("p (b d) -> p b d", d=D)
        order = m.sbuf("e_order", [P, E])
        rsb = m.sbuf("e_rs", [P, 1])
        m1, m2, top, tot = (m.sbuf(f"e_{n}", [P, NT * 2 * H]) for n in ("m1", "m2", "top", "tot"))
        acc = m.sbuf("e_acc", [P, 2, 2, PD])
        dsum = m.sbuf("e_dsum", [P, 2, PD])
        rest = big[:, 2 * T:2 * T + 12 * PD].rearrange("p (a e d) -> p a e d", a=2, d=PD)
        tmp, tsum = rest[:, :, 0:4, :], rest[:, :, 4:6, :]
        tsum1 = m.sbuf("e_tsum1", [P, 2, PD])
        p_t = m.psum("e_pt", [P, 4, 512])
        p_v = m.psum("e_pv", [P, 2, 2, 512])
        p_q = p_v[:, :, :, :].rearrange("p a b n -> p (a b) n")
        s_vst = m.sems("e_s_vst", 5)
        s_sel, s_rs, s_wq, s_wk = (m.sem(f"e_s_{n}") for n in ("sel", "rs", "wq", "wk"))
        s_vw, s_qo = m.sems("e_s_vw", 2), m.sems("e_s_qo", 2)
        s_ord, s_step, s_std, s_xnp = (m.sem(f"e_s_{n}") for n in ("ord", "step", "std", "xnp"))
        s_whi, s_wlo, s_xn, s_t, s_xhi, s_xlo, s_l, s_p, s_g = (
            m.sem(f"e_s_{n}") for n in ("whi", "wlo", "xn", "tr", "xhi", "xlo", "l", "p", "g"))
        s_qk, s_qe, s_vhi, s_vlo, s_vp = (m.sem(f"e_s_{n}") for n in ("qk", "qe", "vhi", "vlo", "vp"))
        s_pass = m.sem("e_s_pass")
        s_even, s_odd, s_av, s_ds, s_ts, s_ts1, s_vo = (
            m.sem(f"e_s_{n}") for n in ("even", "odd", "av", "ds", "ts", "ts1", "vo"))

        def normalize(eng, b):
            return eng.tensor_scalar(xn[:, b % 4, :], x1t[:, b, :], mv[0:SQ, b, 0:1], rstd[:, b:b + 1],
                                     ALU.subtract, ALU.mult)

        def logit_tiles(t, lag=0):
            old = lambda t: (t - 1) * SQ // P if 1 <= t < NB else NT if t >= NB else 0
            return range(old(t - lag - 1), old(t - lag))

        def turned(t):
            return (p_t[:, t % 4, 0:DC * SQ].rearrange("p (c n) -> p c n", c=DC),
                    slice(t * SQ, (t + 1) * SQ))

        NG = NT * 2 * H
        QF = 4
        PARTS = NB // 8
        with nc.Block() as block:

            @block.sync
            def _(sp):
                for u in range(2):
                    sp.sem_inc(s_qo[u], 16)
                sp.dma_start(sst[:, :, :], sel_t.rearrange("(c p) e -> p c e", p=P)).then_inc(s_sel, 16)
                sp.dma_start(rsb[:, :], rs.partition_broadcast(P)).then_inc(s_rs, 16)
                sp.dma_start(wst[:, 0, :, :], q_t.rearrange("(c p) n -> p c n", p=P)).then_inc(s_wq, 16)
                sp.dma_start(wst[:, 1, :, :], k_t.rearrange("(c p) n -> p c n", p=P)).then_inc(s_wk, 16)
                with sp.Fori(0, H) as i:
                    for u in range(2):
                        sp.wait_ge(s_qe, QF + NC * (2 * i + u + 1))
                        sp.dma_start(qk_out[2 * i + u, :, :], qko[:, u, :]).then_inc(s_qo[u], 16)
                with sp.Fori(0, H // 2) as i:
                    for g in range(5):
                        sp.wait_ge(s_vo, 50 * i + 10 * (g + 1) + 2)
                        sp.dma_start(
                            v_out[640 * g:640 * g + 640, bass.ds(i * 2 * PD, 2 * PD)].rearrange(
                                "(t p) n -> p t n", p=P),
                            vout[:, 5 * g:5 * g + 5, :, :].rearrange("p t a d -> p t (a d)")
                        ).then_inc(s_vst[g], 16)
                for g in range(5):
                    sp.wait_ge(s_vst[g], 16 * (1 + H // 2))
                for u in range(2):
                    sp.wait_ge(s_qo[u], 16 * (H + 1))

            @block.gpsimd
            def _(pool):
                for g in range(5):
                    pool.sem_inc(s_vst[g], 16)
                pool.sem_inc(s_ts, 2)
                pool.sem_inc(s_vo, 2)
                pool.wait_ge(s_step, 6)
                for b in range(3, NB, 4):
                    at_least(pool, s_t, b - 3)
                    normalize(pool, b).then_inc(s_xnp, 1)
                for e in range(E):
                    pool.memset(order[:, e:e + 1], float(E - e)).then_inc(s_ord, 1)
                for h in range(H):
                    if h < 2:
                        pool.wait_ge(s_wlo, 2 + h)
                    else:
                        pool.wait_ge(s_vlo, h - 1)
                    pool.dma_start(wst[:, h % 2, :, :],
                                 v_t[:, h * E * PD:(h + 1) * E * PD].rearrange("(c p) n -> p c n", p=P)
                                 ).then_inc(s_vw[h % 2], 16)
                for u in range(2):
                    pool.wait_ge(s_qo[u], 16 * (H + 1))

                def unit(i, g, t, hh):
                    n = 50 * i + 2 * t + hh
                    pool.wait_ge(s_av, 4 * n + 12)
                    pool.tensor_tensor(tsum[:, hh, :, :], tmp[:, hh, 0:2, :], tmp[:, hh, 2:4, :],
                                       ALU.add).then_inc(s_ts, 1)
                    pool.wait_ge(s_ts, n + 3)
                    pool.wait_ge(s_vo, n + 1)
                    pool.tensor_tensor(tsum1[:, hh, :], tsum[:, hh, 0, :], tsum[:, hh, 1, :],
                                       ALU.add).then_inc(s_ts1, 1)
                    pool.wait_ge(s_ts1, n + 1)
                    pool.wait_ge(s_ds, n + 3)
                    pool.tensor_tensor(vout[:, t, hh, :], tsum1[:, hh, :], dsum[:, hh, :],
                                       ALU.add).then_inc(s_vo, 1)

                with pool.Fori(0, H // 2) as i:
                    for g in range(5):
                        pool.wait_ge(s_vst[g], 16 * i + 16)
                        pass_wait(pool, s_pass)
                        with pool.Fori(5 * g, 5 * g + 5) as t:
                            unit(i, g, t, 0)
                            unit(i, g, t, 1)

            @block.vector
            def _(dve):
                dve.sem_inc(s_ds, 2)
                rstd_steps(dve, mv[0:SQ, :, :], std, rstd, half, s_step, s_std, 0)

                def x_lo(t):
                    bank, tok = turned(t)
                    dve.wait_ge(s_xhi, t + 1)
                    dve.tensor_tensor(xlo[:, :, tok], bank, xhi[:, :, tok], ALU.subtract).then_inc(s_xlo, 1)

                for t in range(NB):
                    if t % 4 < 3:
                        at_least(dve, s_t, t - 3)
                        normalize(dve, t).then_inc(s_xn, 1)
                    if t >= 2:
                        x_lo(t - 2)
                    if t == 1:
                        dve.wait_ge(s_whi, 1)
                        dve.scalar_tensor_tensor(out=slo[:, :, :], in0=sst[:, :, :], scalar=WS,
                                                 in1=shi[:, :, :], op0=ALU.mult,
                                                 op1=ALU.subtract).then_inc(s_wlo, 1)
                x_lo(NB - 2)
                x_lo(NB - 1)
                for w in range(2):
                    dve.wait_ge(s_whi, 2 + w)
                    dve.scalar_tensor_tensor(
                        out=qklo[:, :, w * H * PD:(w + 1) * H * PD], in0=wst[:, w, :, :], scalar=WS,
                        in1=qkhi[:, :, w * H * PD:(w + 1) * H * PD],
                        op0=ALU.mult, op1=ALU.subtract).then_inc(s_wlo, 1)

                def spread(v):
                    return v[:, :].unsqueeze(2).broadcast_to([P, NG, E])

                steps = [0]

                def step(ins):
                    ins.then_inc(s_g, 1)
                    steps[0] += 1
                    dve.wait_ge(s_g, steps[0])

                ranks = order[:, :].unsqueeze(1).broadcast_to([P, NG, E])
                dve.wait_ge(s_p, NT)
                dve.wait_ge(s_ord, E)
                step(dve.tensor_reduce(out=m1[:, :], in_=prob, axis=AX, op=ALU.max))
                step(dve.tensor_tensor(pick1, prob, spread(m1), ALU.is_equal))
                step(dve.tensor_tensor(pick1, pick1, ranks, ALU.mult))
                step(dve.tensor_reduce(out=top[:, :], in_=pick1, axis=AX, op=ALU.max))
                step(dve.tensor_tensor(pick1, pick1, spread(top), ALU.is_equal))
                step(dve.scalar_tensor_tensor(out=pick2, in0=pick1, scalar=-3.0, in1=prob,
                                              op0=ALU.mult, op1=ALU.add))
                step(dve.tensor_reduce(out=m2[:, :], in_=pick2, axis=AX, op=ALU.max))
                step(dve.tensor_tensor(pick2, pick2, spread(m2), ALU.is_equal))
                step(dve.tensor_tensor(pick2, pick2, ranks, ALU.mult))
                step(dve.tensor_reduce(out=top[:, :], in_=pick2, axis=AX, op=ALU.max))
                step(dve.tensor_tensor(pick2, pick2, spread(top), ALU.is_equal))
                step(dve.tensor_tensor(tot[:, :], m1[:, :], m2[:, :], ALU.add))
                step(dve.tensor_scalar(tot[:, :], tot[:, :], 1e-9, None, ALU.max))
                step(dve.reciprocal(tot[:, :], tot[:, :]))
                dve.wait_ge(s_rs, 16)
                step(dve.tensor_scalar(tot[:, :], tot[:, :], rsb[:, 0:1], None, ALU.mult))
                step(dve.tensor_scalar(tot[:, :], tot[:, :], 1.0 / WS, None, ALU.mult))
                step(dve.tensor_tensor(m1[:, :], m1[:, :], tot[:, :], ALU.mult))
                step(dve.tensor_tensor(m2[:, :], m2[:, :], tot[:, :], ALU.mult))
                step(dve.tensor_tensor(pick1, pick1, spread(m1), ALU.mult))
                step(dve.tensor_tensor(pick2, pick2, spread(m2), ALU.mult))
                step(dve.tensor_tensor(pick1, pick1, pick2, ALU.add))

                for h in range(H):
                    cut = slice(h * E * PD, (h + 1) * E * PD)
                    dve.wait_ge(s_vw[h % 2], 16 * (h // 2 + 1))
                    dve.tensor_scalar(vhi[:, :, cut], wst[:, h % 2, :, :], WS, None,
                                      ALU.mult).then_inc(s_vhi, 1)
                    dve.wait_ge(s_vhi, h + 1)
                    dve.scalar_tensor_tensor(out=vlo[:, :, cut], in0=wst[:, h % 2, :, :], scalar=WS,
                                             in1=vhi[:, :, cut], op0=ALU.mult,
                                             op1=ALU.subtract).then_inc(s_vlo, 1)

                def unit(i, t, hh):
                    n = 50 * i + 2 * t + hh
                    for e in range(4):
                        gate = k.gates[:, bass.ds(t * P + 2 * E * i + E * hh + e, 1)]
                        chain = s_even if e % 2 == 0 else s_odd
                        if e < 2:
                            if e == 0:
                                dve.wait_ge(s_vp, 2 * n + 1)
                                dve.wait_ge(s_ds, n + 1)
                            dve.tensor_scalar(acc[:, hh, e, :], p_v[:, hh, 0, e * PD:(e + 1) * PD], gate,
                                              None, ALU.mult).then_inc(chain, 1)
                        else:
                            dve.wait_ge(chain, 2 * n + 1)
                            last = dve.scalar_tensor_tensor(
                                out=acc[:, hh, e % 2, :], in0=p_v[:, hh, 0, e * PD:(e + 1) * PD],
                                scalar=gate, in1=acc[:, hh, e % 2, :], op0=ALU.mult, op1=ALU.add)
                            last.then_inc(chain, 1)
                    dve.wait_ge(s_even, 2 * n + 2)
                    dve.wait_ge(s_odd, 2 * n + 2)
                    dve.wait_ge(s_vo, n + 1)
                    dve.tensor_tensor(dsum[:, hh, :], acc[:, hh, 0, :], acc[:, hh, 1, :],
                                      ALU.add).then_inc(s_ds, 1)

                with dve.Fori(0, H // 2) as i:
                    with dve.Fori(0, NT) as t:
                        unit(i, t, 0)
                        unit(i, t, 1)

            @block.scalar
            def _(act):
                act.wait_ge(s_step, 1)
                act.activation(std[:, :], mv[0:SQ, :, 1], ACT.Sqrt).then_inc(s_std, 1)
                act.wait_ge(s_sel, 16)
                act.activation(shi[:, :, :], sst[:, :, :], ACT.Copy, scale=WS).then_inc(s_whi, 1)
                def probabilities(t):
                    act.wait_ge(s_l, t + 1)
                    act.activation(big[:, t * P:(t + 1) * P], p_q[:, t % QF, 0:P], ACT.Sigmoid,
                                   scale=1.0 / WS).then_inc(s_p, 1)

                for t in range(NB):
                    bank, tok = turned(t)
                    act.wait_ge(s_t, t + 1)
                    act.activation(xhi[:, :, tok], bank, ACT.Copy).then_inc(s_xhi, 1)
                    for n in logit_tiles(t, lag=1):
                        probabilities(n)
                    if t >= NB // 2 and t % 2 == 0:
                        w, part = divmod((t - NB // 2) // 2, PARTS)
                        act.wait_ge((s_wq, s_wk)[w], 16)
                        cut = slice(part * H * PD // PARTS, (part + 1) * H * PD // PARTS)
                        last = act.activation(qkhi[:, :, w * H * PD:(w + 1) * H * PD][:, :, cut],
                                              wst[:, w, :, cut], ACT.Copy, scale=WS)
                        if part == PARTS - 1:
                            last.then_inc(s_whi, 1)
                for n in (*logit_tiles(NB - 1), *logit_tiles(NB)):
                    probabilities(n)
                act.sem_inc(s_qe, QF)
                with act.Fori(0, H) as i:
                    for u in range(2):
                        act.wait_ge(s_qo[u], 16 * i + 16)
                        for c in range(NC):
                            act.wait_ge(s_qk, NC * (2 * i + u) + c + 1)
                            act.activation(qko[:, u, c * NW:(c + 1) * NW], p_q[:, c % QF, 0:NW],
                                           ACT.Copy).then_inc(s_qe, 1)
                act.sem_inc(s_av, 8)

                def unit(i, t, hh):
                    n = 50 * i + 2 * t + hh
                    act.wait_ge(s_vp, 2 * n + 2)
                    act.wait_ge(s_ts, n + 1)
                    for e in range(4):
                        gate = k.gates[:, bass.ds(t * P + 2 * E * i + E * hh + 4 + e, 1)]
                        act.activation(tmp[:, hh, e, :], p_v[:, hh, 1, e * PD:(e + 1) * PD], ACT.Copy,
                                       scale=gate).then_inc(s_av, 1)

                with act.Fori(0, H // 2) as i:
                    with act.Fori(0, NT) as t:
                        unit(i, t, 0)
                        unit(i, t, 1)

            @block.tensor
            def _(pe):
                def logits(t):
                    if t == 0:
                        pe.wait_ge(s_wlo, 1)
                    pe.wait_ge(s_xlo, -(-(t + 1) * P // SQ))
                    at_least(pe, s_p, t - QF + 1)
                    tok = slice(t * P, (t + 1) * P)
                    for n, (c, a, b) in enumerate((c, a, b) for c in range(DC)
                                                  for a, b in ((xhi, shi), (xhi, slo), (xlo, shi))):
                        last = pe.matmul(p_q[:, t % QF, 0:P], a[:, c, tok], b[:, c, :],
                                         start=n == 0, stop=n == 3 * DC - 1)
                    last.then_inc(s_l, 1)

                for t in range(NB):
                    if t % 4 < 3:
                        pe.wait_ge(s_xn, 3 * (t // 4) + t % 4 + 1)
                    else:
                        pe.wait_ge(s_xnp, t // 4 + 1)
                    at_least(pe, s_xlo, t - 3)
                    for c in range(DC):
                        last = pe.transpose(p_t[:, t % 4, c * SQ:(c + 1) * SQ],
                                            xn[:, t % 4, c * P:(c + 1) * P], k.ident[0:SQ, 0:SQ])
                    last.then_inc(s_t, 1)
                    for n in logit_tiles(t):
                        logits(n)
                for n in logit_tiles(NB):
                    logits(n)
                pe.wait_ge(s_p, NT)
                for part in range(2):
                    pe.wait_ge(s_wlo, 2 + part)
                    with pe.Fori(part * H, (part + 1) * H) as u:
                        for w in range(NC):
                            pe.wait_ge(s_qe, NC * u + w + 1)
                            tok = slice(w * NW, (w + 1) * NW)
                            for n, (c, a, b) in enumerate((c, a, b) for c in range(DC)
                                                          for a, b in ((qkhi, xhi), (qkhi, xlo), (qklo, xhi))):
                                last = pe.matmul(p_q[:, w % QF, 0:NW], a[:, c, bass.ds(u * PD, PD)],
                                                 b[:, c, tok], start=n == 0, stop=n == 3 * DC - 1)
                            last.then_inc(s_qk, 1)
                pe.wait_ge(s_qe, QF + 2 * H * NC)
                pe.wait_ge(s_vlo, H)

                def unit(i, t, hh):
                    n = 50 * i + 2 * t + hh
                    for half in range(2):
                        if half == 0:
                            pe.wait_ge(s_ds, n + 1)
                        else:
                            pe.wait_ge(s_av, 4 * n + 4)
                        col = 2 * E * PD * i + E * PD * hh + half * 512
                        for j, (c, a, b) in enumerate((c, a, b) for c in range(DC)
                                                      for a, b in ((xhi, vhi), (xhi, vlo), (xlo, vhi))):
                            last = pe.matmul(p_v[:, hh, half, :], a[:, c, bass.ds(t * P, P)],
                                             b[:, c, bass.ds(col, 512)], start=j == 0, stop=j == 3 * DC - 1)
                        last.then_inc(s_vp, 1)

                with pe.Fori(0, H // 2) as i:
                    with pe.Fori(0, NT) as t:
                        unit(i, t, 0)
                        unit(i, t, 1)



def stage_attention_out(nc, k, x1, qk, v, o_w, y):
    SCALE = PD ** -0.5 / WS ** 2
    GB = 4
    GC = GB * SQ
    NGR = NB // GB
    TT = 3
    ACT_PAIRS = ((2,), (0, 3), (2,))
    DVE_PAIRS = tuple(tuple(q for q in range(4) if q not in a) for a in ACT_PAIRS)
    ACT_TURN, DVE_TURN = sum(map(len, ACT_PAIRS)), sum(map(len, DVE_PAIRS))
    ACT_HEAD = NGR * ACT_TURN + len(ACT_PAIRS[-1])
    DVE_HEAD = NGR * DVE_TURN + len(DVE_PAIRS[-1])
    PIECES = NGR // 2
    PIECE = E * D // PIECES

    class Tile:

        def __init__(self, h, j, place, last=False):
            self.t, self.last = j * TT + place, last
            self.place = TT - 1 if last else place
            self.act = h * ACT_HEAD + j * ACT_TURN + sum(map(len, ACT_PAIRS[:place]))
            self.dve = h * DVE_HEAD + j * DVE_TURN + sum(map(len, DVE_PAIRS[:place]))

    def slot(x, r):
        return sum(map(len, ACT_PAIRS[:TT - 2 if x.last else x.place])) + r

    def place(b):
        return bass.ds(b.n % (2 * NGR) * GC, GC)

    def attention_alone(eng, group, piece=lambda h, buf, jj: None):
        for jj in range(2):
            group(fixed(jj), ())
            piece(0, 0, 2 * jj)
            piece(0, 0, 2 * jj + 1)
        with eng.Fori(1, NGR // 2) as jj:
            group(Batch(2 * jj, 0, jj), ())
            group(Batch(2 * jj + 1, 1, jj), ())

    def heads(eng, group, tile, piece, rest, end=lambda x: None):
        def turns(h, buf, more, jj):
            for u in range(2):
                tiles = [Tile(h, 2 * jj + u, p) for p in range(TT)]
                if more:
                    group(Batch(NGR * (h + 1) + 2 * jj + u, u, NGR // 2 * (h + 1) + jj),
                          [(lambda x=x: tile(h, buf, x)) for x in tiles])
                    if u == 0:
                        piece(h + 1, 1 - buf, jj)
                else:
                    for p, x in enumerate(tiles):
                        tile(h, buf, x)
                        if not (isinstance(jj, int) and u == 0):
                            end(Tile(h, 2 * jj + u - 1, p))

        def head(h, buf, more):
            if not more:
                rest()
                turns(h, buf, more, 0)
            with eng.Fori(0 if more else 1, NGR // 2) as jj:
                turns(h, buf, more, jj)
            tile(h, buf, Tile(h, NGR, 0, last=True))
            if not more:
                for p in range(TT):
                    end(Tile(h, NGR - 1, p))
                end(Tile(h, NGR, 0, last=True))

        with eng.Fori(0, H // 2 - 1) as i:
            head(2 * i, 0, True)
            head(2 * i + 1, 1, True)
        head(H - 2, 0, True)
        head(H - 1, 1, False)

    with ExitStack() as ctx:
        m = Store(nc, ctx)
        qb, kb = (m.sbuf(f"a_{n}", [P, 2, GC]) for n in "qk")
        vb = m.sbuf("a_v", [SQ, 2, GB, PD])
        mx, mxs, sums, rsum = (m.sbuf(f"a_{n}", [SQ, 2, GB]) for n in ("mx", "mxs", "sums", "rsum"))
        ex, ext = m.sbuf("a_ex", [SQ, 2, GC]), m.sbuf("a_ext", [SQ, GC])
        chi, clo = (m.sbuf(f"a_c{n}", [P, 2 * T], F16) for n in ("hi", "lo"))
        main = m.sbuf("o_main", [P, NT, D])
        side = m.sbuf("o_side", [P, NT, D])
        wst = m.sbuf("o_wst", [P, E * D])
        whi, wlo = (m.sbuf(f"o_w{n}", [P, 2, E * D], F16) for n in ("hi", "lo"))
        tmp = m.sbuf("o_tmp", [P, ACT_TURN, 2, D])
        p_s = m.psum("a_ps", [P, 2, 512])
        p_t, p_c = (m.psum(f"a_p{n}", [P, 512]) for n in "tc")
        p_y = m.psum("o_py", [P, 4, 2, D])
        s_q, s_k, s_v = (m.sems(f"a_s_{n}", 2) for n in ("q", "k", "v"))
        s_s, s_mx, s_mxs, s_ex, s_rs, s_n, s_t, s_ext, s_c, s_hi, s_lo = (
            m.sem(f"a_s_{n}") for n in ("s", "mx", "mxs", "ex", "rs", "n", "t", "ext", "c", "hi", "lo"))
        s_x, s_y, s_g, s_w, s_whi, s_wlo = (m.sem(f"o_s_{n}") for n in ("x", "y", "g", "w", "whi", "wlo"))
        s_p, s_av, s_main, s_side, s_pool, s_end = (
            m.sem(f"o_s_{n}") for n in ("p", "av", "main", "side", "pool", "end"))
        s_pass_pool, s_pass_sp = (m.sem(f"o_s_pass_{n}") for n in ("pool", "sp"))
        go = k.gates[:, :].rearrange("p (t a n) -> p t a n", a=2, n=HE)[:, :, 1, :]
        ACT_AHEAD, DVE_AHEAD = len(ACT_PAIRS[-1]), len(DVE_PAIRS[-1])
        POOL_AHEAD = 2 * ACT_HEAD
        with nc.Block() as block:

            @block.sync
            def _(sp):
                def load_qk(b):
                    h, tok = b.n // NGR, bass.ds(b.n % NGR * GC, GC)
                    at_least(sp, s_s, b.n - 1)
                    pass_wait(sp, s_pass_sp)
                    sp.dma_start(qb[:, b.par, :], qk[h, :, tok]).then_inc(s_q[b.par], 16)
                    sp.dma_start(kb[:, b.par, :], qk[h + H, :, tok]).then_inc(s_k[b.par], 16)

                def load_v(b):
                    h, tok = b.n // NGR, bass.ds(b.n % NGR * GC, GC)
                    at_least(sp, s_c, b.n - 1)
                    pass_wait(sp, s_pass_sp)
                    sp.dma_start(vb[:, b.par, :, :], v[tok, bass.ds(h * PD, PD)].rearrange(
                        "(i q) d -> q i d", i=GB)).then_inc(s_v[b.par], 16)

                def load_piece(h, jj):
                    sp.dma_start(wst[:, bass.ds(jj * PIECE, PIECE)],
                                 o_w[:, bass.ds(h * E * D + jj * PIECE, PIECE)]).then_inc(s_w, 16)

                def load_x1(g):
                    sp.dma_start(main[:, bass.ds(5 * g, 5), :],
                                 x1[bass.ds(640 * g, 640), :].rearrange("(t p) d -> p t d", p=P)
                                 ).then_inc(s_x, 16)

                def groups(h, jj, last=False):
                    for u in range(2):
                        b = Batch(NGR * h + 2 * jj + u, u, NGR // 2 * h + jj)
                        if not (last and u == 1):
                            load_qk(b.next())
                        load_v(b)

                def weights(h, jj):
                    sp.wait_ge(s_wlo, PIECES * h + jj)
                    pass_wait(sp, s_pass_sp)
                    load_piece(h, jj)

                load_qk(fixed(0))
                load_qk(fixed(1))
                load_v(fixed(0))
                for jj in range(PIECES):
                    load_piece(0, jj)
                load_qk(fixed(2))
                load_v(fixed(1))
                load_x1(0)
                load_x1(1)
                with sp.Fori(1, NGR // 2) as jj:
                    groups(0, jj)
                    load_x1(jj + 1)
                with sp.Fori(1, H - 1) as h:
                    with sp.Fori(0, NGR // 2) as jj:
                        groups(h, jj)
                        weights(h, jj)
                with sp.Fori(0, NGR // 2 - 1) as jj:
                    groups(H - 1, jj)
                    weights(H - 1, jj)
                groups(H - 1, NGR // 2 - 1, last=True)
                weights(H - 1, NGR // 2 - 1)
                cuts = (0, 5, 10, 15, 20, NT - 1, NT)
                for start, end in zip(cuts, cuts[1:]):
                    sp.wait_ge(s_end, end)
                    sp.dma_start(y[P * start:P * end, :].rearrange("(t p) d -> p t d", p=P),
                                 main[:, start:end, :]).then_inc(s_y, 16)
                sp.wait_ge(s_y, 16 * (len(cuts) - 1))

            @block.gpsimd
            def _(pool):
                pool.memset(side[:, :, :], 0.0).then_inc(s_pool, POOL_AHEAD)

                def normalize(b):
                    pool.wait_ge(s_rs, b.n + 1)
                    rows = ex[:, b.par, :].rearrange("p (i s) -> p i s", i=GB)
                    pool.tensor_tensor(rows, rows, rsum[:, b.par, :].unsqueeze(2).broadcast_to([SQ, GB, SQ]),
                                       ALU.mult).then_inc(s_n, 1)

                def tile(h, buf, x):
                    pool.wait_ge(s_side, DVE_AHEAD + x.dve + len(DVE_PAIRS[x.place]))
                    for r in range(len(ACT_PAIRS[x.place])):
                        for j in range(2):
                            n = 2 * (x.act + r) + j
                            pool.wait_ge(s_av, 2 * ACT_AHEAD + n + 1)
                            pool.wait_ge(s_pool, POOL_AHEAD + n)
                            pass_wait(pool, s_pass_pool)
                            pool.tensor_tensor(side[:, x.t, :], side[:, x.t, :],
                                               tmp[:, slot(x, r), j, :], ALU.add).then_inc(s_pool, 1)

                def group(b, tiles):
                    for i, one in enumerate(tiles):
                        one()
                        if i == 0:
                            normalize(b)
                    if not tiles:
                        normalize(b)

                attention_alone(pool, group)
                heads(pool, group, tile, lambda h, buf, jj: None, lambda: None)

            @block.vector
            def _(dve):
                dve.sem_inc(s_side, DVE_AHEAD)
                dve.tensor_scalar(go, go, k.tanh_g[:, 1:2], None, ALU.mult).then_inc(s_g, 1)

                def maxima(b):
                    dve.wait_ge(s_s, b.n + 1)
                    dve.tensor_reduce(out=mx[:, b.par, :], in_=p_s[0:SQ, b.par, 0:GC].rearrange(
                        "p (i s) -> p i s", i=GB), axis=AX, op=ALU.max).then_inc(s_mx, 1)
                    dve.wait_ge(s_mx, b.n + 1)
                    at_least(dve, s_ex, b.n - 1)
                    dve.tensor_scalar(mxs[:, b.par, :], mx[:, b.par, :], -SCALE, None,
                                      ALU.mult).then_inc(s_mxs, 1)

                def invert(b):
                    dve.wait_ge(s_ex, b.n + 1)
                    at_least(dve, s_n, b.n - 1)
                    dve.reciprocal(rsum[:, b.par, :], sums[:, b.par, :]).then_inc(s_rs, 1)

                def copy_ext(b):
                    dve.wait_ge(s_t, b.n + 1)
                    at_least(dve, s_c, b.n)
                    dve.tensor_copy(ext[:, :], p_t[0:SQ, 0:GC]).then_inc(s_ext, 1)

                def low(b, col):
                    dve.wait_ge(s_hi, b.n + 1)
                    dve.tensor_tensor(clo[:, col], p_c[:, 0:GC], chi[:, col],
                                      ALU.subtract).then_inc(s_lo, 1)

                def tile(h, buf, x):
                    dve.wait_ge(s_pool, 2 * (x.act + len(ACT_PAIRS[x.place])))
                    for r, q in enumerate(DVE_PAIRS[x.place]):
                        n = x.dve + r
                        dve.wait_ge(s_p, 4 * NT * h + 4 * x.t + q + 1)
                        for j, (into, chain, ahead) in enumerate(((main, s_main, 0),
                                                                  (side, s_side, DVE_AHEAD))):
                            if r > 0:
                                dve.wait_ge(chain, ahead + n)
                            gate = k.gates[:, bass.ds(x.t * P + HE + h * E + 2 * q + j, 1)]
                            dve.scalar_tensor_tensor(
                                out=into[:, x.t, :], in0=p_y[:, q, j, :], scalar=gate,
                                in1=into[:, x.t, :], op0=ALU.mult, op1=ALU.add).then_inc(chain, 1)

                def group(b, tiles):
                    maxima(b)
                    if not is_first(b):
                        copy_ext(b.before())
                    if tiles:
                        tiles[0]()
                    invert(b)
                    if not is_first(b):
                        low(b.before(), place(b.before()))
                    for one in tiles[1:]:
                        one()

                def piece(h, buf, jj):
                    dve.wait_ge(s_whi, PIECES * h + jj + 1)
                    cut = bass.ds(jj * PIECE, PIECE)
                    dve.scalar_tensor_tensor(out=wlo[:, buf, cut], in0=wst[:, cut], scalar=WS,
                                             in1=whi[:, buf, cut], op0=ALU.mult,
                                             op1=ALU.subtract).then_inc(s_wlo, 1)

                attention_alone(dve, group, piece)
                dve.wait_ge(s_x, 80)

                def rest():
                    b = fixed(NB * H // GB - 1)
                    copy_ext(b)
                    low(b, place(b))

                def end(x):
                    dve.wait_ge(s_pool, POOL_AHEAD + 2 * (x.act + len(ACT_PAIRS[x.place])))
                    dve.wait_ge(s_main, x.dve + len(DVE_PAIRS[x.place]))
                    dve.tensor_tensor(main[:, x.t, :], main[:, x.t, :], side[:, x.t, :],
                                      ALU.add).then_inc(s_end, 1)

                heads(dve, group, tile, piece, rest, end)

            @block.scalar
            def _(act):
                act.sem_inc(s_av, 2 * ACT_AHEAD)

                def exps(b):
                    at_least(act, s_rs, b.n - 1)
                    act.wait_ge(s_mxs, b.n + 1)
                    at_least(act, s_t, b.n - 1)
                    for i in range(GB):
                        cut = slice(i * SQ, (i + 1) * SQ)
                        last = act.activation(ex[:, b.par, cut], p_s[0:SQ, b.par, cut], ACT.Exp,
                                              bias=mxs[:, b.par, i:i + 1], scale=SCALE,
                                              accum_out=sums[:, b.par, i:i + 1])
                    last.then_inc(s_ex, 1)

                def high(b, col):
                    act.wait_ge(s_c, b.n + 1)
                    act.activation(chi[:, col], p_c[:, 0:GC], ACT.Copy).then_inc(s_hi, 1)

                def tile(h, buf, x):
                    for r, q in enumerate(ACT_PAIRS[x.place]):
                        act.wait_ge(s_p, 4 * NT * h + 4 * x.t + q + 1)
                        if r == 0:
                            before = len(ACT_PAIRS[-1 if x.last else (x.place - 1) % TT])
                            act.wait_ge(s_pool, POOL_AHEAD + 2 * (x.act - before))
                        for j in range(2):
                            gate = k.gates[:, bass.ds(x.t * P + HE + h * E + 2 * q + j, 1)]
                            act.activation(tmp[:, slot(x, r), j, :], p_y[:, q, j, :], ACT.Copy,
                                           scale=gate).then_inc(s_av, 1)

                def group(b, tiles):
                    exps(b)
                    if tiles:
                        tiles[0]()
                    if not is_first(b):
                        high(b.before(), place(b.before()))
                    for one in tiles[1:]:
                        one()

                def piece(h, buf, jj):
                    act.wait_ge(s_w, 16 * (PIECES if isinstance(h, int) and h == 0 else PIECES * h + jj + 1))
                    cut = bass.ds(jj * PIECE, PIECE)
                    act.activation(whi[:, buf, cut], wst[:, cut], ACT.Copy, scale=WS).then_inc(s_whi, 1)

                attention_alone(act, group, piece)
                act.wait_ge(s_g, 1)

                def rest():
                    b = fixed(NB * H // GB - 1)
                    high(b, place(b))

                heads(act, group, tile, piece, rest)

            @block.tensor
            def _(pe):
                def scores(b):
                    pe.wait_ge(s_q[b.par], 16 * (b.half + 1))
                    pe.wait_ge(s_k[b.par], 16 * (b.half + 1))
                    at_least(pe, s_ex, b.n - 1)
                    for i in range(GB):
                        cut = slice(i * SQ, (i + 1) * SQ)
                        last = pe.matmul(p_s[0:SQ, b.par, cut], qb[:, b.par, cut], kb[:, b.par, cut],
                                         start=True, stop=True)
                    last.then_inc(s_s, 1)

                def turn(b):
                    pe.wait_ge(s_n, b.n + 1)
                    at_least(pe, s_ext, b.n)
                    for i in range(GB):
                        cut = slice(i * SQ, (i + 1) * SQ)
                        last = pe.transpose(p_t[0:SQ, cut], ex[:, b.par, cut], k.ident[0:SQ, 0:SQ])
                    last.then_inc(s_t, 1)

                def attend(b):
                    pe.wait_ge(s_v[b.par], 16 * (b.half + 1))
                    pe.wait_ge(s_ext, b.n + 1)
                    at_least(pe, s_lo, b.n)
                    for i in range(GB):
                        cut = slice(i * SQ, (i + 1) * SQ)
                        last = pe.matmul(p_c[:, cut], vb[:, b.par, i, :], ext[:, cut], start=True, stop=True)
                    last.then_inc(s_c, 1)

                def tile(h, buf, x):
                    if x.place == 0:
                        pe.wait_ge(s_wlo, PIECES * (h + 1))
                        pe.wait_ge(s_lo, NGR * h + NGR - 1)
                    if not x.last and x.place == TT - 1:
                        pe.wait_ge(s_lo, NGR * h + NGR)
                    before = TT - 1 if x.place == 0 or x.last else x.place - 1
                    for q in range(4):
                        if q in ACT_PAIRS[before]:
                            left = len(ACT_PAIRS[before]) - 1 - ACT_PAIRS[before].index(q)
                            pe.wait_ge(s_av, 2 * (ACT_AHEAD + x.act - left))
                        else:
                            left = len(DVE_PAIRS[before]) - 1 - DVE_PAIRS[before].index(q)
                            pe.wait_ge(s_side, DVE_AHEAD + x.dve - left)
                        cut = slice(2 * D * q, 2 * D * (q + 1))
                        for j, (a, b) in enumerate(((chi, whi), (chi, wlo), (clo, whi))):
                            last = pe.matmul(p_y[:, q, :, :].rearrange("p j d -> p (j d)"),
                                             a[:, bass.ds(buf * T + x.t * P, P)], b[:, buf, cut],
                                             start=j == 0, stop=j == 2)
                        last.then_inc(s_p, 1)

                def group(b, tiles):
                    scores(b)
                    if not is_first(b):
                        turn(b.before())
                    if tiles:
                        tiles[0]()
                    if not is_first(b):
                        attend(b.before())
                    for one in tiles[1:]:
                        one()

                def rest():
                    b = fixed(NB * H // GB - 1)
                    turn(b)
                    attend(b)

                attention_alone(pe, group)
                heads(pe, group, tile, lambda h, buf, jj: None, rest)


class Constants:
    pass


def constants(nc, ctx):
    k = Constants()
    m = Store(nc, ctx)
    k.ident = m.sbuf("ident", [P, P])
    k.tanh_g = m.sbuf("tanh_g", [P, 2])
    k.gates = m.sbuf("gates", [P, NT * 2 * HE])
    return k


def cross_inputs(nc, ctx):
    c = Constants()
    m = Store(nc, ctx)
    c.w = m.sbuf("c_w", [P, 3, DC, D])
    c.bkc, c.bvc = m.sbuf("c_bk", [P, DC]), m.sbuf("c_bv", [P, DC])
    c.bor = m.sbuf("c_bo", [1, D])
    c.whi, c.wlo = (m.sbuf(f"c_w{n}", [P, 2, DC, D], F16) for n in ("hi", "lo"))
    c.ctxb = m.sbuf("c_ctx", [P, 2, DC, SK])
    c.ctxh, c.ctxl = (m.sbuf(f"c_ctx{n}", [P, 2, DC, SK], F16) for n in ("hi", "lo"))
    c.qst = m.sbuf("c_qst", [P, 2, XH, SQ], F16)
    c.vz = m.sbuf("c_v", [KW, 2, KC, XH // 2, 3, XD])
    c.ex = m.sbuf("c_ex", [SQ, 4, SKP])
    return c


def flamingo(nc, x, ctx_t, mask, g_xattn, g_ffn, wq, bq, wk, bk, wv, bv, wo, bo, sel, qw, kw, vw, ow, rs, y):
    def scratch(name, shape, dt=F32):
        return nc.dram_tensor(name, shape, dt, kind="Internal").ap()

    q_parts = scratch("q_parts", [2, D, T], F16)
    k_parts = scratch("k_parts", [2, 2, D, SK], F16)
    x1 = scratch("x1", [T, D])
    qk = scratch("qk", [2 * H, PD, T])
    v = scratch("v", [T, H * PD])
    with ExitStack() as ctx:
        k = constants(nc, ctx)
        with ExitStack() as inner:
            m = Store(nc, inner)
            big = m.sbuf("big", [P, NB * D])
            mv = m.sbuf("x1_mv", [P, NB, 2])
            with ExitStack() as innermost:
                c = cross_inputs(nc, innermost)
                stage_queries(nc, k, c, x, g_xattn, g_ffn, wq, bq, ctx_t, (wk, wv, wo), (bk, bv, bo), q_parts)
                stage_cross(nc, k, c, x, ctx_t, mask, q_parts, k_parts, big, mv, x1)
            stage_experts_in(nc, k, big, mv, sel, qw, kw, vw, rs, qk, v)
        stage_attention_out(nc, k, x1, qk, v, ow, y)


def kernel(**inputs):
    import concourse.bacc as bacc
    import numpy as np
    from concourse.bass_utils import run_bass_kernel_spmd

    def arr(name):
        return np.asarray(inputs[name])

    def turned(name):
        return np.ascontiguousarray(arr(name).T)

    def column(name):
        return np.ascontiguousarray(arr(name).reshape(DC, P).T)

    sel = np.concatenate([arr("L0_ffn_sel_v_w"), arr("L0_ffn_sel_o_w")], axis=0)
    arrays = {
        "x": np.ascontiguousarray(arr("x").reshape(T, D)),
        "ctx_t": np.ascontiguousarray(arr("ctx_1024").transpose(0, 2, 1)),
        "mask": np.ascontiguousarray(arr("mask_BxSxS2_bf1")).view(np.uint8),
        "g_xattn": arr("g_xattn"),
        "g_ffn": arr("g_ffn"),
        "wq": turned("L0_xattn_Wq"), "bq": column("L0_xattn_bq"),
        "wk": turned("L0_xattn_Wk"), "bk": column("L0_xattn_bk"),
        "wv": turned("L0_xattn_Wv"), "bv": column("L0_xattn_bv"),
        "wo": turned("L0_xattn_Wo"), "bo": arr("L0_xattn_bo"),
        "sel": np.ascontiguousarray(sel.T),
        "q_w": turned("L0_ffn_q_w"),
        "k_w": turned("L0_ffn_k_w"),
        "v_w": np.ascontiguousarray(arr("L0_ffn_v_w").transpose(1, 0, 2).reshape(D, HE * PD)),
        "o_w": np.ascontiguousarray(arr("L0_ffn_o_w").transpose(1, 0, 2).reshape(PD, HE * D)),
        "route_scale": arr("L0_ffn_route_scale"),
    }
    nc = bacc.Bacc("TRN2", target_bir_lowering=False, num_devices=1)
    ins = {f"in_{n}": a for n, a in arrays.items()}
    args = [nc.dram_tensor(n, a.shape, mybir.dt.from_np(a.dtype), kind="ExternalInput").ap()
            for n, a in ins.items()]
    y = nc.dram_tensor("y", (T, D), F32, kind="ExternalOutput").ap()
    flamingo(nc, *args, y)
    r = run_bass_kernel_spmd(nc, [ins], core_ids=[0])
    return r.results[0]["y"].reshape(NB, SQ, D)
```
